# Optimizing a Trainium2 kernel written in Bass

```python
import numpy as np
import jax
import jax.numpy as jnp

def _softmax(x, axis=-1):
    return jax.nn.softmax(x, axis=axis)

def _gelu(x):
    return jax.nn.gelu(x, approximate=True)

def _silu(x):
    return jax.nn.silu(x)

def _sigmoid(x):
    return jax.nn.sigmoid(x)

def _layernorm(x, axis=-1, eps=1e-05):
    m = jnp.mean(x, axis=axis, keepdims=True)
    v = jnp.var(x, axis=axis, keepdims=True)
    return (x - m) / jnp.sqrt(v + eps)

def _scatter_add(tgt, idx, src, axis=0):
    return tgt.at[idx].add(src)

def _segment_sum(src, seg, n):
    return jax.ops.segment_sum(src, seg, n)
kernel_name = 'mk_xattn_ffn_d4_seqx_r8_e336cd'

def setup_inputs(seed: int=0):
    np.random.seed(seed)
    _w = jnp.asarray

    def _rec_inputs():
        import jax
        import jax.numpy as jnp
        _rk = jax.random.key(seed)
        x = 7.22e-05 + 1 * jax.random.normal(jax.random.fold_in(_rk, 1), (16, 256, 128), jnp.float32)
        _lenS = 256 - jax.random.randint(jax.random.fold_in(_rk, 7), (16,), 0, max(1, 256 // 4) + 1, jnp.int32)
        _lenS2 = 64 - jax.random.randint(jax.random.fold_in(_rk, 8), (16,), 0, max(1, 64 // 4) + 1, jnp.int32)
        _ctx_1024P = jax.random.normal(jax.random.fold_in(_rk, 11), (16, 16, 128), jnp.float32)
        _ctx_1024c = jax.random.dirichlet(jax.random.fold_in(_rk, 511), 0.3 * jnp.ones((16,), jnp.float32), (16, 64))
        _ctx_1024t = jnp.einsum('bsk,bkd->bsd', _ctx_1024c, _ctx_1024P)
        _ctx_1024t = _ctx_1024t * jax.lax.rsqrt(jnp.mean(jnp.square(_ctx_1024t)) + 1e-12) * 0.953939
        ctx_1024 = 4.13588e-05 + 0.999923 * (_ctx_1024t + 0.3 * jax.random.normal(jax.random.fold_in(_rk, 611), (16, 64, 128), jnp.float32))
        itok_BxS2_0_99 = jax.random.randint(jax.random.fold_in(_rk, 12), (16, 64), 0, 100, jnp.int32)
        _validS = jnp.arange(256)[None, :] < _lenS[:, None]
        _validS2 = jnp.arange(64)[None, :] < _lenS2[:, None]
        _causal = jnp.tril(jnp.ones((256, 256), dtype=bool))
        mask_1x1xSxS2_if1 = jnp.where(jnp.ones((1, 1, 256, 64), dtype=bool), 1, 0).astype(jnp.int32)
        mask_Bx1xSxS2_ff1 = jnp.where(jnp.ones((16, 1, 256, 64), dtype=bool), 1.0, 0.0).astype(jnp.float32)
        return (x, ctx_1024, itok_BxS2_0_99, mask_1x1xSxS2_if1, mask_Bx1xSxS2_ff1)
    x, ctx_1024, itok_BxS2_0_99, mask_1x1xSxS2_if1, mask_Bx1xSxS2_ff1 = _rec_inputs()

    def _L0_xattn_setup():
        import jax, jax.numpy as jnp
        import numpy as np
        B, S, D = (4, 256, 128)
        H = 16
        HD = D // H
        NEG = -1000000000.0
        key = jax.random.key(seed)
        ks = jax.random.split(key, 8)
        x = jax.random.normal(ks[0], (B, S, D), dtype=jnp.float32)
        y = jax.random.normal(ks[1], (B, S, D), dtype=jnp.float32)
        log_seqs = jax.random.randint(ks[2], (B, S), 0, 100, dtype=jnp.int64)
        sc = 1.0 / np.sqrt(D)
        Wq = jax.random.normal(ks[3], (D, D), dtype=jnp.float32) * sc
        Wk = jax.random.normal(ks[4], (D, D), dtype=jnp.float32) * sc
        Wv = jax.random.normal(ks[5], (D, D), dtype=jnp.float32) * sc
        Wo = jax.random.normal(ks[6], (D, D), dtype=jnp.float32) * sc
        bo = jnp.zeros((D,), dtype=jnp.float32)
        return {'x': x, 'y': y, 'log_seqs': log_seqs, 'pad_id': 0, 'Wq': Wq, 'Wk': Wk, 'Wv': Wv, 'Wo': Wo, 'bo': bo}
    _L0_xattn_all = _L0_xattn_setup()
    _L0_xattn_in = {k: v for k, v in _L0_xattn_all.items() if k in ('Wq', 'Wk', 'Wv', 'Wo', 'bo')}
    del _L0_xattn_all

    def _L0_ffn_setup():
        import jax, jax.numpy as jnp
        import numpy as np
        from jax.scipy.linalg import expm
        D = 128
        E = 6
        K = 2
        H = 2 * D
        A4 = 4 * D
        NROT = 4
        LN_EPS = 1e-05

        def _xavier(key, shape):
            fan_in, fan_out = (shape[-2], shape[-1])
            lim = np.sqrt(6.0 / (fan_in + fan_out))
            return jax.random.uniform(key, shape, jnp.float32, -lim, lim)

        def _layernorm(x, g, b):
            mu = jnp.mean(x, axis=-1, keepdims=True)
            var = jnp.var(x, axis=-1, keepdims=True)
            return (x - mu) * jax.lax.rsqrt(var + LN_EPS) * g + b

        def _moe(xn, gate_w, gate_b, ew1, eb1, ew2, eb2):
            logits = xn @ gate_w + gate_b
            tw, ti = jax.lax.top_k(logits, K)
            tw = jax.nn.softmax(tw, axis=-1)
            w_full = jnp.sum(tw[..., None] * jax.nn.one_hot(ti, E, dtype=tw.dtype), axis=-2)
            h = jax.nn.gelu(jnp.einsum('bsd,edh->besh', xn, ew1) + eb1[None, :, None, :], approximate=False)
            eo = jnp.einsum('besh,ehd->besd', h, ew2) + eb2[None, :, None, :]
            return jnp.einsum('bse,besd->bsd', w_full, eo)

        def _rotate(x, gens):
            for i in range(NROT):
                x = x @ expm(gens[i])
            return x
        key = jax.random.key(seed)
        ks = jax.random.split(key, 16)
        x = jax.random.normal(ks[0], (4, 256, D), jnp.float32)
        gens_raw = _xavier(ks[1], (NROT, D, D))
        gens = 0.5 * (gens_raw - jnp.swapaxes(gens_raw, -1, -2))
        return {'x': x, 'ln_g': jnp.ones((D,), jnp.float32), 'ln_b': jnp.zeros((D,), jnp.float32), 'aw1': _xavier(ks[2], (D, A4)), 'ab1': jnp.zeros((A4,), jnp.float32), 'aw2': _xavier(ks[3], (A4, D)), 'ab2': jnp.zeros((D,), jnp.float32), 'gate_w': _xavier(ks[4], (D, E)), 'gate_b': jnp.zeros((E,), jnp.float32), 'ew1': _xavier(ks[5], (E, D, H)), 'eb1': jnp.zeros((E, H), jnp.float32), 'ew2': _xavier(ks[6], (E, H, D)), 'eb2': jnp.zeros((E, D), jnp.float32), 'gens': gens, 'gc_w': _xavier(ks[7], (2 * D, 1)), 'gc_b': jnp.zeros((1,), jnp.float32)}
    _L0_ffn_all = _L0_ffn_setup()
    _L0_ffn_in = {k: v for k, v in _L0_ffn_all.items() if k in ('ln_g', 'ln_b', 'aw1', 'ab1', 'aw2', 'ab2', 'gate_w', 'gate_b', 'ew1', 'eb1', 'ew2', 'eb2', 'gens', 'gc_w', 'gc_b')}
    del _L0_ffn_all

    def _L1_xattn_setup():
        import jax, jax.numpy as jnp
        import numpy as np
        B, T, S, D = (4, 256, 512, 128)
        TOP_K = 32

        def _read(query, mem_state, top_k, Wq, bq, Wk, bk, Wv, bv, Wo, bo):
            b, t, d = query.shape
            s = mem_state.shape[1]
            scale = 1.0 / np.sqrt(d)
            q = query @ Wq.T + bq
            k = mem_state @ Wk.T + bk
            v = mem_state @ Wv.T + bv
            scores = jnp.einsum('btd,bsd->bts', q, k) * scale
            if top_k < s:
                vals, idx = jax.lax.top_k(scores, top_k)
                b_ix = jnp.arange(b)[:, None, None]
                t_ix = jnp.arange(t)[None, :, None]
                masked = jnp.full_like(scores, -jnp.inf)
                scores = masked.at[b_ix, t_ix, idx].set(vals)
            attn = jax.nn.softmax(scores, axis=-1)
            ctx = jnp.einsum('bts,bsd->btd', attn, v)
            return ctx @ Wo.T + bo
        key = jax.random.key(seed)
        ks = jax.random.split(key, 12)
        std = 0.02
        inp = {'query': jax.random.normal(ks[0], (B, T, D), dtype=jnp.float32), 'mem_state': jax.random.normal(ks[1], (B, S, D), dtype=jnp.float32), 'top_k': TOP_K, 'Wq': jax.random.normal(ks[2], (D, D), dtype=jnp.float32) * std, 'bq': jnp.zeros((D,), dtype=jnp.float32), 'Wk': jax.random.normal(ks[3], (D, D), dtype=jnp.float32) * std, 'bk': jnp.zeros((D,), dtype=jnp.float32), 'Wv': jax.random.normal(ks[4], (D, D), dtype=jnp.float32) * std, 'bv': jnp.zeros((D,), dtype=jnp.float32), 'Wo': jax.random.normal(ks[5], (D, D), dtype=jnp.float32) * std, 'bo': jnp.zeros((D,), dtype=jnp.float32)}
        return inp
    _L1_xattn_all = _L1_xattn_setup()
    _L1_xattn_in = {k: v for k, v in _L1_xattn_all.items() if k in ('Wq', 'bq', 'Wk', 'bk', 'Wv', 'bv', 'Wo', 'bo')}
    del _L1_xattn_all

    def _L1_ffn_setup():
        import math
        import jax, jax.numpy as jnp
        import numpy as np
        B, T, D, N, H = (8, 256, 128, 16, 256)
        CAP_FACTOR = 1.25
        key = jax.random.key(seed)
        ks = jax.random.split(key, 4)
        x = jax.random.normal(ks[0], (B, T, D), jnp.float32)
        Wg = jax.random.normal(ks[1], (D, N), jnp.float32) * D ** (-0.5)
        W1 = jax.random.normal(ks[2], (N, D, H), jnp.float32) * D ** (-0.5)
        b1 = jnp.zeros((N, H), jnp.float32)
        W2 = jax.random.normal(ks[3], (N, H, D), jnp.float32) * H ** (-0.5)
        b2 = jnp.zeros((N, D), jnp.float32)
        return {'x': x, 'Wg': Wg, 'W1': W1, 'b1': b1, 'W2': W2, 'b2': b2}
    _L1_ffn_all = _L1_ffn_setup()
    _L1_ffn_in = {k: v for k, v in _L1_ffn_all.items() if k in ('Wg', 'W1', 'b1', 'W2', 'b2')}
    del _L1_ffn_all

    def _L2_xattn_setup():
        import jax, jax.numpy as jnp
        import numpy as np
        B, S, D, H = (2, 256, 128, 16)
        DK = D // H
        key = jax.random.key(seed)
        ks = jax.random.split(key, 8)

        def lin(k):
            kw, kb = jax.random.split(k)
            w = jax.random.normal(kw, (D, D), dtype=jnp.float32) / np.sqrt(D)
            b = jax.random.normal(kb, (D,), dtype=jnp.float32) * 0.01
            return (w, b)
        wq, bq = lin(ks[0])
        wk, bk = lin(ks[1])
        wv, bv = lin(ks[2])
        wo, bo = lin(ks[3])
        return {'q': jax.random.normal(ks[4], (B, S, D), dtype=jnp.float32), 'k': jax.random.normal(ks[5], (B, S, D), dtype=jnp.float32), 'v': jax.random.normal(ks[6], (B, S, D), dtype=jnp.float32), 'mask': jnp.ones((1, 1, S, S), dtype=jnp.int32), 'wq': wq, 'bq': bq, 'wk': wk, 'bk': bk, 'wv': wv, 'bv': bv, 'wo': wo, 'bo': bo}
    _L2_xattn_all = _L2_xattn_setup()
    _L2_xattn_in = {k: v for k, v in _L2_xattn_all.items() if k in ('wq', 'bq', 'wk', 'bk', 'wv', 'bv', 'wo', 'bo')}
    del _L2_xattn_all

    def _L2_ffn_setup():
        import jax, jax.numpy as jnp
        import numpy as np
        LATENT = 128
        LEAF_W = 64
        DEPTH = 4
        N_LEAVES = 2 ** DEPTH
        N_NODES = 2 ** DEPTH - 1
        B, S = (4, 256)

        def _fff_params(key, prefix):
            ks = jax.random.split(key, 4)
            d, h, l, n = (LATENT, LEAF_W, N_LEAVES, N_NODES)
            s_in = 1.0 / np.sqrt(d).astype(np.float32)
            s_h = 1.0 / np.sqrt(h).astype(np.float32)
            return {f'{prefix}_node_w': jax.random.normal(ks[0], (n, d), jnp.float32) * s_in, f'{prefix}_node_b': jax.random.normal(ks[1], (n,), jnp.float32) * s_in, f'{prefix}_w1': jax.random.normal(ks[2], (l, d, h), jnp.float32) * s_in, f'{prefix}_b1': jnp.zeros((l, h), jnp.float32), f'{prefix}_w2': jax.random.normal(ks[3], (l, h, d), jnp.float32) * s_h, f'{prefix}_b2': jnp.zeros((l, d), jnp.float32)}

        def _fff(x, node_w, node_b, w1, b1, w2, b2):
            Bx, Sx, D = x.shape
            xf = x.reshape(-1, D)
            N = xf.shape[0]
            cur = jnp.zeros((N,), jnp.int32)
            for _ in range(DEPTH):
                pw = node_w[cur]
                score = jnp.einsum('nd,nd->n', xf, pw) + node_b[cur]
                cur = 2 * cur + 1 + (score >= 0).astype(jnp.int32)
            leaf = cur - N_NODES
            sel = jax.nn.one_hot(leaf, N_LEAVES, dtype=xf.dtype)
            hidden_all = jax.nn.relu(jnp.einsum('nd,ldh->lnh', xf, w1) + b1[:, None, :])
            hidden = hidden_all * sel.T[:, :, None]
            out = jnp.einsum('lnh,lho->no', hidden, w2) + sel @ b2
            return out.reshape(Bx, Sx, D)
        key = jax.random.key(seed)
        kx, kq, kk, kv = jax.random.split(key, 4)
        inp = {'x': jax.random.normal(kx, (B, S, LATENT), jnp.float32)}
        inp.update(_fff_params(kq, 'q'))
        inp.update(_fff_params(kk, 'k'))
        inp.update(_fff_params(kv, 'v'))
        return inp
    _L2_ffn_all = _L2_ffn_setup()
    _L2_ffn_in = {k: v for k, v in _L2_ffn_all.items() if k in ('q_node_w', 'q_node_b', 'q_w1', 'q_b1', 'q_w2', 'q_b2', 'k_node_w', 'k_node_b', 'k_w1', 'k_b1', 'k_w2', 'k_b2', 'v_node_w', 'v_node_b', 'v_w1', 'v_b1', 'v_w2', 'v_b2')}
    del _L2_ffn_all

    def _L3_xattn_setup():
        import jax, jax.numpy as jnp
        import numpy as np
        N_HEADS, N_UNITS = (16, 128)
        D_K = N_UNITS // N_HEADS
        B, S = (2, 256)
        key = jax.random.key(seed)
        ks = jax.random.split(key, 12)
        s = 1.0 / np.sqrt(N_UNITS)
        return {'query': jax.random.normal(ks[0], (B, S, N_UNITS), jnp.float32), 'key': jax.random.normal(ks[1], (B, S, N_UNITS), jnp.float32), 'value': jax.random.normal(ks[2], (B, S, N_UNITS), jnp.float32), 'mask': jnp.ones((B, 1, S, S), jnp.float32), 'Wq': jax.random.normal(ks[3], (N_HEADS, N_UNITS, D_K), jnp.float32) * s, 'bq': jax.random.normal(ks[4], (N_HEADS, D_K), jnp.float32) * s, 'Wk': jax.random.normal(ks[5], (N_HEADS, N_UNITS, D_K), jnp.float32) * s, 'bk': jax.random.normal(ks[6], (N_HEADS, D_K), jnp.float32) * s, 'Wv': jax.random.normal(ks[7], (N_HEADS, N_UNITS, D_K), jnp.float32) * s, 'bv': jax.random.normal(ks[8], (N_HEADS, D_K), jnp.float32) * s, 'Wo': jax.random.normal(ks[9], (N_UNITS, N_UNITS), jnp.float32) * s, 'bo': jax.random.normal(ks[10], (N_UNITS,), jnp.float32) * s}
    _L3_xattn_all = _L3_xattn_setup()
    _L3_xattn_in = {k: v for k, v in _L3_xattn_all.items() if k in ('Wq', 'bq', 'Wk', 'bk', 'Wv', 'bv', 'Wo', 'bo')}
    del _L3_xattn_all

    def _L3_ffn_setup():
        import jax, jax.numpy as jnp
        import numpy as np
        EPS = 1e-05
        key = jax.random.key(seed)
        kx, kw, kb = jax.random.split(key, 3)
        B, S, K, N = (8, 1024, 128, 128)
        x = jax.random.normal(kx, (B, S, K), dtype=jnp.float32)
        W = jax.random.normal(kw, (N, K), dtype=jnp.float32) * 0.02
        weight_scale = jnp.maximum(jnp.max(jnp.abs(W), axis=1, keepdims=True) / 127.0, EPS)
        weight_int8 = jnp.clip(jnp.round(W / weight_scale), -128, 127).astype(jnp.int8)
        bias = jax.random.normal(kb, (N,), dtype=jnp.float32) * 0.01
        return {'x': x, 'weight_int8': weight_int8, 'weight_scale': weight_scale, 'bias': bias}
    _L3_ffn_all = _L3_ffn_setup()
    _L3_ffn_in = {k: v for k, v in _L3_ffn_all.items() if k in ('weight_int8', 'weight_scale', 'bias')}
    del _L3_ffn_all
    return {'x': x, 'ctx_1024': ctx_1024, 'itok_BxS2_0_99': itok_BxS2_0_99, 'mask_1x1xSxS2_if1': mask_1x1xSxS2_if1, 'mask_Bx1xSxS2_ff1': mask_Bx1xSxS2_ff1, 'L0_xattn_Wq': _L0_xattn_in['Wq'], 'L0_xattn_Wk': _L0_xattn_in['Wk'], 'L0_xattn_Wv': _L0_xattn_in['Wv'], 'L0_xattn_Wo': _L0_xattn_in['Wo'], 'L0_xattn_bo': _L0_xattn_in['bo'], 'L0_ffn_ln_g': _L0_ffn_in['ln_g'], 'L0_ffn_ln_b': _L0_ffn_in['ln_b'], 'L0_ffn_aw1': _L0_ffn_in['aw1'], 'L0_ffn_ab1': _L0_ffn_in['ab1'], 'L0_ffn_aw2': _L0_ffn_in['aw2'], 'L0_ffn_ab2': _L0_ffn_in['ab2'], 'L0_ffn_gate_w': _L0_ffn_in['gate_w'], 'L0_ffn_gate_b': _L0_ffn_in['gate_b'], 'L0_ffn_ew1': _L0_ffn_in['ew1'], 'L0_ffn_eb1': _L0_ffn_in['eb1'], 'L0_ffn_ew2': _L0_ffn_in['ew2'], 'L0_ffn_eb2': _L0_ffn_in['eb2'], 'L0_ffn_gens': _L0_ffn_in['gens'], 'L0_ffn_gc_w': _L0_ffn_in['gc_w'], 'L0_ffn_gc_b': _L0_ffn_in['gc_b'], 'L1_xattn_Wq': _L1_xattn_in['Wq'], 'L1_xattn_bq': _L1_xattn_in['bq'], 'L1_xattn_Wk': _L1_xattn_in['Wk'], 'L1_xattn_bk': _L1_xattn_in['bk'], 'L1_xattn_Wv': _L1_xattn_in['Wv'], 'L1_xattn_bv': _L1_xattn_in['bv'], 'L1_xattn_Wo': _L1_xattn_in['Wo'], 'L1_xattn_bo': _L1_xattn_in['bo'], 'L1_ffn_Wg': _L1_ffn_in['Wg'], 'L1_ffn_W1': _L1_ffn_in['W1'], 'L1_ffn_b1': _L1_ffn_in['b1'], 'L1_ffn_W2': _L1_ffn_in['W2'], 'L1_ffn_b2': _L1_ffn_in['b2'], 'L2_xattn_wq': _L2_xattn_in['wq'], 'L2_xattn_bq': _L2_xattn_in['bq'], 'L2_xattn_wk': _L2_xattn_in['wk'], 'L2_xattn_bk': _L2_xattn_in['bk'], 'L2_xattn_wv': _L2_xattn_in['wv'], 'L2_xattn_bv': _L2_xattn_in['bv'], 'L2_xattn_wo': _L2_xattn_in['wo'], 'L2_xattn_bo': _L2_xattn_in['bo'], 'L2_ffn_q_node_w': _L2_ffn_in['q_node_w'], 'L2_ffn_q_node_b': _L2_ffn_in['q_node_b'], 'L2_ffn_q_w1': _L2_ffn_in['q_w1'], 'L2_ffn_q_b1': _L2_ffn_in['q_b1'], 'L2_ffn_q_w2': _L2_ffn_in['q_w2'], 'L2_ffn_q_b2': _L2_ffn_in['q_b2'], 'L2_ffn_k_node_w': _L2_ffn_in['k_node_w'], 'L2_ffn_k_node_b': _L2_ffn_in['k_node_b'], 'L2_ffn_k_w1': _L2_ffn_in['k_w1'], 'L2_ffn_k_b1': _L2_ffn_in['k_b1'], 'L2_ffn_k_w2': _L2_ffn_in['k_w2'], 'L2_ffn_k_b2': _L2_ffn_in['k_b2'], 'L2_ffn_v_node_w': _L2_ffn_in['v_node_w'], 'L2_ffn_v_node_b': _L2_ffn_in['v_node_b'], 'L2_ffn_v_w1': _L2_ffn_in['v_w1'], 'L2_ffn_v_b1': _L2_ffn_in['v_b1'], 'L2_ffn_v_w2': _L2_ffn_in['v_w2'], 'L2_ffn_v_b2': _L2_ffn_in['v_b2'], 'L3_xattn_Wq': _L3_xattn_in['Wq'], 'L3_xattn_bq': _L3_xattn_in['bq'], 'L3_xattn_Wk': _L3_xattn_in['Wk'], 'L3_xattn_bk': _L3_xattn_in['bk'], 'L3_xattn_Wv': _L3_xattn_in['Wv'], 'L3_xattn_bv': _L3_xattn_in['bv'], 'L3_xattn_Wo': _L3_xattn_in['Wo'], 'L3_xattn_bo': _L3_xattn_in['bo'], 'L3_ffn_weight_int8': _L3_ffn_in['weight_int8'], 'L3_ffn_weight_scale': _L3_ffn_in['weight_scale'], 'L3_ffn_bias': _L3_ffn_in['bias']}

def reference(x, ctx_1024, itok_BxS2_0_99, mask_1x1xSxS2_if1, mask_Bx1xSxS2_ff1, L0_xattn_Wq, L0_xattn_Wk, L0_xattn_Wv, L0_xattn_Wo, L0_xattn_bo, L0_ffn_ln_g, L0_ffn_ln_b, L0_ffn_aw1, L0_ffn_ab1, L0_ffn_aw2, L0_ffn_ab2, L0_ffn_gate_w, L0_ffn_gate_b, L0_ffn_ew1, L0_ffn_eb1, L0_ffn_ew2, L0_ffn_eb2, L0_ffn_gens, L0_ffn_gc_w, L0_ffn_gc_b, L1_xattn_Wq, L1_xattn_bq, L1_xattn_Wk, L1_xattn_bk, L1_xattn_Wv, L1_xattn_bv, L1_xattn_Wo, L1_xattn_bo, L1_ffn_Wg, L1_ffn_W1, L1_ffn_b1, L1_ffn_W2, L1_ffn_b2, L2_xattn_wq, L2_xattn_bq, L2_xattn_wk, L2_xattn_bk, L2_xattn_wv, L2_xattn_bv, L2_xattn_wo, L2_xattn_bo, L2_ffn_q_node_w, L2_ffn_q_node_b, L2_ffn_q_w1, L2_ffn_q_b1, L2_ffn_q_w2, L2_ffn_q_b2, L2_ffn_k_node_w, L2_ffn_k_node_b, L2_ffn_k_w1, L2_ffn_k_b1, L2_ffn_k_w2, L2_ffn_k_b2, L2_ffn_v_node_w, L2_ffn_v_node_b, L2_ffn_v_w1, L2_ffn_v_b1, L2_ffn_v_w2, L2_ffn_v_b2, L3_xattn_Wq, L3_xattn_bq, L3_xattn_Wk, L3_xattn_bk, L3_xattn_Wv, L3_xattn_bv, L3_xattn_Wo, L3_xattn_bo, L3_ffn_weight_int8, L3_ffn_weight_scale, L3_ffn_bias):
    import jax
    import jax.numpy as jnp

    def _L0_xattn_ref(x, y, log_seqs, pad_id, Wq, Wk, Wv, Wo, bo):
        import jax, jax.numpy as jnp
        import numpy as np
        B, S, D = (4, 256, 128)
        H = 16
        HD = D // H
        NEG = -1000000000.0
        b = x.shape[0]
        q = (x @ Wq).reshape(b, -1, H, HD).transpose(0, 2, 1, 3)
        k = (y @ Wk).reshape(b, -1, H, HD).transpose(0, 2, 1, 3)
        v = (y @ Wv).reshape(b, -1, H, HD).transpose(0, 2, 1, 3)
        mask = (log_seqs == pad_id)[:, None, None, :]
        scores = jnp.einsum('bhqd,bhkd->bhqk', q, k)
        scores = jnp.where(mask, NEG, scores)
        probs = jax.nn.softmax(scores / np.sqrt(HD), axis=-1)
        attn = jnp.einsum('bhqk,bhkd->bhqd', probs, v)
        attn = attn.transpose(0, 2, 1, 3).reshape(b, -1, H * HD)
        return attn @ Wo + bo

    def _L0_ffn_ref(x, ln_g, ln_b, aw1, ab1, aw2, ab2, gate_w, gate_b, ew1, eb1, ew2, eb2, gens, gc_w, gc_b):
        import jax, jax.numpy as jnp
        import numpy as np
        from jax.scipy.linalg import expm
        D = 128
        E = 6
        K = 2
        H = 2 * D
        A4 = 4 * D
        NROT = 4
        LN_EPS = 1e-05

        def _xavier(key, shape):
            fan_in, fan_out = (shape[-2], shape[-1])
            lim = np.sqrt(6.0 / (fan_in + fan_out))
            return jax.random.uniform(key, shape, jnp.float32, -lim, lim)

        def _layernorm(x, g, b):
            mu = jnp.mean(x, axis=-1, keepdims=True)
            var = jnp.var(x, axis=-1, keepdims=True)
            return (x - mu) * jax.lax.rsqrt(var + LN_EPS) * g + b

        def _moe(xn, gate_w, gate_b, ew1, eb1, ew2, eb2):
            logits = xn @ gate_w + gate_b
            tw, ti = jax.lax.top_k(logits, K)
            tw = jax.nn.softmax(tw, axis=-1)
            w_full = jnp.sum(tw[..., None] * jax.nn.one_hot(ti, E, dtype=tw.dtype), axis=-2)
            h = jax.nn.gelu(jnp.einsum('bsd,edh->besh', xn, ew1) + eb1[None, :, None, :], approximate=False)
            eo = jnp.einsum('besh,ehd->besd', h, ew2) + eb2[None, :, None, :]
            return jnp.einsum('bse,besd->bsd', w_full, eo)

        def _rotate(x, gens):
            for i in range(NROT):
                x = x @ expm(gens[i])
            return x
        residual = x
        xn = _layernorm(x, ln_g, ln_b)
        abel = jax.nn.gelu(xn @ aw1 + ab1, approximate=False) @ aw2 + ab2
        nonabel = _rotate(_moe(xn, gate_w, gate_b, ew1, eb1, ew2, eb2), gens)
        combined = jnp.concatenate([abel, nonabel], axis=-1)
        gate = jax.nn.sigmoid(combined @ gc_w + gc_b)
        mixed = abel * (1.0 - gate) + nonabel * gate
        return residual + mixed

    def _L1_xattn_ref(query, mem_state, top_k, Wq, bq, Wk, bk, Wv, bv, Wo, bo):
        import jax, jax.numpy as jnp
        import numpy as np
        B, T, S, D = (4, 256, 512, 128)
        TOP_K = 32

        def _read(query, mem_state, top_k, Wq, bq, Wk, bk, Wv, bv, Wo, bo):
            b, t, d = query.shape
            s = mem_state.shape[1]
            scale = 1.0 / np.sqrt(d)
            q = query @ Wq.T + bq
            k = mem_state @ Wk.T + bk
            v = mem_state @ Wv.T + bv
            scores = jnp.einsum('btd,bsd->bts', q, k) * scale
            if top_k < s:
                vals, idx = jax.lax.top_k(scores, top_k)
                b_ix = jnp.arange(b)[:, None, None]
                t_ix = jnp.arange(t)[None, :, None]
                masked = jnp.full_like(scores, -jnp.inf)
                scores = masked.at[b_ix, t_ix, idx].set(vals)
            attn = jax.nn.softmax(scores, axis=-1)
            ctx = jnp.einsum('bts,bsd->btd', attn, v)
            return ctx @ Wo.T + bo
        return _read(query, mem_state, top_k, Wq, bq, Wk, bk, Wv, bv, Wo, bo)

    def _L1_ffn_ref(x, Wg, W1, b1, W2, b2):
        import math
        import jax, jax.numpy as jnp
        import numpy as np
        B, T, D, N, H = (8, 256, 128, 16, 256)
        CAP_FACTOR = 1.25
        b, t, d = x.shape
        n = Wg.shape[1]
        bt = b * t
        cap = math.ceil(CAP_FACTOR * bt / n)
        logits = jnp.einsum('btd,dn->btn', x, Wg)
        probs = jax.nn.softmax(logits, axis=-1)
        top1_val = probs.max(axis=-1).reshape(bt)
        top1_idx = probs.argmax(axis=-1).reshape(bt)
        x_flat = x.reshape(bt, d)
        masked = jnp.where(top1_idx[None, :] == jnp.arange(n)[:, None], top1_val[None, :], -jnp.inf)
        vals, idx = jax.lax.top_k(masked, cap)
        valid = jnp.isfinite(vals)
        xe = x_flat[idx]
        h = jax.nn.gelu(jnp.einsum('ncd,ndh->nch', xe, W1) + b1[:, None, :])
        out = jnp.einsum('nch,nhd->ncd', h, W2) + b2[:, None, :]
        safe_idx = jnp.where(valid, idx, bt)
        y_flat = x_flat.at[safe_idx.reshape(-1)].set(out.reshape(-1, d), mode='drop')
        return y_flat.reshape(b, t, d)

    def _L2_xattn_ref(q, k, v, mask, wq, bq, wk, bk, wv, bv, wo, bo):
        import jax, jax.numpy as jnp
        import numpy as np
        B, S, D, H = (2, 256, 128, 16)
        DK = D // H
        b, s, _ = q.shape
        Q = (q @ wq.T + bq).reshape(b, s, H, DK).transpose(0, 2, 1, 3)
        K = (k @ wk.T + bk).reshape(b, -1, H, DK).transpose(0, 2, 1, 3)
        V = (v @ wv.T + bv).reshape(b, -1, H, DK).transpose(0, 2, 1, 3)
        scores = jnp.einsum('bhqd,bhkd->bhqk', Q, K) / np.sqrt(DK)
        scores = jnp.where(mask == 0, jnp.float32(-1e-09), scores)
        att = jax.nn.softmax(scores, axis=-1)
        x = jnp.einsum('bhqk,bhkd->bhqd', att, V)
        x = x.transpose(0, 2, 1, 3).reshape(b, s, H * DK)
        return x @ wo.T + bo

    def _L2_ffn_ref(x, q_node_w, q_node_b, q_w1, q_b1, q_w2, q_b2, k_node_w, k_node_b, k_w1, k_b1, k_w2, k_b2, v_node_w, v_node_b, v_w1, v_b1, v_w2, v_b2):
        import jax, jax.numpy as jnp
        import numpy as np
        LATENT = 128
        LEAF_W = 64
        DEPTH = 4
        N_LEAVES = 2 ** DEPTH
        N_NODES = 2 ** DEPTH - 1
        B, S = (4, 256)

        def _fff_params(key, prefix):
            ks = jax.random.split(key, 4)
            d, h, l, n = (LATENT, LEAF_W, N_LEAVES, N_NODES)
            s_in = 1.0 / np.sqrt(d).astype(np.float32)
            s_h = 1.0 / np.sqrt(h).astype(np.float32)
            return {f'{prefix}_node_w': jax.random.normal(ks[0], (n, d), jnp.float32) * s_in, f'{prefix}_node_b': jax.random.normal(ks[1], (n,), jnp.float32) * s_in, f'{prefix}_w1': jax.random.normal(ks[2], (l, d, h), jnp.float32) * s_in, f'{prefix}_b1': jnp.zeros((l, h), jnp.float32), f'{prefix}_w2': jax.random.normal(ks[3], (l, h, d), jnp.float32) * s_h, f'{prefix}_b2': jnp.zeros((l, d), jnp.float32)}

        def _fff(x, node_w, node_b, w1, b1, w2, b2):
            Bx, Sx, D = x.shape
            xf = x.reshape(-1, D)
            N = xf.shape[0]
            cur = jnp.zeros((N,), jnp.int32)
            for _ in range(DEPTH):
                pw = node_w[cur]
                score = jnp.einsum('nd,nd->n', xf, pw) + node_b[cur]
                cur = 2 * cur + 1 + (score >= 0).astype(jnp.int32)
            leaf = cur - N_NODES
            sel = jax.nn.one_hot(leaf, N_LEAVES, dtype=xf.dtype)
            hidden_all = jax.nn.relu(jnp.einsum('nd,ldh->lnh', xf, w1) + b1[:, None, :])
            hidden = hidden_all * sel.T[:, :, None]
            out = jnp.einsum('lnh,lho->no', hidden, w2) + sel @ b2
            return out.reshape(Bx, Sx, D)
        q = _fff(x, q_node_w, q_node_b, q_w1, q_b1, q_w2, q_b2)
        k = _fff(x, k_node_w, k_node_b, k_w1, k_b1, k_w2, k_b2)
        v = _fff(x, v_node_w, v_node_b, v_w1, v_b1, v_w2, v_b2)
        scale = 1.0 / np.sqrt(LATENT).astype(np.float32)
        attn = jax.nn.softmax(jnp.einsum('bqd,bkd->bqk', q, k) * scale, axis=-1)
        return jnp.einsum('bqk,bkd->bqd', attn, v)

    def _L3_xattn_ref(query, key, value, mask, Wq, bq, Wk, bk, Wv, bv, Wo, bo):
        import jax, jax.numpy as jnp
        import numpy as np
        N_HEADS, N_UNITS = (16, 128)
        D_K = N_UNITS // N_HEADS
        B, S = (2, 256)
        q = jnp.einsum('bsd,hdk->bhsk', query, Wq) + bq[None, :, None, :]
        k = jnp.einsum('bsd,hdk->bhsk', key, Wk) + bk[None, :, None, :]
        v = jnp.einsum('bsd,hdk->bhsk', value, Wv) + bv[None, :, None, :]
        scores = jnp.einsum('bhqk,bhmk->bhqm', q, k) / jnp.sqrt(jnp.asarray(D_K, q.dtype))
        scores = jnp.where(mask == 0.0, jnp.asarray(-1000000000.0, scores.dtype), scores)
        attn = jax.nn.softmax(scores, axis=-1)
        h = jnp.einsum('bhqm,bhmk->bhqk', attn, v)
        h = h.transpose(0, 2, 1, 3).reshape(query.shape[0], query.shape[1], N_UNITS)
        return h @ Wo + bo

    def _L3_ffn_ref(x, weight_int8, weight_scale, bias):
        import jax, jax.numpy as jnp
        import numpy as np
        EPS = 1e-05
        B, S, K = x.shape
        x2 = x.reshape(-1, K)
        x_scale = jnp.maximum(jnp.abs(x2).max() / 127.0, EPS)
        x_int8 = jnp.clip(jnp.round(x2 / x_scale), -128, 127).astype(jnp.int8)
        acc_i32 = jax.lax.dot_general(x_int8, weight_int8.T, dimension_numbers=(((1,), (0,)), ((), ())), preferred_element_type=jnp.int32)
        out = acc_i32.astype(jnp.float32) * x_scale * weight_scale.T
        out = out + bias
        return out.reshape(B, S, -1)
    x = x + _L0_xattn_ref(_layernorm(x, axis=-1), ctx_1024, itok_BxS2_0_99, 0, L0_xattn_Wq, L0_xattn_Wk, L0_xattn_Wv, L0_xattn_Wo, L0_xattn_bo)
    x = x + _L0_ffn_ref(_layernorm(x, axis=-1), L0_ffn_ln_g, L0_ffn_ln_b, L0_ffn_aw1, L0_ffn_ab1, L0_ffn_aw2, L0_ffn_ab2, L0_ffn_gate_w, L0_ffn_gate_b, L0_ffn_ew1, L0_ffn_eb1, L0_ffn_ew2, L0_ffn_eb2, L0_ffn_gens, L0_ffn_gc_w, L0_ffn_gc_b)
    x = x + _L1_xattn_ref(_layernorm(x, axis=-1), ctx_1024, 32, L1_xattn_Wq, L1_xattn_bq, L1_xattn_Wk, L1_xattn_bk, L1_xattn_Wv, L1_xattn_bv, L1_xattn_Wo, L1_xattn_bo)
    x = x + _L1_ffn_ref(_layernorm(x, axis=-1), L1_ffn_Wg, L1_ffn_W1, L1_ffn_b1, L1_ffn_W2, L1_ffn_b2)
    x = x + _L2_xattn_ref(_layernorm(x, axis=-1), ctx_1024, ctx_1024, mask_1x1xSxS2_if1, L2_xattn_wq, L2_xattn_bq, L2_xattn_wk, L2_xattn_bk, L2_xattn_wv, L2_xattn_bv, L2_xattn_wo, L2_xattn_bo)
    x = x + _L2_ffn_ref(_layernorm(x, axis=-1), L2_ffn_q_node_w, L2_ffn_q_node_b, L2_ffn_q_w1, L2_ffn_q_b1, L2_ffn_q_w2, L2_ffn_q_b2, L2_ffn_k_node_w, L2_ffn_k_node_b, L2_ffn_k_w1, L2_ffn_k_b1, L2_ffn_k_w2, L2_ffn_k_b2, L2_ffn_v_node_w, L2_ffn_v_node_b, L2_ffn_v_w1, L2_ffn_v_b1, L2_ffn_v_w2, L2_ffn_v_b2)
    x = x + _L3_xattn_ref(_layernorm(x, axis=-1), ctx_1024, ctx_1024, mask_Bx1xSxS2_ff1, L3_xattn_Wq, L3_xattn_bq, L3_xattn_Wk, L3_xattn_bk, L3_xattn_Wv, L3_xattn_bv, L3_xattn_Wo, L3_xattn_bo)
    x = x + _L3_ffn_ref(_layernorm(x, axis=-1), L3_ffn_weight_int8, L3_ffn_weight_scale, L3_ffn_bias)
    return x

_drawn_inputs = setup_inputs


def setup_inputs(seed=0):
    import zlib

    import numpy as np

    out = dict(_drawn_inputs(seed))
    spreads = {'L0_xattn_bo': (0.0, 0.1),
     'L0_ffn_ln_g': (1.0, 0.2),
     'L0_ffn_ln_b': (0.0, 0.1),
     'L0_ffn_ab1': (0.0, 0.1),
     'L0_ffn_ab2': (0.0, 0.1),
     'L0_ffn_gate_b': (0.0, 0.1),
     'L0_ffn_eb1': (0.0, 0.1),
     'L0_ffn_eb2': (0.0, 0.1),
     'L1_xattn_bq': (0.0, 0.271),
     'L1_xattn_bk': (0.0, 0.8),
     'L1_xattn_bv': (0.0, 0.1),
     'L1_xattn_bo': (0.0, 0.1),
     'L1_ffn_b1': (0.0, 0.297),
     'L1_ffn_b2': (0.0, 0.1),
     'L2_ffn_q_b1': (0.0, 0.8),
     'L2_ffn_q_b2': (0.0, 0.8),
     'L2_ffn_k_b1': (0.0, 0.8),
     'L2_ffn_k_b2': (0.0, 0.8),
     'L2_ffn_v_b1': (0.0, 0.8),
     'L2_ffn_v_b2': (0.0, 0.642)}
    factors = {'L2_xattn_bq': 8.0,
     'L2_xattn_bk': 8.0,
     'L2_xattn_bv': 8.0,
     'L2_xattn_bo': 8.0,
     'L2_ffn_q_node_w': 6.187,
     'L2_ffn_q_node_b': 8.0,
     'L2_ffn_q_w1': 7.169,
     'L2_ffn_q_w2': 5.959,
     'L2_ffn_k_node_w': 6.042,
     'L2_ffn_k_node_b': 8.0,
     'L2_ffn_k_w1': 7.001,
     'L2_ffn_k_w2': 5.962,
     'L2_ffn_v_node_b': 4.541,
     'L3_xattn_bq': 6.474,
     'L3_xattn_bk': 8.0,
     'L3_ffn_weight_scale': 4.177,
     'L3_ffn_bias': 8.0}
    for name, (base, spread) in spreads.items():
        noise = np.random.default_rng([zlib.crc32(name.encode()), seed]).standard_normal(out[name].shape)
        drawn = base * np.exp(spread * noise) if base else spread * noise
        out[name] = jnp.asarray(drawn.astype(out[name].dtype))
    for name, factor in factors.items():
        out[name] = (out[name] * factor).astype(out[name].dtype)
    return out
```

```python
from contextlib import ExitStack

import concourse.bass as bass
from concourse import mybir

F32 = mybir.dt.float32
F32R = mybir.dt.float32r
BF16 = mybir.dt.bfloat16
I32 = mybir.dt.int32
I8 = mybir.dt.int8
ALU = mybir.AluOpType
ACT = mybir.ActivationFunctionType
AX = mybir.AxisListType

P = 128
B, S, SK = 16, 256, 64
T = B * S // P
TB = S // P
H, HD = 16, 8
CH = H * SK // P
VW = 2 * HD + 2
EPS = 1e-5
NEG = -1e9


def need(eng, sem, value):
    if not isinstance(value, int) or value > 0:
        eng.wait_ge(sem, value)


def need_apart(eng, sem, value, tick):
    if not isinstance(value, int) or value > 0:
        eng.wait_ge(sem, value)
        eng.sem_inc(tick, 1)


class Chain:

    def __init__(self, eng, sem):
        self.eng, self.sem, self.n = eng, sem, 0

    def __call__(self, ins, base=0):
        self.n += 1
        ins.then_inc(self.sem, 1)
        self.eng.wait_ge(self.sem, base + self.n)


def cols(pack, layout, name):
    lo, hi, rows = layout[name]
    return pack[0:rows, lo:hi]


class Core:

    def __init__(self, nc, ctx, A, layouts):
        self.nc, self.ctx, self.A, self.lay = nc, ctx, A, layouts
        self.X = self.sb("X", [P, T, P])
        self.MV = self.sb("MV", [P, T, 2])
        self.RS = self.sb("RS", [P, T])
        self.pack = {}

    def sb(self, name, shape, dt=F32):
        return self.ctx.enter_context(self.nc.sbuf_tensor(name, shape, dt))

    def gpsimd_dma_sem(self, name):
        return self.ctx.enter_context(self.nc.semaphore(name))

    def w(self, pack, name):
        lo, hi, rows = self.lay[pack][name]
        return self.pack[pack][0:rows, lo:hi]


class Stage:

    def __init__(self, core, name):
        self.core, self.name, self.nc = core, name, core.nc
        self.stack = ExitStack()
        self.used = []

    def __enter__(self):
        self.stack.__enter__()
        return self

    def __exit__(self, *a):
        return self.stack.__exit__(*a)

    def sb(self, name, shape, dt=F32):
        return self.stack.enter_context(self.nc.sbuf_tensor(f"{self.name}_{name}", shape, dt))

    def ps(self, name, shape, dt=F32):
        return self.stack.enter_context(self.nc.psum_tensor(f"{self.name}_{name}", shape, dt))

    def sem(self, name):
        sem = self.stack.enter_context(self.nc.semaphore(f"{self.name}_{name}"))
        self.used.append(sem.num)
        return sem

    def block(self):
        self.stack.callback(self.clear)
        return self.stack.enter_context(self.nc.Block())

    def clear(self):
        used = sorted(self.used)
        while used:
            n = 1
            while n < len(used) and used[n] == used[0] + n:
                n += 1
            self.nc.gpsimd.sem_clear(range(used[0], used[0] + n))
            used = used[n:]


def token_scales(core, st, var, out, tag):
    ve = st.sb(f"ve{tag}", [P, T])
    sd = st.sb(f"sd{tag}", [P, T])
    nt = st.sb(f"nt{tag}", [P, T])
    s_ve, s_sd, s_own = st.sem(f"ve{tag}"), st.sem(f"sd{tag}"), st.sem(f"rs{tag}")

    def on_scalar(act):
        act.wait_ge(s_ve, 1)
        act.activation(sd[:], ve[:], ACT.Sqrt).then_inc(s_sd, 1)

    def on_vector(dve):
        dve.tensor_scalar(ve[:], var, EPS, None, ALU.add).then_inc(s_ve, 1)
        dve.wait_ge(s_sd, 1)
        link = Chain(dve, s_own)
        link(dve.reciprocal(out, sd[:]))
        link(dve.tensor_tensor(nt[:], ve[:], out, ALU.mult))
        link(dve.tensor_tensor(nt[:], nt[:], out, ALU.mult))
        link(dve.tensor_scalar(nt[:], nt[:], -0.5, 1.5, ALU.mult, ALU.add))
        link(dve.tensor_tensor(out, out, nt[:], ALU.mult))

    return on_scalar, on_vector


class Slot:

    def __init__(self, i, k):
        self.i, self.k = i, k

    def t(self, d):
        return 4 * self.i + self.k + d

    def has(self, d):
        return not isinstance(self.i, int) or 0 <= self.t(d) < T

    def b(self, d):
        return 2 * self.i + (self.k + d) // 2

    def u(self, d):
        return (self.k + d) // 2 % 2

    def v(self, d):
        return (self.k + d) % 2

    def next_x(self):
        return self.k % 2 == 1 and self.has(3)

    def next_q(self):
        return self.k % 2 == 0 and self.has(2)


def tile_slots(eng, slot, lag):
    for k in range(4):
        slot(Slot(0, k))
    with eng.Fori(1, T // 4 - 1) as i:
        for k in range(4):
            slot(Slot(i, k))
    for t in range(T - 4, T + lag):
        slot(Slot(t // 4, t % 4))


def prep_mha(core, L, key_mask):
    nc = core.nc
    KT = core.KT[L]
    VB = core.VB[L]
    w = lambda n: core.w(f"mha{L}", n)
    with Stage(core, f"prep{L}") as st:
        pk = st.ps("pk", [P, 2, 512])
        pv = st.ps("pv", [P, 4, 4, P])
        s_k, s_v, s_kt, s_z, s_o = (st.sem(n) for n in ("k", "v", "kt", "z", "own"))
        blk = st.block()
        c2 = core.w("ctx", "ctxT2").rearrange("p (b r k) -> p b r k", r=2, k=SK)

        @blk.tensor
        def _(pe):
            for n in range(2):
                pe.matmul(pk[:, n, :], w("wk"), c2[:, 8 * n:8 * n + 8, 0, :], start=True, stop=True).then_inc(s_k, 1)
            for b in range(B):
                pe.matmul(pv[:, b // 4, b % 4, :], c2[:, b, :, :], w("wv"), start=True, stop=True).then_inc(s_v, 1)

        @blk.scalar
        def _(act):
            for n in range(2):
                act.wait_ge(s_k, n + 1)
                act.activation(KT[:, 512 * n:512 * n + 512], pk[:, n, :], ACT.Identity, bias=w("bk")).then_inc(s_kt, 1)

        @blk.vector
        def _(dve):
            dve.memset(VB[:], 0.0).then_inc(s_z, 1)
            dve.wait_ge(s_z, 1)
            bv = w("bv").rearrange("p (c h d) -> p c h d", h=2, d=HD)
            for h in range(2):
                q = slice(64 * h, 64 * h + 64)
                dve.memset(VB[q, :, :, 2 * HD + h:2 * HD + h + 1], 1.0)
                for n in range(4):
                    dve.wait_ge(s_v, 4 * n + 4)
                    src = pv[q, n, :, :].rearrange("p b (c h d) -> p b c h d", h=2, d=HD)[:, :, :, h, :]
                    dst = VB[q, 4 * n:4 * n + 4, :, h * HD:h * HD + HD]
                    for bb in range(4):
                        ins = dve.tensor_tensor(dst[:, bb], src[:, bb], bv[q, :, h, :], ALU.add)
            if key_mask:
                nz = core.keep
                kt3 = KT[:].rearrange("p (b k) -> p b k", k=SK)
                dve.wait_ge(s_kt, 2)
                ins = dve.tensor_tensor(KT[:], KT[:], nz[:], ALU.mult)


def prep_key_mask(core, stack):
    core.keep = stack.enter_context(core.nc.sbuf_tensor("keep", [P, B * SK], F32))
    core.nbias3 = stack.enter_context(core.nc.sbuf_tensor("nbias3", [3, B, SK], BF16))
    core.ones3 = stack.enter_context(core.nc.sbuf_tensor("ones3", [3, P], BF16))
    with Stage(core, "kmask") as st:
        blk = st.block()

        @blk.vector
        def _(dve):
            dve.memset(core.ones3[:], 1.0)
            dve.tensor_scalar(core.keep[:], core.itok[:], 0.0, None, ALU.not_equal)
            dve.tensor_scalar(core.nbias3[:].rearrange("p b k -> p (b k)"), core.itok[0:3, :], 0.0, core.w("mha0", "neg3"),
                              ALU.is_equal, ALU.mult)


class Mask:

    def __init__(self, raw, fill, shared):
        self.raw, self.fill_value, self.shared = raw, fill / HD ** -0.5, shared


def prep_mask(core, L, mask, stack):
    nc = core.nc
    n = mask.raw.shape[1]
    sb = lambda name, shape, dt=F32: stack.enter_context(nc.sbuf_tensor(f"{name}{L}", shape, dt))
    mask.keep, mask.fill, mask.any_word = sb("keep", [P, n, SK]), sb("fill", [P, n, SK]), sb("any_word", [1, 1], I32)
    with Stage(core, f"mask{L}") as st:
        lo, lor = st.sb("lo", [P, P]), st.sb("lor", [1, 1])
        pm = st.ps("pm", [P, P])
        s_m, s_t, s_own = st.sem("m"), st.sem("t"), st.sem("own")
        blk = st.block()

        @blk.tensor
        def _(pe):
            pe.wait_ge(s_m, 1)
            pe.transpose(pm[:], lo[:], core.w("ctx", "ident")).then_inc(s_t, 1)

        @blk.vector
        def _(dve):
            link = Chain(dve, s_own)
            dve.tensor_scalar(mask.fill[:], mask.raw[:], 0.0, mask.fill_value, ALU.is_equal, ALU.mult)
            dve.memset(lo[:], 1.0)
            link(dve.tensor_scalar(mask.keep[:], mask.raw[:], 0.0, None, ALU.not_equal))
            dve.tensor_reduce(lo[:, 0:1], mask.keep[:], AX.XY, ALU.min).then_inc(s_m, 1)
            dve.wait_ge(s_t, 1)
            link(dve.tensor_reduce(lor[:], pm[0:1, :], AX.X, ALU.min))
            dve.tensor_scalar(mask.any_word[:], lor[:], -1.0, 1.0, ALU.mult, ALU.add)


def mha(core, L, mask=None, key_mask=False):
    nc = core.nc
    X, MV, RS = core.X, core.MV, core.RS
    KT, VB = core.KT[L], core.VB[L]
    ident = core.w("ctx", "ident")
    bmask = core.w("ctx", "bmask")
    w = lambda n: core.w(f"mha{L}", n)
    with Stage(core, f"mha{L}") as st:
        xh = [st.sb(f"xh{u}", [P, TB, P]) for u in range(2)]
        xT = [st.sb(f"xT{u}", [P, S]) for u in range(2)]
        qT = [st.sb(f"qT{u}", [P, S]) for u in range(2)]
        kbd = [st.sb(f"kbd{u}", [P, H, SK]) for u in range(2)]
        Z = [st.sb(f"Z{u}", [P, H, SK]) for u in range(2)]
        PR = [st.sb(f"PR{u}", [P, H * SK]) for u in range(2)]
        PT = [st.sb(f"PT{u}", [P, CH * P]) for u in range(2)]
        at = [st.sb(f"at{u}", [P, P]) for u in range(2)]
        aT = [st.sb(f"aT{u}", [P, P]) for u in range(2)]
        nm = [st.sb(f"nm{u}", [P, H]) for u in range(2)]
        rc = [st.sb(f"rc{u}", [P, CH, 2]) for u in range(2)]
        bn = [st.sb(f"bn{u}", [P, 6]) for u in range(2)]
        mv = [st.sb(f"mv{u}", [P, 2]) for u in range(2)]
        pS = st.ps("pS", [P, 2, 512])
        pT = st.ps("pT", [P, CH * P])
        pQ = st.ps("pQ", [P, 512])
        pO = st.ps("pO", [P, 512])
        pAb = st.ps("pA", [P, 512])
        pYb = st.ps("pY", [P, 512])
        pOv = pO[:, 0:CH * VW].rearrange("p (c w) -> p c w", w=VW)
        pA, pY = pAb[:, 0:P], pYb[:, 0:P]
        names = "xh bo kbd xTp xT qp q S nm Z P PTp PT O rc at aTp aT Y X bn mv msk tick".split()
        s = {n: st.sem(n) for n in names}
        rs_act, rs_dve = token_scales(core, st, MV[:, :, 1], RS[:], "a")
        blk = st.block()

        if key_mask:
            @blk.sync
            def _(sp):
                need(sp, core.loaded, 16 * core.loads)

        @blk.tensor
        def _(pe):
            def x_transposes(b, u):
                need(pe, s["xh"], 2 * b + 2)
                need(pe, s["q"], b)
                for j in range(TB):
                    ins = pe.transpose(pQ[:, P * j:P * j + P], xh[u][:, j, :], ident)
                ins.then_inc(s["xTp"], 1)

            def queries(b, u):
                need(pe, s["xT"], b + 1)
                pe.matmul(pQ[:, 0:S], w("wq"), xT[u][:], start=True, stop=True).then_inc(s["qp"], 1)

            def scores(t, b, u, v, n):
                need(pe, s["q"], b + 1)
                need(pe, s["kbd"], b + 1)
                need(pe, s["Z"], 2 * t - 1 + n)
                ins = pe.matmul(pS[:, n, :], qT[u][:, P * v:P * v + P],
                                kbd[u][:, 8 * n:8 * n + 8, :], start=True, stop=not key_mask)
                if key_mask:
                    nb = core.nbias3[:, bass.ds(b, 1), :].to_broadcast([3, 8, SK])
                    ins = pe.matmul(pS[:, n, :], core.ones3[:], nb, start=False, stop=True)
                ins.then_inc(s["S"], 1)

            def slot(a):
                if a.has(1):
                    scores(a.t(1), a.b(1), a.u(1), a.v(1), 0)
                if a.has(-1):
                    r, v = a.t(-1), a.v(-1)
                    need(pe, s["P"], r + 1)
                    need(pe, s["PT"], r)
                    for c in range(CH):
                        ins = pe.transpose(pT[:, P * c:P * c + P], PR[v][:, P * c:P * c + P], ident)
                    ins.then_inc(s["PTp"], 1)
                if a.next_x():
                    x_transposes(a.b(3), a.u(3))
                if a.has(1):
                    scores(a.t(1), a.b(1), a.u(1), a.v(1), 1)
                if a.has(-3):
                    r, v = a.t(-3), a.v(-3)
                    need(pe, s["at"], r + 1)
                    need(pe, s["aT"], r)
                    pe.transpose(pA, at[v][:], ident).then_inc(s["aTp"], 1)
                if a.next_q():
                    queries(a.b(2), a.u(2))
                if a.has(-2):
                    r, v = a.t(-2), a.v(-2)
                    need(pe, s["PT"], r + 1)
                    need(pe, s["at"], r)
                    for c in range(CH):
                        ins = pe.matmul(pOv[:, c, :], PT[v][:, P * c:P * c + P], VB[:, a.b(-2), c, :], start=True, stop=True)
                    ins.then_inc(s["O"], 1)
                if a.has(-3):
                    r, v = a.t(-3), a.v(-3)
                    need(pe, s["aT"], r + 1)
                    need(pe, s["X"], r)
                    pe.matmul(pY, aT[v][:], w("wo"), start=True, stop=True).then_inc(s["Y"], 1)

            x_transposes(0, 0)
            queries(0, 0)
            scores(0, 0, 0, 0, 0)
            scores(0, 0, 0, 0, 1)
            x_transposes(1, 1)
            tile_slots(pe, slot, 4)

        @blk.scalar
        def _(act):
            def x_evac(b, u):
                need(act, s["xTp"], b + 1)
                need(act, s["qp"], b - 1)
                act.activation(xT[u][:], pQ[:, 0:S], ACT.Copy).then_inc(s["xT"], 1)

            def q_evac(b, u):
                need(act, s["qp"], b + 1)
                need(act, s["S"], 4 * b - 4)
                act.activation(qT[u][:], pQ[:, 0:S], ACT.Identity, bias=w("bq")).then_inc(s["q"], 1)

            def slot(a):
                if a.has(0):
                    r, v = a.t(0), a.v(0)
                    need(act, s["Z"], 2 * r + 2)
                    need(act, s["PTp"], r - 1)
                    act.activation(PR[v][:], Z[v][:].rearrange("p h k -> p (h k)"), ACT.Exp, scale=HD ** -0.5).then_inc(s["P"], 1)
                if a.has(-1):
                    r, v = a.t(-1), a.v(-1)
                    need(act, s["PTp"], r + 1)
                    need(act, s["O"], r - 1)
                    act.activation(PT[v][:], pT[:], ACT.Copy).then_inc(s["PT"], 1)
                if a.next_x():
                    x_evac(a.b(3), a.u(3))
                if a.has(-3):
                    r, v = a.t(-3), a.v(-3)
                    need(act, s["aTp"], r + 1)
                    need(act, s["Y"], r)
                    act.activation(aT[v][:], pA, ACT.Copy).then_inc(s["aT"], 1)
                if a.next_q():
                    q_evac(a.b(2), a.u(2))

            rs_act(act)
            x_evac(0, 0)
            q_evac(0, 0)
            x_evac(1, 1)
            tile_slots(act, slot, 4)

        @blk.gpsimd
        def _(pool):
            def prepare(b, u):
                need(pool, s["S"], 4 * b - 4)
                kb = KT[:].rearrange("p (b k) -> p b k", k=SK)[:, bass.ds(b, 1), :].to_broadcast([P, H, SK])
                pool.tensor_tensor(kbd[u][:], kb, bmask.unsqueeze(2).to_broadcast([P, H, SK]), ALU.mult).then_inc(s["kbd"], 1)
                need(pool, s["xh"], 2 * b + 2)
                pool.tensor_tensor(X[:, bass.ds(2 * b, TB), :], X[:, bass.ds(2 * b, TB), :],
                                   w("bo").rearrange("p (t d) -> p t d", t=TB), ALU.add).then_inc(s["bo"], 1)

            prepare(0, 0)
            prepare(1, 1)
            with pool.Fori(1, B // 2) as i:
                prepare(2 * i, 0)
                prepare(2 * i + 1, 1)

        @blk.vector
        def _(dve):
            def pipeline(masked):
                def normalise(b, u):
                    need(dve, s["xTp"], b - 1)
                    for j in range(TB):
                        dve.tensor_scalar(xh[u][:, j, :], X[:, 2 * b + j, :], MV[:, 2 * b + j, 0:1], RS[:, bass.ds(2 * b + j, 1)],
                                          ALU.subtract, ALU.mult).then_inc(s["xh"], 1)

                def softmax_shift(t, v, halves=(0, 1)):
                    HH = H // 2
                    for n in halves:
                        sc = pS[:, n, :].rearrange("p (h k) -> p h k", k=SK)
                        mx = nm[v][:, HH * n:HH * n + HH]
                        need(dve, s["S"], 2 * t + n + 1)
                        if masked:
                            mi = v if mask.shared else t
                            kp = mask.keep[:, bass.ds(mi, 1), :].to_broadcast([P, HH, SK])
                            ng = mask.fill[:, bass.ds(mi, 1), :].to_broadcast([P, HH, SK])
                            dve.tensor_tensor(sc, sc, kp, ALU.mult).then_inc(s["msk"], 1)
                            need(dve, s["msk"], 4 * t + 2 * n + 1)
                            dve.tensor_tensor(sc, sc, ng, ALU.add).then_inc(s["msk"], 1)
                            need(dve, s["msk"], 4 * t + 2 * n + 2)
                        dve.tensor_reduce(mx, sc, AX.X, ALU.max, negate=True).then_inc(s["nm"], 1)
                        need(dve, s["P"], t - 1)
                        need(dve, s["nm"], 2 * t + n + 1)
                        dve.tensor_tensor(Z[v][:, HH * n:HH * n + HH, :], sc, mx.unsqueeze(2).to_broadcast([P, HH, SK]),
                                          ALU.add).then_inc(s["Z"], 1)

                def slot(a):
                    if a.has(-3):
                        r, v = a.t(-3), a.v(-3)
                        need(dve, s["O"], r + 1)
                        dve.reciprocal(rc[v][:], pOv[:, :, 2 * HD:VW]).then_inc(s["rc"], 1)
                        need(dve, s["aTp"], r)
                        need(dve, s["rc"], r + 1)
                        dve.tensor_tensor(at[v][:].rearrange("p (c h d) -> p c h d", h=2, d=HD),
                                          pOv[:, :, 0:2 * HD].rearrange("p c (h d) -> p c h d", d=HD),
                                          rc[v][:].unsqueeze(3).to_broadcast([P, CH, 2, HD]), ALU.mult).then_inc(s["at"], 1)
                    if a.next_x():
                        normalise(a.b(3), a.u(3))
                    if a.has(1):
                        softmax_shift(a.t(1), a.v(1), (0,))
                    if a.has(-4):
                        r, v = a.t(-4), a.v(-4)
                        need(dve, s["Y"], r + 1)
                        need(dve, s["bo"], a.b(-4) + 1)
                        dve.tensor_tensor(X[:, r, :], pY, X[:, r, :], ALU.add).then_inc(s["X"], 1)
                        need_apart(dve, s["X"], r + 1, s["tick"])
                        dve.bn_stats(bn[v][:], X[:, r, :]).then_inc(s["bn"], 1)
                    if a.has(1):
                        softmax_shift(a.t(1), a.v(1), (1,))
                    if a.has(-4):
                        need_apart(dve, s["bn"], r + 1, s["tick"])
                        dve.bn_aggr(mv[v][:], bn[v][:]).then_inc(s["mv"], 1)
                        need(dve, s["mv"], r + 1)
                        dve.tensor_scalar(MV[:, r, :], mv[v][:], 1.0, None, ALU.mult)

                normalise(0, 0)
                normalise(1, 1)
                softmax_shift(0, 0)
                tile_slots(dve, slot, 4)

            rs_dve(dve)
            if mask is None:
                pipeline(False)
            else:
                flag = dve.alloc_register(f"masked{L}")
                dve.reg_load(flag, mask.any_word[0:1, 0:1])
                with dve.If_eq(flag, 0):
                    pipeline(False)
                with dve.If_ne(flag, 0):
                    pipeline(True)


def batch_slots(eng, fn, lag):
    fn(0, 0)
    fn(1, 1)
    fn(2, 0)
    fn(3, 1)
    with eng.Fori(2, B // 2 - 1) as i:
        fn(2 * i, 0)
        fn(2 * i + 1, 1)
    for b in range(B - 2, B + lag):
        fn(b, b % 2)


def live(b):
    return not isinstance(b, int) or 0 <= b < B


MARK = -3e38


def prep_top(core):
    w = lambda n: core.w("top", n)
    with Stage(core, "ptop") as st:
        VT = st.sb("VT", [P, B, 2, SK])
        pk, pv, pw = st.ps("pk", [P, 2, 512]), st.ps("pv", [P, 2, 512]), st.ps("pw", [P, 4, 4, P])
        s_k, s_v, s_w = st.sem("k"), st.sem("v"), st.sem("w")
        blk = st.block()
        c2 = core.w("ctx", "ctxT2").rearrange("p (b r k) -> p b r k", r=2, k=SK)

        @blk.tensor
        def _(pe):
            for n in range(2):
                pe.matmul(pk[:, n, :], w("wk"), c2[:, 8 * n:8 * n + 8, 0, :], start=True, stop=True).then_inc(s_k, 1)
                pe.matmul(pv[:, n, :], w("wv"), c2[:, 8 * n:8 * n + 8, 0, :], start=True, stop=True).then_inc(s_k, 1)
            pe.wait_ge(s_v, 2)
            for b in range(B):
                ins = pe.matmul(pw[:, b // 4, b % 4, :], VT[:, b, :, :], w("wo"), start=True, stop=True)
                if b % 4 == 3:
                    ins.then_inc(s_w, 1)

        @blk.scalar
        def _(act):
            for n in range(2):
                act.wait_ge(s_k, 2 * n + 1)
                act.activation(core.KT[1][:, 512 * n:512 * n + 512], pk[:, n, :], ACT.Identity, bias=w("bk"))
                act.wait_ge(s_k, 2 * n + 2)
                src = pv[:, n, :].rearrange("p (b k) -> p b k", k=SK)
                for r in range(2):
                    ins = act.activation(VT[:, 8 * n:8 * n + 8, r, :], src, ACT.Identity, bias=w("bv"))
                ins.then_inc(s_v, 1)
            for n in range(4):
                act.wait_ge(s_w, n + 1)
                act.activation(core.VWo[:, 4 * n:4 * n + 4, :], pw[:, n, :, :], ACT.Copy)


def attention_top(core):
    X, MV, RS = core.X, core.MV, core.RS
    ident = core.w("ctx", "ident")
    w = lambda n: core.w("top", n)
    TOP, R8 = 32, 8
    with Stage(core, "top") as st:
        two = lambda name, shape: [st.sb(f"{name}{u}", shape) for u in range(2)]
        xh, xT, qT = two("xh", [P, TB, P]), two("xT", [P, S]), two("qT", [P, S])
        sc, wk, pr = (two(n, [P, TB, SK]) for n in ("sc", "wk", "pr"))
        pk = two("pk", [P, TB, P])
        PT = two("PT", [P, S])
        m8 = two("m8", [P, TB, TOP // R8, R8])
        nm, sm, rc = two("nm", [P, TB]), two("sm", [P, TB]), two("rc", [P, TB])
        bn, mv = st.sb("bn", [P, TB, 6]), st.sb("mv", [P, TB, 2])
        pQ = st.ps("pQ", [P, 512])
        pS = [st.ps(f"pS{u}", [P, 512]) for u in range(2)]
        pT = st.ps("pT", [P, 512])
        pY = st.ps("pY", [P, 512])
        names = "xh bo xTp xT qp q S sc top nm P pk PTp PT Y X bn own zero tick".split()
        s = {n: st.sem(n) for n in names}
        rs_act, rs_dve = token_scales(core, st, MV[:, :, 1], RS[:], "a")
        blk = st.block()

        @blk.tensor
        def _(pe):
            def x_transposes(b, u):
                need(pe, s["xh"], b + 1)
                need(pe, s["q"], b)
                for j in range(TB):
                    ins = pe.transpose(pQ[:, P * j:P * j + P], xh[u][:, j, :], ident)
                ins.then_inc(s["xTp"], 1)

            def queries(b, u):
                need(pe, s["xT"], b + 1)
                pe.matmul(pQ[:, 0:S], w("wq"), xT[u][:], start=True, stop=True).then_inc(s["qp"], 1)

            def scores(b, u):
                need(pe, s["q"], b + 1)
                need(pe, s["sc"], b - 1)
                for j in range(TB):
                    ins = pe.matmul(pS[u][:, SK * j:SK * j + SK], qT[u][:, P * j:P * j + P],
                                    core.KT[1][:, bass.ds(SK * b, SK)], start=True, stop=True)
                ins.then_inc(s["S"], 1)

            def slot(b, u):
                if live(b - 1):
                    need(pe, s["pk"], b)
                    need(pe, s["PT"], b - 1)
                    for j in range(TB):
                        ins = pe.transpose(pT[:, P * j:P * j + P], pk[1 - u][:, j, :], ident)
                    ins.then_inc(s["PTp"], 1)
                if live(b + 2):
                    x_transposes(b + 2, u)
                if live(b - 1):
                    need(pe, s["PT"], b)
                    need(pe, s["X"], b - 1)
                    for j in range(TB):
                        ins = pe.matmul(pY[:, P * j:P * j + P], PT[1 - u][:, P * j:P * j + P], core.VWo[:, b - 1, :], start=True, stop=True)
                    ins.then_inc(s["Y"], 1)
                if live(b + 2):
                    queries(b + 2, u)
                    scores(b + 2, u)

            for b in range(2):
                x_transposes(b, b)
                queries(b, b)
                scores(b, b)
            batch_slots(pe, slot, 2)

        @blk.scalar
        def _(act):
            def x_evac(b, u):
                need(act, s["xTp"], b + 1)
                need(act, s["qp"], b - 1)
                act.activation(xT[u][:], pQ[:, 0:S], ACT.Copy).then_inc(s["xT"], 1)

            def q_evac(b, u):
                need(act, s["qp"], b + 1)
                need(act, s["S"], b - 1)
                act.activation(qT[u][:], pQ[:, 0:S], ACT.Identity, bias=w("bq")).then_inc(s["q"], 1)

            def slot(b, u):
                if live(b - 1):
                    need(act, s["PTp"], b)
                    need(act, s["Y"], b - 2)
                    act.activation(PT[1 - u][:], pT[:, 0:S], ACT.Copy).then_inc(s["PT"], 1)
                if live(b + 2):
                    x_evac(b + 2, u)
                if live(b):
                    need(act, s["nm"], b + 1)
                    need(act, s["pk"], b - 1)
                    for j in range(TB):
                        ins = act.activation(pr[u][:, j, :], sc[u][:, j, :], ACT.Exp, bias=nm[u][:, j:j + 1])
                    ins.then_inc(s["P"], 1)
                if live(b + 2):
                    q_evac(b + 2, u)

            rs_act(act)
            for b in range(2):
                x_evac(b, b)
                q_evac(b, b)
            batch_slots(act, slot, 2)

        @blk.gpsimd
        def _(pool):
            def slot(b):
                need(pool, s["xh"], b + 1)
                xs = X[:, bass.ds(TB * b, TB), :]
                pool.tensor_tensor(xs, xs, w("bo").rearrange("p (t d) -> p t d", t=TB), ALU.add).then_inc(s["bo"], 1)

            with pool.Fori(0, B) as b:
                slot(b)

        @blk.vector
        def _(dve):
            OWN = TB * 2 * (TOP // R8)

            def normalise(b, u):
                need(dve, s["xTp"], b - 1)
                for j in range(TB):
                    t = TB * b + j
                    ins = dve.tensor_scalar(xh[u][:, j, :], X[:, t, :], MV[:, t, 0:1], RS[:, bass.ds(t, 1)], ALU.subtract, ALU.mult)
                ins.then_inc(s["xh"], 1)

            def best(b, u):
                need(dve, s["S"], b + 1)
                need(dve, s["P"], b - 1)
                dve.tensor_scalar(sc[u][:], pS[u][:, 0:TB * SK].rearrange("p (t k) -> p t k", t=TB), float(P) ** -0.5, None,
                                  ALU.mult).then_inc(s["sc"], 1)
                need_apart(dve, s["sc"], b + 1, s["tick"])
                n = 0
                for r in range(TOP // R8):
                    src = sc if r == 0 else wk
                    for j in range(TB):
                        n += 1
                        ins = dve.max(m8[u][:, j, r, :], src[u][:, j, :]).then_inc(s["own"], 1)
                    need_apart(dve, s["own"], OWN * b + n, s["tick"])
                    if r == 0:
                        dve.tensor_scalar(nm[u][:], m8[u][:, :, 0, 0], -1.0, None, ALU.mult).then_inc(s["nm"], 1)
                    for j in range(TB):
                        n += 1
                        dve.match_replace(wk[u][:, j, :], m8[u][:, j, r, :], src[u][:, j, :], MARK).then_inc(s["own"], 1)
                    need_apart(dve, s["own"], OWN * b + n, s["tick"])
                need(dve, s["P"], b + 1)
                need(dve, s["PTp"], b - 1)
                for j in range(TB):
                    ins = dve.scalar_tensor_tensor(pk[u][:, j, 0:SK], wk[u][:, j, :], MARK, pr[u][:, j, :], ALU.is_equal, ALU.mult,
                                                   accum_out=sm[u][:, j:j + 1])
                ins.then_inc(s["pk"], 1)
                need(dve, s["pk"], b + 1)
                dve.reciprocal(rc[u][:], sm[u][:]).then_inc(s["top"], 1)

            def final(b, u):
                need(dve, s["Y"], b + 1)
                need(dve, s["bo"], b + 1)
                need(dve, s["top"], b + 1)
                for j in range(TB):
                    t = TB * b + j
                    ins = dve.scalar_tensor_tensor(X[:, t, :], pY[:, P * j:P * j + P], rc[u][:, j:j + 1], X[:, t, :], ALU.mult, ALU.add)
                ins.then_inc(s["X"], 1)
                need_apart(dve, s["X"], b + 1, s["tick"])
                for j in range(TB):
                    ins = dve.bn_stats(bn[:, j, :], X[:, TB * b + j, :])
                ins.then_inc(s["bn"], 1)
                need_apart(dve, s["bn"], 2 * b + 1, s["tick"])
                for j in range(TB):
                    ins = dve.bn_aggr(mv[:, j, :], bn[:, j, :])
                ins.then_inc(s["bn"], 1)
                need(dve, s["bn"], 2 * b + 2)
                dve.tensor_scalar(MV[:, bass.ds(TB * b, TB), :], mv[:], 1.0, None, ALU.mult)

            def slot(b, u):
                if live(b - 2):
                    final(b - 2, u)
                if live(b + 2):
                    normalise(b + 2, u)
                if live(b):
                    best(b, u)

            for u in range(2):
                dve.memset(pk[u][:, :, SK:P], 0.0).then_inc(s["zero"], 1)
            rs_dve(dve)
            normalise(0, 0)
            normalise(1, 1)
            batch_slots(dve, slot, 2)


NROT, NE, EH = 4, 6, 256
TAYLOR = 8
SQUARINGS = 6


def fold_rotations(core):
    w = lambda n: core.w("rot", n)
    ident = core.w("ctx", "ident")
    N4 = NROT * P
    with Stage(core, "rot") as st:
        A1, A1T = st.sb("A1", [P, N4]), st.sb("A1T", [P, N4])
        E = [st.sb(f"E{u}", [P, N4]) for u in range(2)]
        ET = [st.sb(f"ET{u}", [P, N4]) for u in range(2)]
        tmp, R = st.sb("tmp", [P, N4]), st.sb("R", [P, P])
        MT, M34 = st.sb("MT", [P, P]), st.sb("M34", [P, P])
        pE, pF = st.ps("pE", [P, N4]), st.ps("pF", [P, N4])
        pW = st.ps("pW", [P, 3, 512])
        pB = st.ps("pB", [P, 512])
        s_pe, s_dve, s_own = st.sem("pe"), st.sem("dve"), st.sem("own")
        blk = st.block()
        g = lambda t, n: t[:, P * n:P * n + P]

        @blk.tensor
        def _(pe):
            step = 0
            for k in range(TAYLOR - 1, 0, -1):
                step += 1
                pe.wait_ge(s_dve, step)
                for n in range(NROT):
                    ins = pe.matmul(g(pE, n), g(A1T, n), g(E[(step - 1) % 2], n), start=True, stop=True)
                ins.then_inc(s_pe, 1)
            u = step % 2
            step += 1
            pe.wait_ge(s_dve, step)
            for n in range(NROT):
                ins = pe.transpose(g(pF, n), g(E[u], n), ident)
            ins.then_inc(s_pe, 1)
            for k in range(SQUARINGS):
                step += 1
                pe.wait_ge(s_dve, step)
                for n in range(NROT):
                    pe.matmul(g(pE, n), g(ET[k % 2], n), g(E[(u + k) % 2], n), start=True, stop=True)
                    ins = pe.matmul(g(pF, n), g(E[(u + k) % 2], n), g(ET[k % 2], n), start=True, stop=True)
                ins.then_inc(s_pe, 1)
            step += 1
            pe.wait_ge(s_dve, step)
            v, vT = (u + SQUARINGS) % 2, SQUARINGS % 2
            pe.matmul(g(pE, 0), g(E[v], 1), g(ET[vT], 0), start=True, stop=True)
            pe.matmul(g(pE, 1), g(ET[vT], 2), g(E[v], 3), start=True, stop=True).then_inc(s_pe, 1)
            step += 1
            pe.wait_ge(s_dve, step)
            pe.matmul(g(pF, 0), MT[:], M34[:], start=True, stop=True).then_inc(s_pe, 1)
            step += 1
            pe.wait_ge(s_dve, step)
            for c in range(2 * NE):
                pe.matmul(pW[:, c // 4, P * (c % 4):P * (c % 4) + P], w("ew2T")[:, P * c:P * c + P], R[:], start=True, stop=True)
            pe.matmul(pB[0:NE, 0:P], w("eb2T"), R[:], start=True, stop=True).then_inc(s_pe, 1)

        @blk.vector
        def _(dve):
            link = Chain(dve, s_own)
            dve.tensor_scalar(A1[:], w("gens"), 2.0 ** -SQUARINGS, None, ALU.mult).then_inc(s_own, 1)
            dve.tensor_scalar(A1T[:], w("gensT"), 2.0 ** -SQUARINGS, None, ALU.mult).then_inc(s_own, 1)
            link.n = 2
            dve.wait_ge(s_own, 2)
            dve.tensor_scalar(E[0][:], A1[:], 1.0 / TAYLOR, None, ALU.mult).then_inc(s_dve, 1)
            step, u = 0, 0
            for k in range(TAYLOR - 1, 0, -1):
                step += 1
                dve.wait_ge(s_pe, step)
                link(dve.tensor_tensor(tmp[:], pE[:], A1[:], ALU.add))
                dve.tensor_scalar(E[step % 2][:], tmp[:], 1.0 / k, None, ALU.mult).then_inc(s_dve, 1)
            u = step % 2
            step += 1
            dve.wait_ge(s_pe, step)
            dve.tensor_copy(ET[0][:], pF[:]).then_inc(s_dve, 1)
            for k in range(SQUARINGS):
                step += 1
                dve.wait_ge(s_pe, step)
                if k == 0:
                    dve.wait_ge(s_dve, step)
                else:
                    dve.wait_ge(s_dve, step)
                dve.scalar_tensor_tensor(E[(u + k + 1) % 2][:], E[(u + k) % 2][:], 2.0, pE[:], ALU.mult, ALU.add).then_inc(s_own, 1)
                link.n += 1
                dve.wait_ge(s_own, link.n)
                dve.scalar_tensor_tensor(ET[(k + 1) % 2][:], ET[k % 2][:], 2.0, pF[:], ALU.mult, ALU.add).then_inc(s_dve if k < SQUARINGS - 1 else s_own, 1)
            link.n += 1
            dve.wait_ge(s_own, link.n)
            v, vT = (u + SQUARINGS) % 2, SQUARINGS % 2
            i4 = ident.unsqueeze(1).to_broadcast([P, NROT, P])
            m4 = lambda t: t[:].rearrange("p (n d) -> p n d", n=NROT)
            link(dve.tensor_tensor(m4(E[v]), m4(E[v]), i4, ALU.add))
            dve.tensor_tensor(m4(ET[vT]), m4(ET[vT]), i4, ALU.add).then_inc(s_dve, 1)
            step += 1
            dve.wait_ge(s_pe, step)
            dve.tensor_copy(MT[:], g(pE, 0)).then_inc(s_own, 1)
            link.n += 1
            dve.wait_ge(s_own, link.n)
            dve.tensor_copy(M34[:], g(pE, 1)).then_inc(s_dve, 1)
            step += 1
            dve.wait_ge(s_pe, step)
            dve.tensor_copy(R[:], g(pF, 0)).then_inc(s_dve, 1)
            step += 1
            dve.wait_ge(s_pe, step)
            for n in range(3):
                dve.tensor_copy(core.W2R[:, 512 * n:512 * n + 512], pW[:, n, :])
            dve.tensor_copy(core.b2R[:], pB[0:NE, 0:P])


GT = 4
NG = T // GT


def group_slots(eng, fn):
    fn(0, 0)
    fn(1, 1)
    with eng.Fori(1, NG // 2 - 1) as i:
        fn(2 * i, 0)
        fn(2 * i + 1, 1)
    fn(NG - 2, 0)
    fn(NG - 1, 1)


def more(g, n=1):
    return not isinstance(g, int) or g + n < NG


def ffn_moe_rotated(core):
    X, MV, RS = core.X, core.MV, core.RS
    ident = core.w("ctx", "ident")
    w = lambda n: core.w("ffn0", n)
    NP = NE + 2
    with Stage(core, "ffn0") as st:
        RR = st.sb("RR", [P, T])
        v2 = st.sb("v2", [P, T])
        xn = [st.sb(f"xn{u}", [P, GT, P]) for u in range(2)]
        xh = [st.sb(f"xh{u}", [P, GT, P]) for u in range(2)]
        xT = [st.sb(f"xT{u}", [P, GT * P]) for u in range(2)]
        hid = [st.sb(f"hid{u}", [P, 2, GT * P]) for u in range(2)]
        acc = [st.sb(f"acc{u}", [P, GT, P]) for u in range(2)]
        ab = [st.sb(f"ab{u}", [P, GT, P]) for u in range(2)]
        wt = [st.sb(f"wt{u}", [P, GT, NE]) for u in range(2)]
        wT = [st.sb(f"wT{u}", [NE, GT * P]) for u in range(2)]
        lg, oa, ob, pr = (st.sb(n, [P, GT, NE]) for n in ("lg", "oa", "ob", "pr"))
        sm = st.sb("sm", [P, 8, GT])
        junk = st.sb("junk", [P, P])
        zz = st.sb("zz", [P, 2, GT])
        gz = st.sb("gz", [P, 2, GT])
        bn = st.sb("bn", [P, GT, 6])
        mv = st.sb("mv", [P, GT, 2])
        pX, pG, pI, pA = (st.ps(n, [P, 512]) for n in ("pX", "pG", "pI", "pA"))
        pH = [st.ps(f"pH{u}", [P, 512]) for u in range(2)]
        pE = [st.ps(f"pE{u}", [P, GT, P]) for u in range(2)]
        names = ("xn xhp xr xTp xT lg wt wTp wT in0 acc H h O cmb ab D pab z gt xf own df th z2 own2 own3 vv tick").split()
        s = {n: st.sem(n) for n in names}
        rs_act, rs_dve = token_scales(core, st, MV[:, :, 1], RS[:], "a")
        rr_act, rr_dve = token_scales(core, st, v2[:], RR[:], "b")
        blk = st.block()

        @blk.tensor
        def _(pe):
            def x_transposes(g, u):
                need(pe, s["xn"], g + 1)
                need(pe, s["xT"], g)
                for j in range(GT):
                    ins = pe.transpose(pX[:, P * j:P * j + P], xn[u][:, j, :], ident)
                ins.then_inc(s["xTp"], 1)

            def logits(g, u):
                need(pe, s["xT"], g + 1)
                need(pe, s["wT"], g)
                for j in range(GT):
                    ins = pe.matmul(pG[:, NE * j:NE * j + NE], xT[u][:, P * j:P * j + P], w("gate_w"), start=True, stop=True)
                ins.then_inc(s["lg"], 1)

            def weights_T(g, u):
                need(pe, s["wt"], g + 1)
                for j in range(GT):
                    ins = pe.transpose(pG[0:NE, P * j:P * j + P], wt[u][:, j, :], ident)
                ins.then_inc(s["wTp"], 1)

            def bias_rows(g, u):
                need(pe, s["wT"], g + 1)
                need(pe, s["acc"], g)
                for j in range(GT):
                    ins = pe.matmul(pI[:, P * j:P * j + P], wT[u][:, P * j:P * j + P], core.b2R[:], start=True, stop=True)
                ins.then_inc(s["in0"], 1)

            def up(g, u, p):
                w1 = w("ew1")[:, EH * p:EH * p + EH] if p < NE else w("aw1")[:, EH * (p - NE):EH * (p - NE) + EH]
                for c in range(2):
                    need(pe, s["h"], 2 * NP * g + 2 * p + c - 1)
                    pe.matmul(pH[c][:], w1[:, P * c:P * c + P], xT[u][:], start=True, stop=True).then_inc(s["H"], 1)

            def down(g, p):
                need(pe, s["h"], 2 * NP * g + 2 * p + 2)
                if p < NE:
                    need(pe, s["cmb"], NE * g + p - 1)
                elif p == NE:
                    need(pe, s["ab"], g)
                for j in range(GT):
                    for c in range(2):
                        hc = hid[p % 2][:, c, P * j:P * j + P]
                        if p < NE:
                            r = 2 * p + c
                            ins = pe.matmul(pE[p % 2][:, j, :], hc, core.W2R[:, P * r:P * r + P], start=(c == 0), stop=(c == 1))
                        else:
                            r = 2 * (p - NE) + c
                            ins = pe.matmul(pA[:, P * j:P * j + P], hc, w("aw2")[:, P * r:P * r + P],
                                            start=(r == 0 and j == 0), stop=(r == 3), skip_group_check=True)
                ins.then_inc(s["O"], 1)

            def group(g, u):
                for p in range(NP):
                    up(g, u, p)
                    if p > 0:
                        down(g, p - 1)
                    elif not isinstance(g, int) or g > 0:
                        down(g - 1, NP - 1)
                    if more(g):
                        if p == 1:
                            x_transposes(g + 1, 1 - u)
                        if p == 2:
                            logits(g + 1, 1 - u)
                        if p == 4:
                            weights_T(g + 1, 1 - u)
                        if p == 6:
                            bias_rows(g + 1, 1 - u)

            x_transposes(0, 0)
            logits(0, 0)
            weights_T(0, 0)
            bias_rows(0, 0)
            group_slots(pe, group)
            down(NG - 1, NP - 1)

        @blk.scalar
        def _(act):
            def x_evac(g, u):
                need(act, s["xTp"], g + 1)
                need(act, s["H"], 2 * NP * (g - 1))
                act.activation(xT[u][:], pX[:], ACT.Identity, bias=w("ln_b"), scale=w("ln_g")).then_inc(s["xT"], 1)

            def tanh_half(g):
                need(act, s["df"], g + 1)
                act.activation(sm[:, 5, :], sm[:, 4, :], ACT.Tanh, scale=0.5).then_inc(s["th"], 1)

            def w_evac(g, u):
                need(act, s["wTp"], g + 1)
                act.activation(wT[u][:], pG[0:NE, :], ACT.Copy).then_inc(s["wT"], 1)

            def acc_evac(g, u):
                need(act, s["in0"], g + 1)
                need(act, s["xf"], g - 1)
                act.activation(acc[u][:].rearrange("p t d -> p (t d)"), pI[:], ACT.Copy).then_inc(s["acc"], 1)

            def gate(g):
                need(act, s["z"], g + 1)
                act.activation(gz[:, 0, :], zz[:, 0, :], ACT.Tanh, scale=0.5).then_inc(s["gt"], 1)

            def group(g, u):
                for p in range(NP):
                    for c in range(2):
                        r = 2 * p + c
                        need(act, s["H"], 2 * NP * g + r + 1)
                        need(act, s["O"], NP * g + p - 1)
                        b = w("eb1")[:, r:r + 1] if p < NE else w("ab1")[:, r - 2 * NE:r - 2 * NE + 1]
                        act.activation(hid[p % 2][:, c, :], pH[c][:], ACT.Gelu, bias=b).then_inc(s["h"], 1)
                    if more(g):
                        if p == 1:
                            x_evac(g + 1, 1 - u)
                        if p == 3:
                            tanh_half(g + 1)
                        if p == 4:
                            w_evac(g + 1, 1 - u)
                        if p == 6:
                            acc_evac(g + 1, 1 - u)
                    if p == 1 and (not isinstance(g, int) or g > 0):
                        gate(g - 1)

            rs_act(act)
            rr_act(act)
            x_evac(0, 0)
            tanh_half(0)
            w_evac(0, 0)
            acc_evac(0, 0)
            group_slots(act, group)
            gate(NG - 1)

        @blk.gpsimd
        def _(pool):
            def residual(g, u):
                need(pool, s["xhp"], g + 1)
                pool.tensor_tensor(X[:, bass.ds(GT * g, GT), :], X[:, bass.ds(GT * g, GT), :], xh[u][:], ALU.add).then_inc(s["xr"], 1)

            def add_abel(g, u):
                need(pool, s["ab"], g + 1)
                need(pool, s["xr"], g + 1)
                pool.tensor_tensor(X[:, bass.ds(GT * g, GT), :], X[:, bass.ds(GT * g, GT), :], ab[u][:], ALU.add).then_inc(s["pab"], 1)

            def group(g, u):
                if more(g):
                    residual(g + 1, 1 - u)
                if not isinstance(g, int) or g > 0:
                    add_abel(g - 1, 1 - u)

            residual(0, 0)
            group_slots(pool, group)
            add_abel(NG - 1, 1)

        @blk.vector
        def _(dve):
            GATE = 16

            def normalise(g, u):
                need(dve, s["xTp"], g - 1)
                need(dve, s["xr"], g - 1)
                for j in range(GT):
                    t = GT * g + j
                    ins = dve.tensor_scalar(xn[u][:, j, :], X[:, t, :], MV[:, t, 0:1], RR[:, bass.ds(t, 1)], ALU.subtract, ALU.mult)
                ins.then_inc(s["xn"], 1)
                for j in range(GT):
                    t = GT * g + j
                    ins = dve.tensor_scalar(xh[u][:, j, :], X[:, t, :], MV[:, t, 0:1], RS[:, bass.ds(t, 1)], ALU.subtract, ALU.mult)
                ins.then_inc(s["xhp"], 1)

            def gating(g, u):
                n = [0]

                def link(ins):
                    n[0] += 1
                    ins.then_inc(s["own"], 1)
                    dve.wait_ge(s["own"], GATE * g + n[0])

                bc = lambda a: a.unsqueeze(2).to_broadcast([P, GT, NE])
                row = lambda a: a.unsqueeze(1).to_broadcast([P, GT, NE])
                need(dve, s["lg"], g + 1)
                need(dve, s["th"], g)
                link(dve.tensor_tensor(lg[:], pG[:, 0:GT * NE].rearrange("p (t e) -> p t e", e=NE), row(w("gate_b")), ALU.add))
                for k, (o, m) in enumerate(((oa, 0), (ob, 2))):
                    link(dve.tensor_reduce(sm[:, m, :], lg[:], AX.X, ALU.max))
                    link(dve.tensor_tensor(pr[:], lg[:], bc(sm[:, m, :]), ALU.is_equal))
                    link(dve.tensor_tensor(pr[:], pr[:], row(w("prio")), ALU.mult))
                    link(dve.tensor_reduce(sm[:, m + 1, :], pr[:], AX.X, ALU.max))
                    link(dve.tensor_tensor(o[:], pr[:], bc(sm[:, m + 1, :]), ALU.is_equal))
                    if k == 0:
                        link(dve.scalar_tensor_tensor(lg[:], o[:], -3e38, lg[:], ALU.mult, ALU.add))
                dve.tensor_tensor(sm[:, 4, :], sm[:, 0, :], sm[:, 2, :], ALU.subtract).then_inc(s["df"], 1)
                need(dve, s["th"], g + 1)
                link(dve.tensor_scalar(sm[:, 6, :], sm[:, 5, :], 0.5, 0.5, ALU.mult, ALU.add))
                link(dve.tensor_scalar(sm[:, 7, :], sm[:, 5, :], -0.5, 0.5, ALU.mult, ALU.add))
                link(dve.tensor_tensor(oa[:], oa[:], bc(sm[:, 6, :]), ALU.mult))
                link(dve.tensor_tensor(ob[:], ob[:], bc(sm[:, 7, :]), ALU.mult))
                assert n[0] == GATE
                dve.tensor_tensor(wt[u][:], oa[:], ob[:], ALU.add).then_inc(s["wt"], 1)
                need(dve, s["wt"], g + 1)

            def combine(g, u, p):
                need(dve, s["O"], NP * g + p + 1)
                if p == 0:
                    need(dve, s["acc"], g + 1)
                else:
                    need(dve, s["cmb"], NE * g + p)
                for j in range(GT):
                    ins = dve.scalar_tensor_tensor(acc[u][:, j, :], pE[p % 2][:, j, :], wt[u][:, j, p:p + 1], acc[u][:, j, :], ALU.mult, ALU.add)
                ins.then_inc(s["cmb"], 1)

            def tail(g, u):
                need(dve, s["O"], NP * g + NP)
                need(dve, s["pab"], g)
                dve.tensor_tensor(ab[u][:], pA[:].rearrange("p (t d) -> p t d", t=GT), w("ab2").unsqueeze(1).to_broadcast([P, GT, P]),
                                  ALU.add).then_inc(s["ab"], 1)
                need(dve, s["ab"], g + 1)
                need(dve, s["gt"], g)
                for j in range(GT):
                    dve.tensor_tensor_reduce(junk[:], ab[u][:, j, :], w("g1"), 1.0, 0.0, ALU.mult, ALU.add, zz[:, 0, j:j + 1]).then_inc(s["own2"], 1)
                    dve.wait_ge(s["own2"], 2 * GT * g + 2 * j + 1)
                    dve.tensor_tensor_reduce(junk[:], acc[u][:, j, :], w("g2"), 1.0, 0.0, ALU.mult, ALU.add, zz[:, 1, j:j + 1]).then_inc(s["own2"], 1)
                    dve.wait_ge(s["own2"], 2 * GT * g + 2 * j + 2)
                dve.tensor_tensor(zz[:, 0, :], zz[:, 0, :], zz[:, 1, :], ALU.add).then_inc(s["z2"], 1)
                need(dve, s["z2"], g + 1)
                dve.tensor_scalar(zz[:, 0, :], zz[:, 0, :], w("gc_b"), None, ALU.add).then_inc(s["z"], 1)
                dve.tensor_tensor(acc[u][:], acc[u][:], ab[u][:], ALU.subtract).then_inc(s["D"], 1)

            def final(g, u):
                need(dve, s["gt"], g + 1)
                dve.tensor_scalar(gz[:, 1, :], gz[:, 0, :], 0.5, 0.5, ALU.mult, ALU.add).then_inc(s["own3"], 1)
                need(dve, s["own3"], g * 3 + 1)
                need(dve, s["D"], g + 1)
                need(dve, s["pab"], g + 1)
                for j in range(GT):
                    t = GT * g + j
                    ins = dve.scalar_tensor_tensor(X[:, t, :], acc[u][:, j, :], gz[:, 1, j:j + 1], X[:, t, :], ALU.mult, ALU.add)
                ins.then_inc(s["xf"], 1)
                need_apart(dve, s["xf"], g + 1, s["tick"])
                for j in range(GT):
                    ins = dve.bn_stats(bn[:, j, :], X[:, GT * g + j, :])
                ins.then_inc(s["own3"], 1)
                need_apart(dve, s["own3"], g * 3 + 2, s["tick"])
                for j in range(GT):
                    ins = dve.bn_aggr(mv[:, j, :], bn[:, j, :])
                ins.then_inc(s["own3"], 1)
                need(dve, s["own3"], g * 3 + 3)
                dve.tensor_scalar(MV[:, bass.ds(GT * g, GT), :], mv[:], 1.0, None, ALU.mult)

            def group(g, u):
                if not isinstance(g, int) or g > 0:
                    tail(g - 1, 1 - u)
                if more(g):
                    normalise(g + 1, 1 - u)
                for p in range(NE):
                    combine(g, u, p)
                    if p == 0 and (not isinstance(g, int) or g > 0):
                        final(g - 1, 1 - u)
                    if p == 1 and more(g):
                        gating(g + 1, 1 - u)

            rs_dve(dve)
            dve.tensor_tensor(v2[:], MV[:, :, 1], RS[:], ALU.mult).then_inc(s["vv"], 1)
            dve.wait_ge(s["vv"], 1)
            dve.tensor_tensor(v2[:], v2[:], RS[:], ALU.mult).then_inc(s["vv"], 1)
            dve.wait_ge(s["vv"], 2)
            rr_dve(dve)
            dve.tensor_tensor(RR[:], RR[:], RS[:], ALU.mult).then_inc(s["vv"], 1)
            dve.wait_ge(s["vv"], 3)
            normalise(0, 0)
            gating(0, 0)
            group_slots(dve, group)
            tail(NG - 1, 1)
            final(NG - 1, 1)


N1, H1 = 16, 256
CAP = -(-5 * T * P // (4 * N1))
BITS = 28
SUB = [(0, P), (P, P), (2 * P, CAP - 2 * P)]


def route_top1(core):
    X, MV, RS = core.X, core.MV, core.RS
    nc = core.nc
    ident = core.w("ctx", "ident")
    w = lambda n: core.w("route", n)
    slots = core.slots
    with Stage(core, "route") as st:
        XH = core.XH
        xT = [st.sb(f"xT{u}", [P, GT * P]) for u in range(2)]
        ex, oh, mv, ca, cb, kp = (st.sb(n, [P, T, N1]) for n in ("ex", "oh", "mv", "ca", "cb", "kp"))
        mx, sm, vv = (st.sb(n, [P, T]) for n in ("mx", "sm", "vv"))
        MT = st.sb("MT", [P, 4 * P])
        ones = st.sb("ones", [P, 4 * P])
        hit = st.sb("hit", [P, 4 * P])
        cand, thr, cnt, ge = (st.sb(n, [P, 2]) for n in ("cand", "thr", "cnt", "ge"))
        dg, rows = st.sb("dg", [N1, 2 * N1]), st.sb("rows", [P, 2 * N1])
        zero = st.sb("zero", [P, P])
        pX, pL, pM, pC, pP, pR = (st.ps(n, [P, 512]) for n in ("pX", "pL", "pM", "pC", "pP", "pR"))
        names = "xh xTp xT L own cnt tot thr dx ex mvp MTp rowsp dgr eqr ca prf z zst sl zfill".split()
        s = {n: st.sem(n) for n in names}
        s["scat"] = core.gpsimd_dma_sem("scattered")
        rs_act, rs_dve = token_scales(core, st, MV[:, :, 1], RS[:], "a")
        blk = st.block()
        SH = [P, T, N1]
        te = lambda t: t[:].rearrange("p (t e) -> p t e", e=N1)
        bt = lambda a: a.unsqueeze(2).to_broadcast(SH)
        be = lambda a: a.unsqueeze(1).to_broadcast(SH)

        @blk.tensor
        def _(pe):
            pe.sem_inc(s["L"], 1)
            with pe.Fori(0, NG // 2) as i:
                for u in range(2):
                    g = 2 * i + u
                    pe.wait_ge(s["xh"], g + 1)
                    pe.wait_ge(s["z"], g + 1)
                    for j in range(GT):
                        ins = pe.transpose(pX[:, P * j:P * j + P], core.xg[u][:, j, :], ident)
                    ins.then_inc(s["xTp"], 1)
                    pe.wait_ge(s["xT"], g + 1)
                    for j in range(GT):
                        ins = pe.matmul(pL[:, bass.ds((GT * g + j) * N1, N1)], xT[u][:, P * j:P * j + P], w("Wg"), start=True, stop=True)
                    ins.then_inc(s["L"], 1)
            pe.wait_ge(s["mvp"], 1)
            for j in range(4):
                ins = pe.transpose(pM[:, P * j:P * j + P], mv[:].rearrange("p t e -> p (t e)")[:, P * j:P * j + P], ident)
            ins.then_inc(s["MTp"], 1)
            with pe.Fori(0, BITS + 1) as k:
                pe.wait_ge(s["cnt"], k + 1)
                pe.matmul(pC[:, 0:1], w("same"), cnt[:, 0:1], start=True, stop=True).then_inc(s["tot"], 1)
            pe.wait_ge(s["dgr"], 1)
            pe.matmul(pR[:, 0:2 * N1], ones[0:N1, 0:P], dg[:], start=True, stop=True).then_inc(s["rowsp"], 1)
            for n in range(2):
                src = (ca, kp)[n]
                pe.wait_ge(s["eqr"], n + 1)
                pe.matmul(pP[:], w("below"), src[:].rearrange("p t e -> p (t e)"), start=True, stop=False)
                pe.wait_ge(s["ca"], n + 1)
                pe.matmul(pP[:], ones[:, 0:P], cb[:].rearrange("p t e -> p (t e)"), start=False, stop=True).then_inc(s["prf"], 1)

        @blk.scalar
        def _(act):
            rs_act(act)
            act.sem_inc(s["z"], 1)
            with act.Fori(0, NG // 2) as i:
                for u in range(2):
                    act.wait_ge(s["xTp"], 2 * i + u + 1)
                    act.activation(xT[u][:], pX[:], ACT.Copy).then_inc(s["xT"], 1)
                    act.wait_ge(s["xT"], 2 * i + u + 1)
                    act.sem_inc(s["z"], 1)
            act.wait_ge(s["dx"], 1)
            act.activation(ex[:], ex[:], ACT.Exp).then_inc(s["ex"], 1)

        @blk.vector
        def _(dve):
            link = Chain(dve, s["own"])
            dve.memset(ones[:], 1.0)
            dve.memset(zero[:], 0.0).then_inc(s["zst"], 1)
            rs_dve(dve)
            with dve.Fori(0, NG // 2) as i:
                for u in range(2):
                    g = 2 * i + u
                    if u == 0:
                        dve.wait_ge(s["L"], 2 * i + 1)
                    for j in range(GT):
                        t = GT * g + j
                        ins = dve.tensor_scalar(core.xg[u][:, j, :], X[:, t, :], MV[:, t, 0:1], RS[:, bass.ds(t, 1)], ALU.subtract, ALU.mult)
                    ins.then_inc(s["xh"], 1)
            dve.wait_ge(s["L"], NG + 1)
            L3 = pL[:].rearrange("p (t e) -> p t e", e=N1)
            link(dve.tensor_reduce(mx[:], L3, AX.X, ALU.max))
            dve.tensor_tensor(ex[:], L3, bt(mx[:]), ALU.subtract).then_inc(s["dx"], 1)
            for t in range(T):
                dve.tensor_scalar(XH[:, t, :], X[:, t, :], MV[:, t, 0:1], RS[:, t:t + 1], ALU.subtract, ALU.mult)
            dve.wait_ge(s["ex"], 1)
            link(dve.tensor_reduce(mx[:], ex[:], AX.X, ALU.max))
            link(dve.tensor_reduce(sm[:], ex[:], AX.X, ALU.add))
            link(dve.reciprocal(vv[:], sm[:]))
            link(dve.tensor_tensor(vv[:], vv[:], mx[:], ALU.mult))
            link(dve.tensor_tensor(oh[:], ex[:], bt(mx[:]), ALU.is_equal))
            link(dve.tensor_tensor(oh[:], oh[:], be(w("prio")), ALU.mult))
            link(dve.tensor_reduce(mx[:], oh[:], AX.X, ALU.max))
            link(dve.tensor_tensor(oh[:], oh[:], bt(mx[:]), ALU.is_equal))
            dve.tensor_tensor(mv[:], oh[:], bt(vv[:]), ALU.mult).then_inc(s["mvp"], 1)
            dve.memset(thr[:], 0.0)
            link(dve.memset(cand[:], 1.0))
            dve.wait_ge(s["MTp"], 1)
            link(dve.tensor_copy(MT[:], pM[:]))
            own0 = link.n
            with dve.Fori(0, BITS) as k:
                dve.scalar_tensor_tensor(hit[:], MT[:], cand[:, 0:1], ones[:], ALU.is_ge, ALU.mult, accum_out=cnt[:, 0:1]).then_inc(s["cnt"], 1)
                dve.wait_ge(s["tot"], k + 1)
                dve.tensor_scalar(ge[:, 0:1], pC[:, 0:1], float(CAP), w("pow2")[:, bass.ds(k, 1)], ALU.is_ge, ALU.mult).then_inc(s["thr"], 1)
                dve.wait_ge(s["thr"], 2 * k + 1)
                dve.tensor_scalar(thr[:, 0:1], thr[:, 0:1], ge[:, 0:1], None, ALU.add).then_inc(s["thr"], 1)
                dve.wait_ge(s["thr"], 2 * k + 2)
                dve.tensor_scalar(cand[:, 0:1], w("pow2")[:, bass.ds(k + 1, 1)], thr[:, 0:1], None, ALU.add).then_inc(s["own"], 1)
                dve.wait_ge(s["own"], own0 + k + 1)
            link.n = own0 + BITS
            dve.scalar_tensor_tensor(hit[:], MT[:], thr[:, 0:1], ones[:], ALU.is_gt, ALU.mult, accum_out=cnt[:, 0:1]).then_inc(s["cnt"], 1)
            dve.wait_ge(s["tot"], BITS + 1)
            link(dve.tensor_scalar(ge[:, 0:1], pC[:, 0:1], -1.0, float(CAP), ALU.mult, ALU.add))
            dve.tensor_scalar(dg[:, 0:N1], ident[0:N1, 0:N1], thr[0:N1, 0:1], None, ALU.mult).then_inc(s["own"], 1)
            link.n += 1
            dve.wait_ge(s["own"], link.n)
            dve.tensor_scalar(dg[:, N1:2 * N1], ident[0:N1, 0:N1], ge[0:N1, 0:1], None, ALU.mult).then_inc(s["dgr"], 1)
            dve.wait_ge(s["rowsp"], 1)
            link(dve.tensor_copy(rows[:], pR[:, 0:2 * N1]))
            link(dve.tensor_tensor(ca[:], mv[:], be(rows[:, 0:N1]), ALU.is_equal))
            dve.tensor_tensor(ca[:], ca[:], oh[:], ALU.mult).then_inc(s["eqr"], 1)
            dve.wait_ge(s["eqr"], 1)

            def tiles_before(src):
                link(dve.memset(cb[:, 0:1, :], 0.0))
                link(dve.tensor_copy(cb[:, 1:T, :], src[:, 0:T - 1, :]))
                a, b = cb, ex
                for d in (1, 2, 4, 8, 16):
                    dve.tensor_copy(b[:, 0:d, :], a[:, 0:d, :])
                    last = dve.tensor_tensor(b[:, d:T, :], a[:, d:T, :], a[:, 0:T - d, :], ALU.add)
                    link(last)
                    a, b = b, a
                dve.tensor_copy(cb[:], a[:]).then_inc(s["ca"], 1)

            tiles_before(ca)
            link(dve.tensor_tensor(kp[:], mv[:], be(rows[:, 0:N1]), ALU.is_gt))
            dve.wait_ge(s["prf"], 1)
            P3 = pP[:].rearrange("p (t e) -> p t e", e=N1)
            link(dve.tensor_tensor(ex[:], P3, be(rows[:, N1:2 * N1]), ALU.is_lt))
            link(dve.tensor_tensor(ex[:], ex[:], ca[:], ALU.mult))
            dve.tensor_tensor(kp[:], kp[:], ex[:], ALU.add).then_inc(s["eqr"], 1)
            dve.wait_ge(s["eqr"], 2)
            tiles_before(kp)
            link(dve.tensor_reduce(sm[:], kp[:], AX.X, ALU.add))
            dve.wait_ge(s["prf"], 2)
            link(dve.tensor_tensor(ex[:], P3, be(w("base")), ALU.add))
            link(dve.tensor_tensor(ex[:], ex[:], kp[:], ALU.mult))
            link(dve.tensor_reduce(mx[:], ex[:], AX.X, ALU.add))
            link(dve.tensor_scalar(sm[:], sm[:], -float(2 * N1 * CAP), float(2 * N1 * CAP), ALU.mult, ALU.add))
            dve.tensor_tensor(slots[:], sm[:], mx[:], ALU.add).then_inc(s["sl"], 1)

        @blk.sync
        def _(sp):
            sp.dma_start(core.pack["tree_full"][:], core.A["tree_full"]).then_inc(core.trees_loaded, 16)
            sp.wait_ge(s["zst"], 1)
            for q in range(N1 * CAP // P):
                sp.dma_start(core.xs[P * q:P * q + P, :], zero[:]).then_inc(s["zfill"], 16)

        @blk.gpsimd
        def _(pool):
            pool.wait_ge(s["sl"], 1)
            pool.wait_ge(s["zfill"], 16 * (N1 * CAP // P))
            for t in range(T):
                pool.indirect_dma_start(core.xs[:, :], bass.IndirectOffsetOnAxis(ap=slots[:, t:t + 1], axis=0), XH[:, t, :], None,
                                        bounds_check=N1 * CAP - 1, oob_is_err=False).then_inc(s["scat"], 16)
            pool.wait_ge(s["scat"], 16 * T)


def run_experts(core):
    X, MV = core.X, core.MV
    ident = core.w("ctx", "ident")
    w = lambda n: core.w("route", n)
    A = core.A
    with Stage(core, "exp") as st:
        two = lambda name, shape: [st.sb(f"{name}{u}", shape) for u in range(2)]
        W1, W2, b2, xe = two("W1", [P, H1]), two("W2", [P, 2, P]), two("b2", [P, P]), two("xe", [P, 3, P])
        xT, hid, ye = two("xT", [P, CAP]), two("hid", [P, 2, CAP]), two("ye", [P, 3, P])
        YG = core.XH
        bn, mv = st.sb("bn", [P, GT, 6]), st.sb("mv", [P, GT, 2])
        pX = [st.ps(f"pX{u}", [P, 512]) for u in range(2)]
        pH = [st.ps(f"pH{u}", [P, 512]) for u in range(2)]
        pY = [st.ps(f"pY{u}", [P, 512]) for u in range(2)]
        names = "xTp xT H h Yp Y own bn".split()
        s = {n: st.sem(n) for n in names}
        s_ld, s_st = [st.sem(f"ld{u}") for u in range(2)], [core.gpsimd_dma_sem(f"rows_stored{u}") for u in range(2)]
        s_g = [core.gpsimd_dma_sem(f"gathered{u}") for u in range(4)]
        blk = st.block()
        LD = 16 * 5

        @blk.sync
        def _(sp):
            def load(e, i, u):
                need(sp, s["Yp"], e - 1)
                need(sp, s["Y"], e - 1)
                sp.dma_start(W1[u][:], A["L1_W1"][bass.ds(e, 1), :, :].rearrange("e d h -> (e d) h")).then_inc(s_ld[u], 16)
                sp.dma_start(W2[u][:], A["L1_W2"][bass.ds(e, 1), :, :].rearrange("e (c h) d -> (e h) c d", c=2)).then_inc(s_ld[u], 16)
                sp.dma_start(b2[u][:], A["L1_b2"][bass.ds(e, 1), :].to_broadcast([P, P])).then_inc(s_ld[u], 16)
                sp.dma_start(xe[u][:, 0:2, :], core.xs[bass.ds(CAP * e, 2 * P), :].rearrange("(t p) d -> p t d", t=2)).then_inc(s_ld[u], 16)
                sp.dma_start(xe[u][0:CAP - 2 * P, 2, :], core.xs[bass.ds(CAP * e + 2 * P, CAP - 2 * P), :]).then_inc(s_ld[u], 16)

            load(0, 0, 0)
            load(1, 0, 1)
            with sp.Fori(1, N1 // 2) as i:
                load(2 * i, i, 0)
                load(2 * i + 1, i, 1)

        @blk.tensor
        def _(pe):
            def expert(e, i, u):
                pe.wait_ge(s_ld[u], LD * (i + 1))
                for j, (o, n) in enumerate(SUB):
                    ins = pe.transpose(pX[u][:, o:o + n], xe[u][0:n, j, :], ident[0:n, 0:n])
                ins.then_inc(s["xTp"], 1)
                need(pe, s["xT"], e + 1)
                for c in range(2):
                    need(pe, s["h"], 2 * e + c - 1)
                    pe.matmul(pH[c][:, 0:CAP], W1[u][:, P * c:P * c + P], xT[u][:], start=True, stop=True).then_inc(s["H"], 1)
                need(pe, s["h"], 2 * e + 2)
                need(pe, s["Y"], e - 1)
                for j, (o, n) in enumerate(SUB):
                    for c in range(2):
                        ins = pe.matmul(pY[u][0:n, P * j:P * j + P], hid[u][:, c, o:o + n], W2[u][:, c, :], start=(c == 0), stop=(c == 1))
                ins.then_inc(s["Yp"], 1)

            expert(0, 0, 0)
            expert(1, 0, 1)
            with pe.Fori(1, N1 // 2) as i:
                expert(2 * i, i, 0)
                expert(2 * i + 1, i, 1)

        @blk.scalar
        def _(act):
            def expert(e, i, u):
                for c in range(2):
                    need(act, s["H"], 2 * e + c + 1)
                    need(act, s["Yp"], e - 1)
                    act.activation(hid[u][:, c, :], pH[c][:, 0:CAP], ACT.Gelu_apprx_tanh,
                                   bias=w("b1")[:, bass.ds(2 * e + c, 1)]).then_inc(s["h"], 1)

            expert(0, 0, 0)
            expert(1, 0, 1)
            with act.Fori(1, N1 // 2) as i:
                expert(2 * i, i, 0)
                expert(2 * i + 1, i, 1)

        @blk.vector
        def _(dve):
            def expert(e, i, u):
                need(dve, s["xTp"], e + 1)
                need(dve, s["H"], 2 * (e - 1))
                dve.tensor_copy(xT[u][:], pX[u][:, 0:CAP]).then_inc(s["xT"], 1)
                need(dve, s["Yp"], e + 1)
                need(dve, s_st[u], 32 * i)
                for j, (o, n) in enumerate(SUB):
                    ins = dve.tensor_tensor(ye[u][0:n, j, :], pY[u][0:n, P * j:P * j + P], b2[u][0:n, :], ALU.add)
                ins.then_inc(s["Y"], 1)

            expert(0, 0, 0)
            expert(1, 0, 1)
            with dve.Fori(1, N1 // 2) as i:
                expert(2 * i, i, 0)
                expert(2 * i + 1, i, 1)
            split_trees(core, st, dve)
            for g in range(NG):
                dve.wait_ge(s_g[g % 4], 16 * GT * (g // 4 + 1))
                x4 = X[:, GT * g:GT * g + GT, :]
                dve.tensor_tensor(x4, x4, YG[:, GT * g:GT * g + GT, :], ALU.add).then_inc(s["own"], 1)
                dve.wait_ge(s["own"], g + 1)
                for j in range(GT):
                    ins = dve.bn_stats(bn[:, j, :], X[:, GT * g + j, :])
                ins.then_inc(s["bn"], 1)
                dve.wait_ge(s["bn"], g + 1)
                for j in range(GT):
                    dve.bn_aggr(MV[:, GT * g + j, :], bn[:, j, :])

        @blk.gpsimd
        def _(pool):
            def store(e, i, u):
                need(pool, s["Y"], e + 1)
                pool.dma_start(core.ys[bass.ds(CAP * e, 2 * P), :].rearrange("(t p) d -> p t d", t=2), ye[u][:, 0:2, :]).then_inc(s_st[u], 16)
                pool.dma_start(core.ys[bass.ds(CAP * e + 2 * P, CAP - 2 * P), :], ye[u][0:CAP - 2 * P, 2, :]).then_inc(s_st[u], 16)

            store(0, 0, 0)
            store(1, 0, 1)
            with pool.Fori(1, N1 // 2) as i:
                store(2 * i, i, 0)
                store(2 * i + 1, i, 1)
            for u in range(2):
                pool.wait_ge(s_st[u], 16 * N1)
            for t in range(T):
                g = t // GT
                if g >= 4 and t % GT == 0:
                    pool.wait_ge(s_g[g % 4], 16 * GT * (g // 4))
                pool.indirect_dma_start(YG[:, t, :], None, core.ys[:, :], bass.IndirectOffsetOnAxis(ap=core.slots[:, t:t + 1], axis=0),
                                        bounds_check=N1 * CAP - 1, oob_is_err=False).then_inc(s_g[g % 4], 16)


NT, LW, NLEAF = 3, 64, 16
NCH = NLEAF * LW // P
STEPS = NT * NCH
SELP = 64
MIXC = NCH * P + P
BIG = 2.0 ** 100
GT_P = GT * P


def tree_buffers(core, stack):
    sb = lambda name, shape, dt: stack.enter_context(core.nc.sbuf_tensor(name, shape, dt))
    core.w1h, core.w2h = sb("w1h", [P, STEPS * P], F32R), sb("w2h", [P, STEPS * P], F32R)
    core.w1l, core.w2l = sb("w1l", [P, STEPS * P], F32R), sb("w2l", [P, STEPS * P], F32R)
    core.mix = sb("mix", [P, 2, MIXC], BF16)


def split_trees(core, st, dve):
    w = lambda n: core.w("tree_full", n)
    dve.wait_ge(core.trees_loaded, 16)
    link = Chain(dve, st.sem("split"))
    t1, t2 = st.sb("t1", [P, MIXC], BF16), st.sb("t2", [P, MIXC], BF16)
    r = st.sb("r", [P, MIXC])
    for full, hi, lo in ((w("w1"), core.w1h, core.w1l), (w("w2"), core.w2h, core.w2l)):
        link(dve.tensor_copy(hi[:], full))
        dve.tensor_tensor(lo[:], full, hi[:], ALU.subtract)
    part = lambda rows, i: core.w("tree", "part")[0:rows, i:i + 1]
    for n, (name, rows) in enumerate((("mixqk", P), ("mixv", SELP))):
        q = slice(0, rows)
        out = core.mix[q, n, :]
        link(dve.tensor_copy(t1[q, :], w(name)))
        link(dve.tensor_tensor(r[q, :], w(name), t1[q, :], ALU.subtract))
        link(dve.tensor_copy(t2[q, :], r[q, :]))
        link(dve.tensor_tensor(r[q, :], r[q, :], t2[q, :], ALU.subtract))
        link(dve.tensor_scalar(t1[q, :], t1[q, :], part(rows, 0), None, ALU.mult))
        link(dve.scalar_tensor_tensor(t1[q, :], t2[q, :], part(rows, 1), t1[q, :], ALU.mult, ALU.add))
        link(dve.scalar_tensor_tensor(out, r[q, :], part(rows, 2), t1[q, :], ALU.mult, ALU.add))


def attention_trees(core):
    X, MV, RS = core.X, core.MV, core.RS
    ident = core.w("ctx", "ident")
    w = lambda n: core.w("tree", n)
    SC = float(P) ** -0.5
    with Stage(core, "tree") as st:
        two = lambda name, shape, dt=F32: [st.sb(f"{name}{u}", shape, dt) for u in range(2)]
        xh, xT = st.sb("xh", [P, GT, P]), st.sb("xT", [P, GT_P])
        xTh, xTl = two("xTh", [P, GT_P], F32R), two("xTl", [P, GT_P], F32R)
        zs, go = st.sb("zs", [P, GT * NT, NLEAF]), st.sb("go", [P, GT * NT, NLEAF, 2])
        r2, r3 = st.sb("r2", [P, GT * NT, 2, 2]), st.sb("r3", [P, GT * NT, 4, 2])
        r4 = st.sb("r4", [P, GT * NT, 8, 2])
        oh = st.sb("oh", [P, GT, NT + 1, 4, NLEAF])
        sel = two("sel", [P, 2, GT_P], BF16)
        hh, hl = two("hh", [P, GT_P], F32R), two("hl", [P, GT_P], F32R)
        qT, kT, vv = two("qT", [P, GT_P]), two("kT", [P, GT_P]), two("vv", [P, GT_P])
        vT = st.sb("vT", [P, GT_P])
        pr, PT = two("pr", [P, S]), two("PT", [P, S])
        nm, sm, rc = two("nm", [P, 1]), two("sm", [P, 1]), two("rc", [P, 1])
        bn, mv = two("bn", [P, 6]), two("mv", [P, 2])
        pX, pS, pT, pO = (st.ps(n, [P, 512]) for n in ("pX", "pS", "pT", "pO"))
        pH = [st.ps(f"pH{u}", [P, 512]) for u in range(2)]
        pY = [st.ps(f"pY{u}", [P, 512]) for u in range(2)]
        names = "xh xTp xT xs np own oh ohp sel zero H h lo c Y y vTp v S nm mx P PTp PT O rc X bn mv tick".split()
        s = {n: st.sem(n) for n in names}
        rs_act, rs_dve = token_scales(core, st, MV[:, :, 1], RS[:], "a")
        blk = st.block()
        past = lambda g: not isinstance(g, int) or g > 0
        rows = lambda p: (slice(SELP * (p % 2), SELP * (p % 2) + SELP), p // 2)

        @blk.tensor
        def _(pe):
            def x_transposes(g, u):
                need(pe, s["xh"], g + 1)
                need(pe, s["sel"], 2 * g)
                for j in range(GT):
                    ins = pe.transpose(pX[:, P * j:P * j + P], xh[:, j, :], ident)
                ins.then_inc(s["xTp"], 1)

            def nodes(g, u):
                need(pe, s["xT"], g + 1)
                for j in range(GT):
                    ins = pe.matmul(pX[:, NT * NLEAF * j:NT * NLEAF * (j + 1)], xT[:, P * j:P * j + P], w("nodes"), start=True, stop=True)
                ins.then_inc(s["np"], 1)

            def select(g, u, n):
                if n == 0:
                    need(pe, s["oh"], g + 1)
                else:
                    need(pe, s["sel"], 2 * g + 1)
                for j in range(GT):
                    src = oh[:, j, 2 * n:2 * n + 2, :, :].rearrange("p n r l -> p (n r l)")
                    ins = pe.transpose(pX[:, P * j:P * j + P], src, ident)
                ins.then_inc(s["ohp"], 1)

            def hidden(g, u, k):
                m = STEPS * g + k
                p, c = divmod(k, NCH)
                if k == 0:
                    need(pe, s["xs"], g + 1)
                    need(pe, s["sel"], 2 * g + 2)
                need(pe, s["lo"], m - 1)
                q, n = rows(p)
                k0 = slice(P * k, P * k + P)
                pe.matmul(pH[k % 2][:], core.w1h[:, k0], xTh[u][:], start=True, stop=False)
                pe.matmul(pH[k % 2][:], core.w1h[:, k0], xTl[u][:], start=False, stop=False)
                pe.matmul(pH[k % 2][:], core.w1l[:, k0], xTh[u][:], start=False, stop=False)
                pe.matmul(pH[k % 2][:], core.mix[q, n, P * c:P * c + P], sel[u][q, n, :], start=False, stop=True).then_inc(s["H"], 1)

            def out(g, u, k):
                m = STEPS * g + k
                p, c = divmod(k, NCH)
                q, n = rows(p)
                bank = pY[(u + p) % 2]
                if c == 0:
                    need(pe, s["y"], NT * g + p - 1)
                need(pe, s["lo"], m + 1)
                k0 = slice(P * k, P * k + P)
                b2 = core.mix[q, n, NCH * P:MIXC]
                parts = ((hh, core.w2h), (hh, core.w2l), (hl, core.w2h))
                for i, (h, w2) in enumerate(parts):
                    ins = pe.matmul(bank[:], w2[:, k0], h[k % 2][:], start=(c == 0 and i == 0), stop=False)
                ins.then_inc(s["c"], 1)
                if c == NCH - 1:
                    pe.matmul(bank[:], b2, sel[u][q, n, :], start=False, stop=True).then_inc(s["Y"], 1)

            def v_transposes(g, u):
                need(pe, s["y"], NT * (g + 1))
                need(pe, s["PT"], GT * g)
                for j in range(GT):
                    ins = pe.transpose(pT[:, P * j:P * j + P], vT[:, P * j:P * j + P], ident)
                ins.then_inc(s["vTp"], 1)

            def scores(g, u, j):
                t = GT * g + j
                need(pe, s["y"], NT * (g + 1))
                need(pe, s["P"], t)
                b0 = S * (j // TB)
                pe.matmul(pS[:, 0:S], qT[u][:, P * j:P * j + P], kT[u][:, b0:b0 + S], start=True, stop=True).then_inc(s["S"], 1)

            def turn(g, u, j):
                t = GT * g + j
                need(pe, s["P"], t + 1)
                need(pe, s["PT"], t)
                if j == 0:
                    need(pe, s["v"], g + 1)
                for n in range(TB):
                    ins = pe.transpose(pT[:, P * n:P * n + P], pr[j % 2][:, P * n:P * n + P], ident)
                ins.then_inc(s["PTp"], 1)

            def attend(g, u, j):
                t = GT * g + j
                need(pe, s["PT"], t + 1)
                need(pe, s["X"], t)
                for n in range(TB):
                    k0 = P * (TB * (j // TB) + n)
                    ins = pe.matmul(pO[:, 0:P], PT[j % 2][:, P * n:P * n + P], vv[u][:, k0:k0 + P], start=(n == 0), stop=(n == TB - 1))
                ins.then_inc(s["O"], 1)

            def attention(g, u, k):
                if k == 1:
                    v_transposes(g, u)
                for j in range(GT):
                    if k == 3 * j + 1:
                        scores(g, u, j)
                    if k == 3 * j + 4:
                        turn(g, u, j)
                    if k == 3 * j + 6:
                        attend(g, u, j)

            def group(g, u):
                for k in range(STEPS):
                    if k < STEPS - 1:
                        hidden(g, u, k + 1)
                    elif more(g):
                        hidden(g + 1, 1 - u, 0)
                    if past(g):
                        attention(g - 1, 1 - u, k)
                    if more(g):
                        if k == 14:
                            x_transposes(g + 1, 1 - u)
                        if k == 16:
                            nodes(g + 1, 1 - u)
                        if k == 20:
                            select(g + 1, 1 - u, 0)
                        if k == 21:
                            select(g + 1, 1 - u, 1)
                    out(g, u, k)

            x_transposes(0, 0)
            nodes(0, 0)
            select(0, 0, 0)
            select(0, 0, 1)
            hidden(0, 0, 0)
            group_slots(pe, group)
            for k in range(STEPS):
                attention(NG - 1, 1, k)

        @blk.scalar
        def _(act):
            def hidden(g, u, k):
                m = STEPS * g + k
                need(act, s["H"], m + 1)
                need(act, s["c"], m - 1)
                act.activation(hh[k % 2][:], pH[k % 2][:], ACT.Relu).then_inc(s["h"], 1)

            def x_evac(g, u):
                need(act, s["xTp"], g + 1)
                need(act, s["xs"], g)
                act.activation(xT[:], pX[:], ACT.Copy).then_inc(s["xT"], 1)

            def out(g, u, p):
                need(act, s["Y"], NT * g + p + 1)
                if p == 0:
                    need(act, s["O"], GT * (g - 1))
                if p == 2:
                    need(act, s["vTp"], g)
                act.activation((qT[u], kT[u], vT)[p][:], pY[(u + p) % 2][:], ACT.Copy).then_inc(s["y"], 1)

            def attention(g, u, k):
                if k == 1:
                    need(act, s["vTp"], g + 1)
                    act.activation(vv[u][:], pT[:], ACT.Copy).then_inc(s["v"], 1)
                for j in range(GT):
                    t = GT * g + j
                    if k == 3 * j + 2:
                        need(act, s["nm"], t + 1)
                        need(act, s["PTp"], t - 1)
                        need(act, s["rc"], t - 1)
                        act.activation(pr[j % 2][:], pS[:, 0:S], ACT.Exp, bias=nm[j % 2][:, 0:1], scale=SC,
                                       accum_out=sm[j % 2][:, 0:1]).then_inc(s["P"], 1)
                    if k == 3 * j + 4:
                        need(act, s["PTp"], t + 1)
                        need(act, s["O"], t - 1)
                        act.activation(PT[j % 2][:], pT[:, 0:S], ACT.Copy).then_inc(s["PT"], 1)

            def group(g, u):
                for k in range(STEPS):
                    hidden(g, u, k)
                    if k == 0 and past(g):
                        out(g - 1, 1 - u, 2)
                    if k in (NCH, 2 * NCH):
                        out(g, u, k // NCH - 1)
                    if past(g):
                        attention(g - 1, 1 - u, k)
                    if k == 14 and more(g):
                        x_evac(g + 1, 1 - u)

            rs_act(act)
            x_evac(0, 0)
            group_slots(act, group)
            out(NG - 1, 1, 2)
            for k in range(STEPS):
                attention(NG - 1, 1, k)

        @blk.vector
        def _(dve):
            def normalise(g, u):
                need(dve, s["xTp"], g)
                for j in range(GT):
                    t = GT * g + j
                    ins = dve.tensor_scalar(xh[:, j, :], X[:, t, :], MV[:, t, 0:1], RS[:, bass.ds(t, 1)], ALU.subtract, ALU.mult)
                ins.then_inc(s["xh"], 1)

            LINKS = 5

            def route(g, u, step):
                def link(n, ins):
                    ins.then_inc(s["own"], 1)
                    need(dve, s["own"], LINKS * g + n)
                if step == 0:
                    need(dve, s["xT"], g + 1)
                    link(1, dve.tensor_copy(xTh[u][:], xT[:]))
                if step == 1:
                    dve.tensor_tensor(xTl[u][:], xT[:], xTh[u][:], ALU.subtract).then_inc(s["xs"], 1)
                if step == 2:
                    need(dve, s["np"], g + 1)
                    nb = w("node_b").rearrange("p (n l) -> p n l", l=NLEAF).unsqueeze(1).to_broadcast([P, GT, NT, NLEAF])
                    link(2, dve.tensor_tensor(zs[:].rearrange("p (t n) l -> p t n l", n=NT),
                                              pX[:, 0:GT * NT * NLEAF].rearrange("p (t n l) -> p t n l", n=NT, l=NLEAF), nb, ALU.add))
                    dve.tensor_scalar(go[:, :, :, 1], zs[:], 0.0, None, ALU.is_ge)
                    link(3, dve.tensor_scalar(go[:, :, :, 0], zs[:], 0.0, None, ALU.is_lt))
                if step == 3:
                    link(4, dve.tensor_tensor(r2[:], go[:, :, 1:3, :], go[:, :, 0, :].unsqueeze(3).to_broadcast([P, GT * NT, 2, 2]), ALU.mult))
                    r2f = r2[:].rearrange("p t a b -> p t (a b)")
                    link(5, dve.tensor_tensor(r3[:], go[:, :, 3:7, :], r2f.unsqueeze(3).to_broadcast([P, GT * NT, 4, 2]), ALU.mult))
                    r3f = r3[:].rearrange("p t a b -> p t (a b)")
                    dve.tensor_tensor(r4[:], go[:, :, 7:15, :], r3f.unsqueeze(3).to_broadcast([P, GT * NT, 8, 2]), ALU.mult).then_inc(s["zero"], 1)
                if step == 4:
                    need(dve, s["zero"], g + 2)
                    need(dve, s["ohp"], 2 * g)
                    r4f = r4[:].rearrange("p t a b -> p t (a b)")
                    for j in range(GT):
                        leaves = r4f[:, NT * j:NT * j + NT, :].unsqueeze(2).to_broadcast([P, NT, 4, NLEAF])
                        ins = dve.tensor_copy(oh[:, j, 0:NT, :, :], leaves)
                    ins.then_inc(s["oh"], 1)
                if step in (5, 6):
                    n = step - 5
                    need(dve, s["ohp"], 2 * g + n + 1)
                    r = P if n == 0 else SELP
                    dve.tensor_scalar(sel[u][0:r, n, :], pX[0:r, :], w("part")[0:r, 3:4], None, ALU.subtract).then_inc(s["sel"], 1)

            def low(g, u, k):
                m = STEPS * g + k
                need(dve, s["h"], m + 1)
                dve.scalar_tensor_tensor(hl[k % 2][:], pH[k % 2][:], 0.0, hh[k % 2][:], ALU.max, ALU.subtract).then_inc(s["lo"], 1)

            def shift(g, u, j):
                t = GT * g + j
                need(dve, s["S"], t + 1)
                need(dve, s["P"], t - 1)
                dve.tensor_reduce(nm[j % 2][:], pS[:, 0:S], AX.X, ALU.max, negate=True).then_inc(s["mx"], 1)
                need(dve, s["mx"], t + 1)
                dve.tensor_scalar(nm[j % 2][:], nm[j % 2][:], SC, None, ALU.mult).then_inc(s["nm"], 1)

            def final(g, u, j):
                t = GT * g + j
                need(dve, s["P"], t + 1)
                dve.reciprocal(rc[j % 2][:], sm[j % 2][:]).then_inc(s["rc"], 1)
                need(dve, s["rc"], t + 1)
                need(dve, s["O"], t + 1)
                dve.scalar_tensor_tensor(X[:, t, :], pO[:, 0:P], rc[j % 2][:, 0:1], X[:, t, :], ALU.mult, ALU.add).then_inc(s["X"], 1)

            def statistics(g, u, j):
                t = GT * g + j
                need_apart(dve, s["X"], t + 1, s["tick"])
                dve.bn_stats(bn[j % 2][:], X[:, t, :]).then_inc(s["bn"], 1)
                need_apart(dve, s["bn"], t + 1, s["tick"])
                dve.bn_aggr(mv[j % 2][:], bn[j % 2][:]).then_inc(s["mv"], 1)
                need(dve, s["mv"], t + 1)
                dve.tensor_scalar(MV[:, t, :], mv[j % 2][:], 1.0, None, ALU.mult)

            def attention(g, u, k):
                for j in range(GT):
                    if k == 3 * j + 1:
                        shift(g, u, j)
                    if k == 3 * j + 6:
                        final(g, u, j)
                    if k == 3 * j + 8:
                        statistics(g, u, j)

            def group(g, u):
                for k in range(STEPS):
                    low(g, u, k)
                    if past(g):
                        attention(g - 1, 1 - u, k)
                    if more(g):
                        if k == 12:
                            normalise(g + 1, 1 - u)
                        if 15 <= k < 22:
                            route(g + 1, 1 - u, k - 15)

            rs_dve(dve)
            dve.memset(oh[:], 0.0).then_inc(s["zero"], 1)
            normalise(0, 0)
            for step in range(7):
                route(0, 0, step)
            group_slots(dve, group)
            for k in range(STEPS):
                attention(NG - 1, 1, k)


MAGIC = 1.5 * 2.0 ** 23


def quantised_linear(core):
    X, MV, RS, XH = core.X, core.MV, core.RS, core.XH
    ident = core.w("ctx", "ident")
    w = lambda n: core.w("q8", n)
    with Stage(core, "q8") as st:
        two = lambda name, shape, dt=F32: [st.sb(f"{name}{u}", shape, dt) for u in range(2)]
        W8, idb = st.sb("W8", [P, P], BF16), st.sb("idb", [P, P], BF16)
        XQ = st.sb("XQ", [P, T, P], BF16)
        qT, yo = two("qT", [P, GT_P], BF16), two("yo", [P, GT, P])
        am, amr, one, xs = st.sb("am", [P, NG]), st.sb("amr", [P, P]), st.sb("one", [1, P]), st.sb("xs", [P, 2])
        pA, pB = st.ps("pA", [P, 512]), st.ps("pB", [P, 512])
        pT = [st.ps(f"pT{u}", [P, 1024], BF16) for u in range(2)]
        pY = [st.ps(f"pY{u}", [P, 512]) for u in range(2)]
        names = "w8 own amx amt am1 xsp xq qTp qT Y o b out".split()
        s = {n: st.sem(n) for n in names}
        rs_act, rs_dve = token_scales(core, st, MV[:, :, 1], RS[:], "a")
        blk = st.block()

        @blk.tensor
        def _(pe):
            pe.wait_ge(s["amx"], 1)
            pe.transpose(pA[:, 0:P], amr[:], ident).then_inc(s["amt"], 1)
            pe.wait_ge(s["am1"], 1)
            pe.matmul(pB[:, 0:1], one[:], xs[0:1, 0:1], start=True, stop=True).then_inc(s["xsp"], 1)
            pe.wait_ge(s["w8"], 2)

            def turn(g):
                pe.wait_ge(s["xq"], g + 1)
                if g >= 2:
                    pe.wait_ge(s["qT"], g - 1)
                for j in range(GT):
                    ins = pe.transpose(pT[g % 2][:, P * j:P * j + P], XQ[:, GT * g + j, :], idb[:])
                ins.then_inc(s["qTp"], 1)

            turn(0)
            for g in range(NG):
                if g + 1 < NG:
                    turn(g + 1)
                pe.wait_ge(s["qT"], g + 1)
                if g >= 2:
                    pe.wait_ge(s["o"], g - 1)
                for j in range(GT):
                    ins = pe.matmul(pY[g % 2][:, P * j:P * j + P], qT[g % 2][:, P * j:P * j + P], W8[:], start=True, stop=True)
                ins.then_inc(s["Y"], 1)

        @blk.scalar
        def _(act):
            rs_act(act)
            act.activation(W8[:], core.W8i[:].bitcast(I8), ACT.Copy).then_inc(s["w8"], 1)
            act.activation(idb[:], ident, ACT.Copy).then_inc(s["w8"], 1)
            for g in range(NG):
                act.wait_ge(s["qTp"], g + 1)
                if g >= 2:
                    act.wait_ge(s["Y"], g - 1)
                act.activation(qT[g % 2][:], pT[g % 2][:, 0:GT_P], ACT.Copy).then_inc(s["qT"], 1)

        @blk.gpsimd
        def _(pool):
            for g in range(NG):
                pool.wait_ge(s["b"], g + 1)
                x4 = X[:, GT * g:GT * g + GT, :]
                pool.tensor_tensor(x4, x4, w("bias").unsqueeze(1).to_broadcast([P, GT, P]), ALU.add).then_inc(s["out"], 1)

        @blk.vector
        def _(dve):
            link = Chain(dve, s["own"])
            dve.memset(one[:], 1.0)
            dve.memset(amr[:], 0.0)
            rs_dve(dve)
            for g in range(NG):
                for j in range(GT):
                    t = GT * g + j
                    ins = dve.tensor_scalar(XH[:, t, :], X[:, t, :], MV[:, t, 0:1], RS[:, t:t + 1], ALU.subtract, ALU.mult)
                ins.then_inc(s["b"], 1)
                dve.wait_ge(s["b"], g + 1)
                ins = dve.tensor_reduce(am[:, g:g + 1], XH[:, GT * g:GT * g + GT, :], AX.XY, ALU.max, apply_absolute_value=True)
            link(ins)
            dve.tensor_reduce(amr[:, 0:1], am[:], AX.X, ALU.max).then_inc(s["amx"], 1)
            dve.wait_ge(s["amt"], 1)
            dve.tensor_reduce(xs[0:1, 0:1], pA[0:1, 0:P], AX.X, ALU.max).then_inc(s["am1"], 1)
            dve.wait_ge(s["xsp"], 1)
            link(dve.tensor_scalar(xs[:, 1:2], pB[:, 0:1], 1.0 / 127.0, EPS, ALU.mult, ALU.max))
            link(dve.reciprocal(xs[:, 0:1], xs[:, 1:2]))
            for g in range(NG):
                x4 = XH[:, GT * g:GT * g + GT, :]
                link(dve.tensor_scalar(x4, x4, xs[:, 0:1], MAGIC, ALU.mult, ALU.add))
                link(dve.tensor_scalar(x4, x4, MAGIC, 127.0, ALU.subtract, ALU.min))
                dve.tensor_scalar(XQ[:, GT * g:GT * g + GT, :], x4, -128.0, None, ALU.max).then_inc(s["xq"], 1)
            for g in range(NG):
                dve.wait_ge(s["Y"], g + 1)
                yv = pY[g % 2][:].rearrange("p (t d) -> p t d", t=GT)
                dve.scalar_tensor_tensor(yo[g % 2][:], yv, xs[:, 1:2], w("wscale").unsqueeze(1).to_broadcast([P, GT, P]),
                                         ALU.mult, ALU.mult).then_inc(s["o"], 1)
                dve.wait_ge(s["o"], g + 1)
                dve.wait_ge(s["out"], g + 1)
                x4 = X[:, GT * g:GT * g + GT, :]
                dve.tensor_tensor(x4, x4, yo[g % 2][:], ALU.add).then_inc(s["b"], 1)

        @blk.sync
        def _(sp):
            for g in range(NG):
                sp.wait_ge(s["b"], NG + g + 1)
                sp.dma_start(core.A["out"].rearrange("(t p) d -> p t d", p=P)[:, GT * g:GT * g + GT, :],
                             X[:, GT * g:GT * g + GT, :]).then_inc(core.stored, 16)
            sp.wait_ge(core.stored, 16 * NG)


PACKS = ("ctx", "mha0", "top", "route", "mha2", "tree", "mha3", "q8")


def tiles(a, n=T):
    return a.rearrange("(t p) d -> p t d", t=n)


def place(core, stack, names):
    for name in names:
        width = max(hi for _, hi, _ in core.lay[name].values())
        core.pack[name] = stack.enter_context(core.nc.sbuf_tensor("w_" + name, [P, width], F32))


def load(core):
    A = core.A
    core.loads = 0
    with Stage(core, "load") as st:
        s_first, s_bn = st.sem("first"), st.sem("bn")
        s_x = [st.sem(f"x{q}") for q in range(NG)]
        bn = st.sb("bn", [P, T, 6])
        blk = st.block()

        @blk.sync
        def _(sp):
            for q in range(NG):
                sp.dma_start(core.X[:, GT * q:GT * q + GT, :], tiles(A["x"])[:, GT * q:GT * q + GT, :]).then_inc(s_x[q], 16)
                if q == 0:
                    for name in ("ctx", "mha0"):
                        sp.dma_start(core.pack[name][:], A[name]).then_inc(s_first, 16)
                    sp.dma_start(core.itok[:], A["itok"].to_broadcast([P, B * SK])).then_inc(s_first, 16)

            def later(to, src):
                sp.dma_start(to, src).then_inc(core.loaded, 16)
                core.loads += 1

            for name in ("rot", "ffn0"):
                later(core.pack[name][:], A[name])
            for name in PACKS[2:]:
                later(core.pack[name][:], A[name])
            later(core.W8i[:], A["W8"])
            later(core.raw2[:], tiles(A["mask2"], TB))
            for q in range(NG):
                later(core.raw3[:, GT * q:GT * q + GT, :], tiles(A["mask3"])[:, GT * q:GT * q + GT, :])
            sp.wait_ge(s_first, 48)

        @blk.vector
        def _(dve):
            for q in range(NG):
                dve.wait_ge(s_x[q], 16)
                for t in range(GT * q, GT * q + GT):
                    ins = dve.bn_stats(bn[:, t, :], core.X[:, t, :])
                ins.then_inc(s_bn, 1)
                dve.wait_ge(s_bn, q + 1)
                for t in range(GT * q, GT * q + GT):
                    dve.bn_aggr(core.MV[:, t, :], bn[:, t, :])


def four_layers(nc, A, layouts):
    with ExitStack() as ctx:
        core = Core(nc, ctx, A, layouts)
        core.loaded = ctx.enter_context(nc.semaphore("loaded"))
        core.stored = ctx.enter_context(nc.semaphore("stored"))
        core.KT, core.VB = {}, {}
        core.XH = core.sb("XH", [P, T, P])
        place(core, ctx, PACKS)
        core.W8i = core.sb("W8i", [P, P // 4], I32)
        core.raw2, core.raw3 = core.sb("raw2", [P, TB, SK], I32), core.sb("raw3", [P, T, SK])
        core.slots = core.sb("slots", [P, T], I32)
        core.xs = nc.dram_tensor("slots_in", [N1 * CAP, P], F32, kind="Internal").ap()
        core.ys = nc.dram_tensor("slots_out", [N1 * CAP, P], F32, kind="Internal").ap()
        sb = lambda stack, name, shape, dt=F32: stack.enter_context(nc.sbuf_tensor(name, shape, dt))

        def attention(L, stack, mask=None):
            core.KT[L], core.VB[L] = sb(stack, f"KT{L}", [P, B * SK]), sb(stack, f"VB{L}", [P, B, CH, VW])
            if mask is None:
                prep_key_mask(core, stack)
            else:
                prep_mask(core, L, mask, stack)
            prep_mha(core, L, mask is None)
            mha(core, L, mask, key_mask=mask is None)

        with ExitStack() as layer0:
            core.W2R, core.b2R = sb(layer0, "W2R", [P, 2 * NE * P]), sb(layer0, "b2R", [NE, P])
            place(core, layer0, ["ffn0"])
            with ExitStack() as early:
                place(core, early, ["rot"])
                core.itok = sb(early, "itok", [P, B * SK], I32)
                load(core)
                attention(0, early)
                fold_rotations(core)
            ffn_moe_rotated(core)
        with ExitStack() as layer:
            core.KT[1], core.VWo = sb(layer, "KT1", [P, B * SK]), sb(layer, "VWo", [P, B, P])
            prep_top(core)
            attention_top(core)
        with ExitStack() as trees:
            tree_buffers(core, trees)
            with ExitStack() as layer:
                core.trees_loaded = ctx.enter_context(nc.semaphore("trees_loaded"))
                place(core, layer, ["tree_full"])
                core.xg = [sb(layer, f"xg{u}", [P, GT, P]) for u in range(2)]
                route_top1(core)
                run_experts(core)
            with ExitStack() as layer:
                attention(2, layer, Mask(core.raw2, -1e-9, True))
            attention_trees(core)
        with ExitStack() as layer:
            attention(3, layer, Mask(core.raw3, NEG, False))
        quantised_linear(core)


def packs(I):
    import numpy as np
    f = lambda a: np.asarray(a, np.float32)
    row = lambda v, n=1: np.tile(np.asarray(v).reshape(1, -1), (P, n))
    col = lambda v: np.asarray(v).reshape(-1, P).T
    z = np.zeros(P, np.float32)
    ctxT = np.asarray(I["ctx_1024"]).transpose(2, 0, 1)
    pidx = np.arange(P)
    neg3, rest = np.zeros(3, np.float32), np.float32(NEG)
    for i in range(3):
        neg3[i] = (np.array([rest]).view(np.uint32) & np.uint32(0xFFFF0000)).view(np.float32)[0]
        rest = np.float32(rest - neg3[i])
    out = {}
    out["ctx"] = [("ident", np.eye(P, dtype=np.float32)),
                  ("ctxT2", np.repeat(ctxT[:, :, None, :], 2, 2).reshape(P, -1)),
                  ("bmask", (pidx[:, None] // HD == np.arange(H)[None]).astype(np.float32))]
    n = "L0_xattn_"
    out["mha0"] = [("wq", I[n + "Wq"]), ("wk", I[n + "Wk"]), ("wv", I[n + "Wv"]), ("wo", I[n + "Wo"]),
                   ("bq", col(z)), ("bk", col(z)), ("bv", row(z)), ("bo", row(I[n + "bo"], 2)), ("neg3", neg3[:, None])]
    n = "L0_ffn_"
    A = lambda k: np.asarray(I[n + k])
    out["rot"] = [("gens", A("gens").transpose(1, 0, 2).reshape(P, -1)), ("gensT", A("gens").transpose(2, 0, 1).reshape(P, -1)),
                  ("ew2T", A("ew2").reshape(-1, P).T), ("eb2T", A("eb2").T)]
    out["ffn0"] = [("ew1", A("ew1").transpose(1, 0, 2).reshape(P, -1)), ("aw1", A("aw1")),
                   ("aw2", A("aw2").reshape(4, P, P).transpose(1, 0, 2).reshape(P, -1)),
                   ("eb1", col(A("eb1"))), ("ab1", col(A("ab1"))), ("gate_w", A("gate_w")), ("gate_b", row(A("gate_b"))),
                   ("prio", row(NE - np.arange(NE, dtype=np.float32))), ("ln_g", col(A("ln_g"))), ("ln_b", col(A("ln_b"))),
                   ("ab2", row(A("ab2"))), ("g1", row(A("gc_w")[:P])), ("g2", row(A("gc_w")[P:])), ("gc_b", row(A("gc_b")))]
    n = "L1_xattn_"
    out["top"] = [(k, np.asarray(I[n + "W" + k[1]]).T) for k in ("wq", "wk", "wv", "wo")] + [
        (k, col(I[n + k])) for k in ("bq", "bk", "bv")] + [("bo", row(I[n + "bo"], 2))]
    n = "L1_ffn_"
    A = lambda k: np.asarray(I[n + k])
    out["route"] = [("Wg", A("Wg")), ("b1", col(A("b1"))), ("prio", row(N1 - np.arange(N1, dtype=np.float32))),
                    ("same", (pidx[:, None] % N1 == pidx[None] % N1).astype(np.float32)),
                    ("below", (pidx[:, None] < pidx[None]).astype(np.float32)),
                    ("base", row(CAP * np.arange(N1, dtype=np.float32))),
                    ("pow2", row(2.0 ** -np.arange(BITS + 1, dtype=np.float32)))]
    n = "L2_xattn_"
    out["mha2"] = [(k, np.asarray(I[n + k]).T) for k in ("wq", "wk", "wv", "wo")] + [
        ("bq", col(I[n + "bq"])), ("bk", col(I[n + "bk"])), ("bv", row(I[n + "bv"])), ("bo", row(I[n + "bo"], 2))]
    n = "L3_xattn_"
    out["mha3"] = [(k.lower(), np.asarray(I[n + k]).transpose(1, 0, 2).reshape(P, P)) for k in ("Wq", "Wk", "Wv")] + [
        ("wo", I[n + "Wo"]), ("bq", col(I[n + "bq"])), ("bk", col(I[n + "bk"])), ("bv", row(I[n + "bv"])), ("bo", row(I[n + "bo"], 2))]
    trees = lambda key: [np.asarray(I[f"L2_ffn_{p}_{key}"]) for p in "qkv"]
    pad = lambda a, rows: np.concatenate([a, np.zeros((rows - len(a),) + a.shape[1:], a.dtype)])
    chosen = np.arange(NCH * P)[None] // LW == np.arange(NLEAF)[:, None]
    mixes = []
    for b1, b2 in zip(trees("b1"), trees("b2")):
        own = np.where(chosen, b1.reshape(1, -1), np.float32(0))
        first = np.concatenate([np.where(chosen, np.float32(BIG), np.float32(0)), np.zeros((NLEAF, P), np.float32)], 1)
        mixes.append(np.concatenate([first] + 3 * [np.concatenate([own, b2], 1)]))
    copy = pidx % SELP // NLEAF
    part = np.stack([copy <= 1, copy == 2, copy == 3, copy == 0], 1).astype(np.float32)
    out["tree_full"] = [
                   ("w1", np.concatenate([a.transpose(1, 0, 2).reshape(P, -1) for a in trees("w1")], 1)),
                   ("w2", np.concatenate([a.reshape(NCH, P, P).transpose(1, 0, 2).reshape(P, -1) for a in trees("w2")], 1)),
                   ("mixqk", np.concatenate(mixes[0:2])), ("mixv", mixes[2])]
    out["tree"] = [("part", part),
                   ("nodes", np.concatenate([pad(a, NLEAF).T for a in trees("node_w")], 1)),
                   ("node_b", row(np.concatenate([pad(a, NLEAF) for a in trees("node_b")])))]
    out["q8"] = [("wscale", row(I["L3_ffn_weight_scale"])), ("bias", row(I["L3_ffn_bias"]))]
    return out


def pack_layout(pack):
    lay, at = {}, 0
    for name, a in pack:
        lay[name] = (at, at + a.shape[1], a.shape[0])
        at += a.shape[1]
    return lay


def kernel(**inputs):
    import numpy as np
    import concourse.bacc as bacc
    from concourse.bass_utils import run_bass_kernel_spmd

    I = {name: np.asarray(a) for name, a in inputs.items()}
    parts = packs(I)
    layouts = {name: pack_layout(pack) for name, pack in parts.items()}
    arrays = {name: np.concatenate([np.concatenate([a, np.zeros((P - a.shape[0], a.shape[1]), a.dtype)]) for _, a in pack], 1)
              for name, pack in parts.items()}
    arrays["x"] = I["x"].reshape(B * S, P)
    arrays["itok"] = I["itok_BxS2_0_99"].reshape(1, B * SK)
    arrays["mask2"] = I["mask_1x1xSxS2_if1"].reshape(S, SK)
    arrays["mask3"] = I["mask_Bx1xSxS2_ff1"].reshape(B * S, SK)
    arrays["W8"] = np.ascontiguousarray(I["L3_ffn_weight_int8"].T).view(np.int32)
    for key in ("W1", "W2", "b2"):
        arrays["L1_" + key] = I["L1_ffn_" + key]
    arrays = {name: np.ascontiguousarray(a) for name, a in arrays.items()}

    nc = bacc.Bacc("TRN2", target_bir_lowering=False, num_devices=1)
    A = {name: nc.dram_tensor(f"in_{name}_dram", a.shape, mybir.dt.from_np(a.dtype), kind="ExternalInput").ap()
         for name, a in arrays.items()}
    A["out"] = nc.dram_tensor("out_0_dram", [B * S, P], F32, kind="ExternalOutput").ap()
    four_layers(nc, A, layouts)
    r = run_bass_kernel_spmd(nc, [{f"in_{name}_dram": a for name, a in arrays.items()}], core_ids=[0])
    return r.results[0]["out_0_dram"].reshape(B, S, P)
```

```python
from contextlib import ExitStack

import concourse.bass as bass
from concourse import mybir

F32 = mybir.dt.float32
F32R = mybir.dt.float32r
BF16 = mybir.dt.bfloat16
I32 = mybir.dt.int32
I8 = mybir.dt.int8
ALU = mybir.AluOpType
ACT = mybir.ActivationFunctionType
AX = mybir.AxisListType

P = 128
B, S, SK = 16, 256, 64
T = B * S // P
TB = S // P
H, HD = 16, 8
CH = H * SK // P
VW = 2 * HD + 2
EPS = 1e-5
NEG = -1e9


def need(eng, sem, value):
    if not isinstance(value, int) or value > 0:
        eng.wait_ge(sem, value)


def need_apart(eng, sem, value, tick):
    if not isinstance(value, int) or value > 0:
        eng.wait_ge(sem, value)
        eng.sem_inc(tick, 1)


class Chain:

    def __init__(self, eng, sem):
        self.eng, self.sem, self.n = eng, sem, 0

    def __call__(self, ins, base=0):
        self.n += 1
        ins.then_inc(self.sem, 1)
        self.eng.wait_ge(self.sem, base + self.n)


def cols(pack, layout, name):
    lo, hi, rows = layout[name]
    return pack[0:rows, lo:hi]


class Core:

    def __init__(self, nc, ctx, A, layouts):
        self.nc, self.ctx, self.A, self.lay = nc, ctx, A, layouts
        self.X = self.sb("X", [P, T, P])
        self.MV = self.sb("MV", [P, T, 2])
        self.RS = self.sb("RS", [P, T])
        self.pack = {}

    def sb(self, name, shape, dt=F32):
        return self.ctx.enter_context(self.nc.sbuf_tensor(name, shape, dt))

    def gpsimd_dma_sem(self, name):
        return self.ctx.enter_context(self.nc.semaphore(name))

    def w(self, pack, name):
        lo, hi, rows = self.lay[pack][name]
        return self.pack[pack][0:rows, lo:hi]


class Stage:

    def __init__(self, core, name):
        self.core, self.name, self.nc = core, name, core.nc
        self.stack = ExitStack()
        self.used = []

    def __enter__(self):
        self.stack.__enter__()
        return self

    def __exit__(self, *a):
        return self.stack.__exit__(*a)

    def sb(self, name, shape, dt=F32):
        return self.stack.enter_context(self.nc.sbuf_tensor(f"{self.name}_{name}", shape, dt))

    def ps(self, name, shape, dt=F32):
        return self.stack.enter_context(self.nc.psum_tensor(f"{self.name}_{name}", shape, dt))

    def sem(self, name):
        sem = self.stack.enter_context(self.nc.semaphore(f"{self.name}_{name}"))
        self.used.append(sem.num)
        return sem

    def block(self):
        self.stack.callback(self.clear)
        return self.stack.enter_context(self.nc.Block())

    def clear(self):
        used = sorted(self.used)
        while used:
            n = 1
            while n < len(used) and used[n] == used[0] + n:
                n += 1
            self.nc.gpsimd.sem_clear(range(used[0], used[0] + n))
            used = used[n:]


def token_scales(core, st, var, out, tag):
    ve = st.sb(f"ve{tag}", [P, T])
    sd = st.sb(f"sd{tag}", [P, T])
    nt = st.sb(f"nt{tag}", [P, T])
    s_ve, s_sd, s_own = st.sem(f"ve{tag}"), st.sem(f"sd{tag}"), st.sem(f"rs{tag}")

    def on_scalar(act):
        act.wait_ge(s_ve, 1)
        act.activation(sd[:], ve[:], ACT.Sqrt).then_inc(s_sd, 1)

    def on_vector(dve):
        dve.tensor_scalar(ve[:], var, EPS, None, ALU.add).then_inc(s_ve, 1)
        dve.wait_ge(s_sd, 1)
        link = Chain(dve, s_own)
        link(dve.reciprocal(out, sd[:]))
        link(dve.tensor_tensor(nt[:], ve[:], out, ALU.mult))
        link(dve.tensor_tensor(nt[:], nt[:], out, ALU.mult))
        link(dve.tensor_scalar(nt[:], nt[:], -0.5, 1.5, ALU.mult, ALU.add))
        link(dve.tensor_tensor(out, out, nt[:], ALU.mult))

    return on_scalar, on_vector


class Slot:

    def __init__(self, i, k):
        self.i, self.k = i, k

    def t(self, d):
        return 4 * self.i + self.k + d

    def has(self, d):
        return not isinstance(self.i, int) or 0 <= self.t(d) < T

    def b(self, d):
        return 2 * self.i + (self.k + d) // 2

    def u(self, d):
        return (self.k + d) // 2 % 2

    def v(self, d):
        return (self.k + d) % 2

    def next_x(self):
        return self.k % 2 == 1 and self.has(3)

    def next_q(self):
        return self.k % 2 == 0 and self.has(2)


def tile_slots(eng, slot, lag):
    for k in range(4):
        slot(Slot(0, k))
    with eng.Fori(1, T // 4 - 1) as i:
        for k in range(4):
            slot(Slot(i, k))
    for t in range(T - 4, T + lag):
        slot(Slot(t // 4, t % 4))


def prep_parts(core, L, key_mask, st, pk, pv):
    KT, VB = core.KT[L], core.VB[L]
    w = lambda n: core.w(f"mha{L}", n)
    s_k, s_v, s_kt, s_z = (st.sem(n) for n in ("prep_k", "prep_v", "prep_kt", "prep_z"))
    c2 = core.w("ctx", "ctxT2").rearrange("p (b r k) -> p b r k", r=2, k=SK)

    def on_tensor(pe):
        for n in range(2):
            pe.matmul(pk[n], w("wk"), c2[:, 8 * n:8 * n + 8, 0, :], start=True, stop=True).then_inc(s_k, 1)
        for b in range(B):
            pe.matmul(pv[b // 4][:, P * (b % 4):P * (b % 4) + P], c2[:, b, :, :], w("wv"), start=True, stop=True).then_inc(s_v, 1)

    def on_scalar(act):
        for n in range(2):
            act.wait_ge(s_k, n + 1)
            act.activation(KT[:, 512 * n:512 * n + 512], pk[n], ACT.Identity, bias=w("bk")).then_inc(s_kt, 1)

    def on_vector(dve):
        dve.memset(VB[:], 0.0).then_inc(s_z, 1)
        dve.wait_ge(s_z, 1)
        bv = w("bv").rearrange("p (c h d) -> p c h d", h=2, d=HD)
        for h in range(2):
            q = slice(64 * h, 64 * h + 64)
            dve.memset(VB[q, :, :, 2 * HD + h:2 * HD + h + 1], 1.0)
            for n in range(4):
                dve.wait_ge(s_v, 4 * n + 4)
                src = pv[n][q, :].rearrange("p (b c h d) -> p b c h d", b=4, h=2, d=HD)[:, :, :, h, :]
                dst = VB[q, 4 * n:4 * n + 4, :, h * HD:h * HD + HD]
                for bb in range(4):
                    dve.tensor_tensor(dst[:, bb], src[:, bb], bv[q, :, h, :], ALU.add)
        if key_mask:
            dve.wait_ge(s_kt, 2)
            dve.tensor_tensor(KT[:], KT[:], core.keep[:], ALU.mult)

    return on_tensor, on_scalar, on_vector


def prep_mha(core, L, key_mask, statistics=False):
    with Stage(core, f"prep{L}") as st:
        pk = [st.ps(f"pk{n}", [P, 512])[:] for n in range(2)]
        pv = [st.ps(f"pv{n}", [P, 512])[:] for n in range(4)]
        on_tensor, on_scalar, on_vector = prep_parts(core, L, key_mask, st, pk, pv)
        if statistics:
            bn, s_bn = st.sb("bn", [P, T, 6]), st.sem("bn")
        blk = st.block()

        if statistics:
            @blk.sync
            def _(sp):
                sp.wait_ge(core.x_loaded[NG - 1], 16)
                load_later(core, sp)

        @blk.tensor
        def _(pe):
            on_tensor(pe)

        @blk.scalar
        def _(act):
            on_scalar(act)

        @blk.vector
        def _(dve):
            on_vector(dve)
            if statistics:
                first_statistics(core, dve, bn, s_bn, range(NG // 2, NG))


def first_statistics(core, dve, bn, s_bn, groups):
    for n, q in enumerate(groups):
        dve.wait_ge(core.x_loaded[q], 16)
        for t in range(GT * q, GT * q + GT):
            ins = dve.bn_stats(bn[:, t, :], core.X[:, t, :])
        ins.then_inc(s_bn, 1)
        dve.wait_ge(s_bn, n + 1)
        for t in range(GT * q, GT * q + GT):
            dve.bn_aggr(core.MV[:, t, :], bn[:, t, :])


def prep_key_mask(core, stack):
    core.keep = stack.enter_context(core.nc.sbuf_tensor("keep", [P, B * SK], F32))
    core.nbias3 = stack.enter_context(core.nc.sbuf_tensor("nbias3", [3, B, SK], BF16))
    core.ones3 = stack.enter_context(core.nc.sbuf_tensor("ones3", [3, P], BF16))
    with Stage(core, "kmask") as st:
        blk = st.block()

        @blk.vector
        def _(dve):
            dve.memset(core.ones3[:], 1.0)
            dve.tensor_scalar(core.keep[:], core.itok[:], 0.0, None, ALU.not_equal)
            dve.tensor_scalar(core.nbias3[:].rearrange("p b k -> p (b k)"), core.itok[0:3, :], 0.0, core.w("mha0", "neg3"),
                              ALU.is_equal, ALU.mult)


class Mask:

    def __init__(self, raw, fill, shared):
        self.raw, self.fill_value, self.shared = raw, fill / HD ** -0.5, shared


def mask_buffers(core, L, mask, stack):
    n = mask.raw.shape[1]
    sb = lambda name, shape, dt=F32: stack.enter_context(core.nc.sbuf_tensor(f"{name}{L}", shape, dt))
    mask.keep = mask.raw if mask.raw.dtype == F32 else sb("keep", [P, n, SK])
    mask.fill, mask.any_word = sb("fill", [P, n, SK]), sb("any_word", [1, 1], I32)


def mask_parts(core, L, mask, st, pm):
    lo, lor = st.sb(f"lo{L}", [P, P]), st.sb(f"lor{L}", [1, 1])
    s_m, s_t, s_own = st.sem(f"mask_m{L}"), st.sem(f"mask_t{L}"), st.sem(f"mask_own{L}")

    def on_tensor(pe):
        pe.wait_ge(s_m, 1)
        pe.transpose(pm, lo[:], core.w("ctx", "ident")).then_inc(s_t, 1)

    def on_vector(dve):
        link = Chain(dve, s_own)
        link(dve.tensor_scalar(mask.fill[:], mask.raw[:], 0.0, mask.fill_value, ALU.is_equal, ALU.mult))
        dve.memset(lo[:], 1.0)
        link(dve.tensor_scalar(mask.keep[:], mask.raw[:], 0.0, None, ALU.not_equal))
        dve.tensor_reduce(lo[:, 0:1], mask.keep[:], AX.XY, ALU.min).then_inc(s_m, 1)
        dve.wait_ge(s_t, 1)
        link(dve.tensor_reduce(lor[:], pm[0:1, :], AX.X, ALU.min))
        dve.tensor_scalar(mask.any_word[:], lor[:], -1.0, 1.0, ALU.mult, ALU.add)

    return on_tensor, on_vector


def mha(core, L, mask=None, key_mask=False):
    nc = core.nc
    X, MV, RS = core.X, core.MV, core.RS
    KT, VB = core.KT[L], core.VB[L]
    ident = core.w("ctx", "ident")
    bmask = core.w("ctx", "bmask")
    w = lambda n: core.w(f"mha{L}", n)
    with Stage(core, f"mha{L}") as st:
        xh = [st.sb(f"xh{u}", [P, TB, P]) for u in range(2)]
        xT = [st.sb(f"xT{u}", [P, S]) for u in range(2)]
        qT = [st.sb(f"qT{u}", [P, S]) for u in range(2)]
        kbd = [st.sb(f"kbd{u}", [P, H, SK]) for u in range(2)]
        Z = [st.sb(f"Z{u}", [P, H, SK]) for u in range(2)]
        PR = [st.sb(f"PR{u}", [P, H * SK]) for u in range(2)]
        PT = [st.sb(f"PT{u}", [P, CH * P]) for u in range(2)]
        at = [st.sb(f"at{u}", [P, P]) for u in range(2)]
        aT = [st.sb(f"aT{u}", [P, P]) for u in range(2)]
        nm = [st.sb(f"nm{u}", [P, H]) for u in range(2)]
        rc = [st.sb(f"rc{u}", [P, CH, 2]) for u in range(2)]
        bn = [st.sb(f"bn{u}", [P, 6]) for u in range(2)]
        mv = [st.sb(f"mv{u}", [P, 2]) for u in range(2)]
        pS = st.ps("pS", [P, 2, 512])
        pT = st.ps("pT", [P, CH * P])
        pQ = st.ps("pQ", [P, 512])
        pO = st.ps("pO", [P, 512])
        pAb = st.ps("pA", [P, 512])
        pYb = st.ps("pY", [P, 512])
        pOv = pO[:, 0:CH * VW].rearrange("p (c w) -> p c w", w=VW)
        pA, pY = pAb[:, 0:P], pYb[:, 0:P]
        names = "xh bo kbd xTp xT qp q S nm Z P PTp PT O rc at aTp aT Y X bn mv msk tick".split()
        s = {n: st.sem(n) for n in names}
        rs_act, rs_dve = token_scales(core, st, MV[:, :, 1], RS[:], "a")
        blk = st.block()

        if key_mask:
            @blk.sync
            def _(sp):
                need(sp, core.loaded, 16 * core.loads)

        @blk.tensor
        def _(pe):
            def x_transposes(b, u):
                need(pe, s["xh"], 2 * b + 2)
                need(pe, s["q"], b)
                for j in range(TB):
                    ins = pe.transpose(pQ[:, P * j:P * j + P], xh[u][:, j, :], ident)
                ins.then_inc(s["xTp"], 1)

            def queries(b, u):
                need(pe, s["xT"], b + 1)
                pe.matmul(pQ[:, 0:S], w("wq"), xT[u][:], start=True, stop=True).then_inc(s["qp"], 1)

            def scores(t, b, u, v, n):
                need(pe, s["q"], b + 1)
                need(pe, s["kbd"], b + 1)
                need(pe, s["Z"], 2 * t - 1 + n)
                ins = pe.matmul(pS[:, n, :], qT[u][:, P * v:P * v + P],
                                kbd[u][:, 8 * n:8 * n + 8, :], start=True, stop=not key_mask)
                if key_mask:
                    nb = core.nbias3[:, bass.ds(b, 1), :].to_broadcast([3, 8, SK])
                    ins = pe.matmul(pS[:, n, :], core.ones3[:], nb, start=False, stop=True)
                ins.then_inc(s["S"], 1)

            def slot(a):
                if a.has(1):
                    scores(a.t(1), a.b(1), a.u(1), a.v(1), 0)
                if a.has(-1):
                    r, v = a.t(-1), a.v(-1)
                    need(pe, s["P"], r + 1)
                    need(pe, s["PT"], r)
                    for c in range(CH):
                        ins = pe.transpose(pT[:, P * c:P * c + P], PR[v][:, P * c:P * c + P], ident)
                    ins.then_inc(s["PTp"], 1)
                if a.next_x():
                    x_transposes(a.b(3), a.u(3))
                if a.has(1):
                    scores(a.t(1), a.b(1), a.u(1), a.v(1), 1)
                if a.has(-3):
                    r, v = a.t(-3), a.v(-3)
                    need(pe, s["at"], r + 1)
                    need(pe, s["aT"], r)
                    pe.transpose(pA, at[v][:], ident).then_inc(s["aTp"], 1)
                if a.next_q():
                    queries(a.b(2), a.u(2))
                if a.has(-2):
                    r, v = a.t(-2), a.v(-2)
                    need(pe, s["PT"], r + 1)
                    need(pe, s["at"], r)
                    for c in range(CH):
                        ins = pe.matmul(pOv[:, c, :], PT[v][:, P * c:P * c + P], VB[:, a.b(-2), c, :], start=True, stop=True)
                    ins.then_inc(s["O"], 1)
                if a.has(-3):
                    r, v = a.t(-3), a.v(-3)
                    need(pe, s["aT"], r + 1)
                    need(pe, s["X"], r)
                    pe.matmul(pY, aT[v][:], w("wo"), start=True, stop=True).then_inc(s["Y"], 1)

            x_transposes(0, 0)
            queries(0, 0)
            scores(0, 0, 0, 0, 0)
            scores(0, 0, 0, 0, 1)
            x_transposes(1, 1)
            tile_slots(pe, slot, 4)

        @blk.scalar
        def _(act):
            def x_evac(b, u):
                need(act, s["xTp"], b + 1)
                need(act, s["qp"], b - 1)
                act.activation(xT[u][:], pQ[:, 0:S], ACT.Copy).then_inc(s["xT"], 1)

            def q_evac(b, u):
                need(act, s["qp"], b + 1)
                need(act, s["S"], 4 * b - 4)
                act.activation(qT[u][:], pQ[:, 0:S], ACT.Identity, bias=w("bq")).then_inc(s["q"], 1)

            def slot(a):
                if a.has(0):
                    r, v = a.t(0), a.v(0)
                    need(act, s["Z"], 2 * r + 2)
                    need(act, s["PTp"], r - 1)
                    act.activation(PR[v][:], Z[v][:].rearrange("p h k -> p (h k)"), ACT.Exp, scale=HD ** -0.5).then_inc(s["P"], 1)
                if a.has(-1):
                    r, v = a.t(-1), a.v(-1)
                    need(act, s["PTp"], r + 1)
                    need(act, s["O"], r - 1)
                    act.activation(PT[v][:], pT[:], ACT.Copy).then_inc(s["PT"], 1)
                if a.next_x():
                    x_evac(a.b(3), a.u(3))
                if a.has(-3):
                    r, v = a.t(-3), a.v(-3)
                    need(act, s["aTp"], r + 1)
                    need(act, s["Y"], r)
                    act.activation(aT[v][:], pA, ACT.Copy).then_inc(s["aT"], 1)
                if a.next_q():
                    q_evac(a.b(2), a.u(2))

            rs_act(act)
            x_evac(0, 0)
            q_evac(0, 0)
            x_evac(1, 1)
            tile_slots(act, slot, 4)

        @blk.gpsimd
        def _(pool):
            def prepare(b, u):
                need(pool, s["S"], 4 * b - 4)
                kb = KT[:].rearrange("p (b k) -> p b k", k=SK)[:, bass.ds(b, 1), :].to_broadcast([P, H, SK])
                pool.tensor_tensor(kbd[u][:], kb, bmask.unsqueeze(2).to_broadcast([P, H, SK]), ALU.mult).then_inc(s["kbd"], 1)
                need(pool, s["xh"], 2 * b + 2)
                pool.tensor_tensor(X[:, bass.ds(2 * b, TB), :], X[:, bass.ds(2 * b, TB), :],
                                   w("bo").rearrange("p (t d) -> p t d", t=TB), ALU.add).then_inc(s["bo"], 1)

            prepare(0, 0)
            prepare(1, 1)
            with pool.Fori(1, B // 2) as i:
                prepare(2 * i, 0)
                prepare(2 * i + 1, 1)

        @blk.vector
        def _(dve):
            def pipeline(masked):
                def normalise(b, u):
                    need(dve, s["xTp"], b - 1)
                    for j in range(TB):
                        dve.tensor_scalar(xh[u][:, j, :], X[:, 2 * b + j, :], MV[:, 2 * b + j, 0:1], RS[:, bass.ds(2 * b + j, 1)],
                                          ALU.subtract, ALU.mult).then_inc(s["xh"], 1)

                def softmax_shift(t, v, halves=(0, 1)):
                    HH = H // 2
                    for n in halves:
                        sc = pS[:, n, :].rearrange("p (h k) -> p h k", k=SK)
                        mx = nm[v][:, HH * n:HH * n + HH]
                        need(dve, s["S"], 2 * t + n + 1)
                        if masked:
                            mi = v if mask.shared else t
                            kp = mask.keep[:, bass.ds(mi, 1), :].to_broadcast([P, HH, SK])
                            ng = mask.fill[:, bass.ds(mi, 1), :].to_broadcast([P, HH, SK])
                            dve.tensor_tensor(sc, sc, kp, ALU.mult).then_inc(s["msk"], 1)
                            need(dve, s["msk"], 4 * t + 2 * n + 1)
                            dve.tensor_tensor(sc, sc, ng, ALU.add).then_inc(s["msk"], 1)
                            need(dve, s["msk"], 4 * t + 2 * n + 2)
                        dve.tensor_reduce(mx, sc, AX.X, ALU.max, negate=True).then_inc(s["nm"], 1)
                        need(dve, s["P"], t - 1)
                        need(dve, s["nm"], 2 * t + n + 1)
                        dve.tensor_tensor(Z[v][:, HH * n:HH * n + HH, :], sc, mx.unsqueeze(2).to_broadcast([P, HH, SK]),
                                          ALU.add).then_inc(s["Z"], 1)

                def slot(a):
                    if a.has(-3):
                        r, v = a.t(-3), a.v(-3)
                        need(dve, s["O"], r + 1)
                        dve.reciprocal(rc[v][:], pOv[:, :, 2 * HD:VW]).then_inc(s["rc"], 1)
                        need(dve, s["aTp"], r)
                        need(dve, s["rc"], r + 1)
                        dve.tensor_tensor(at[v][:].rearrange("p (c h d) -> p c h d", h=2, d=HD),
                                          pOv[:, :, 0:2 * HD].rearrange("p c (h d) -> p c h d", d=HD),
                                          rc[v][:].unsqueeze(3).to_broadcast([P, CH, 2, HD]), ALU.mult).then_inc(s["at"], 1)
                    if a.next_x():
                        normalise(a.b(3), a.u(3))
                    if a.has(1):
                        softmax_shift(a.t(1), a.v(1), (0,))
                    if a.has(-4):
                        r, v = a.t(-4), a.v(-4)
                        need(dve, s["Y"], r + 1)
                        need(dve, s["bo"], a.b(-4) + 1)
                        dve.tensor_tensor(X[:, r, :], pY, X[:, r, :], ALU.add).then_inc(s["X"], 1)
                        need_apart(dve, s["X"], r + 1, s["tick"])
                        dve.bn_stats(bn[v][:], X[:, r, :]).then_inc(s["bn"], 1)
                    if a.has(1):
                        softmax_shift(a.t(1), a.v(1), (1,))
                    if a.has(-4):
                        need_apart(dve, s["bn"], r + 1, s["tick"])
                        dve.bn_aggr(mv[v][:], bn[v][:]).then_inc(s["mv"], 1)
                        need(dve, s["mv"], r + 1)
                        dve.tensor_scalar(MV[:, r, :], mv[v][:], 1.0, None, ALU.mult)

                normalise(0, 0)
                normalise(1, 1)
                softmax_shift(0, 0)
                tile_slots(dve, slot, 4)

            rs_dve(dve)
            if mask is None:
                pipeline(False)
            else:
                flag = dve.alloc_register(f"masked{L}")
                dve.reg_load(flag, mask.any_word[0:1, 0:1])
                with dve.If_eq(flag, 0):
                    pipeline(False)
                with dve.If_ne(flag, 0):
                    pipeline(True)


def batch_slots(eng, fn, lag):
    fn(0, 0)
    fn(1, 1)
    fn(2, 0)
    fn(3, 1)
    with eng.Fori(2, B // 2 - 1) as i:
        fn(2 * i, 0)
        fn(2 * i + 1, 1)
    for b in range(B - 2, B + lag):
        fn(b, b % 2)


def live(b):
    return not isinstance(b, int) or 0 <= b < B


MARK = -3e38


def prep_top(core):
    w = lambda n: core.w("top", n)
    with Stage(core, "ptop") as st:
        VT = st.sb("VT", [P, B, 2, SK])
        pk, pv, pw = st.ps("pk", [P, 2, 512]), st.ps("pv", [P, 2, 512]), st.ps("pw", [P, 4, 4, P])
        s_k, s_v, s_w = st.sem("k"), st.sem("v"), st.sem("w")
        blk = st.block()
        c2 = core.w("ctx", "ctxT2").rearrange("p (b r k) -> p b r k", r=2, k=SK)

        @blk.tensor
        def _(pe):
            for n in range(2):
                pe.matmul(pk[:, n, :], w("wk"), c2[:, 8 * n:8 * n + 8, 0, :], start=True, stop=True).then_inc(s_k, 1)
                pe.matmul(pv[:, n, :], w("wv"), c2[:, 8 * n:8 * n + 8, 0, :], start=True, stop=True).then_inc(s_k, 1)
            pe.wait_ge(s_v, 2)
            for b in range(B):
                ins = pe.matmul(pw[:, b // 4, b % 4, :], VT[:, b, :, :], w("wo"), start=True, stop=True)
                if b % 4 == 3:
                    ins.then_inc(s_w, 1)

        @blk.scalar
        def _(act):
            for n in range(2):
                act.wait_ge(s_k, 2 * n + 1)
                act.activation(core.KT[1][:, 512 * n:512 * n + 512], pk[:, n, :], ACT.Identity, bias=w("bk"))
                act.wait_ge(s_k, 2 * n + 2)
                src = pv[:, n, :].rearrange("p (b k) -> p b k", k=SK)
                for r in range(2):
                    ins = act.activation(VT[:, 8 * n:8 * n + 8, r, :], src, ACT.Identity, bias=w("bv"))
                ins.then_inc(s_v, 1)
            for n in range(4):
                act.wait_ge(s_w, n + 1)
                act.activation(core.VWo[:, 4 * n:4 * n + 4, :], pw[:, n, :, :], ACT.Copy)


def attention_top(core):
    X, MV, RS = core.X, core.MV, core.RS
    ident = core.w("ctx", "ident")
    w = lambda n: core.w("top", n)
    TOP, R8 = 32, 8
    with Stage(core, "top") as st:
        two = lambda name, shape: [st.sb(f"{name}{u}", shape) for u in range(2)]
        xh, xT, qT = two("xh", [P, TB, P]), two("xT", [P, S]), two("qT", [P, S])
        sc, wk, pr = (two(n, [P, TB, SK]) for n in ("sc", "wk", "pr"))
        pk = two("pk", [P, TB, P])
        PT = two("PT", [P, S])
        m8 = two("m8", [P, TB, TOP // R8, R8])
        nm, sm, rc = two("nm", [P, TB]), two("sm", [P, TB]), two("rc", [P, TB])
        bn, mv = st.sb("bn", [P, TB, 6]), st.sb("mv", [P, TB, 2])
        pQ = st.ps("pQ", [P, 512])
        pS = [st.ps(f"pS{u}", [P, 512]) for u in range(2)]
        pT = st.ps("pT", [P, 512])
        pY = st.ps("pY", [P, 512])
        names = "xh bo xTp xT qp q S sc top nm P pk PTp PT Y X bn own zero tick".split()
        s = {n: st.sem(n) for n in names}
        rs_act, rs_dve = token_scales(core, st, MV[:, :, 1], RS[:], "a")
        blk = st.block()

        @blk.tensor
        def _(pe):
            def x_transposes(b, u):
                need(pe, s["xh"], b + 1)
                need(pe, s["q"], b)
                for j in range(TB):
                    ins = pe.transpose(pQ[:, P * j:P * j + P], xh[u][:, j, :], ident)
                ins.then_inc(s["xTp"], 1)

            def queries(b, u):
                need(pe, s["xT"], b + 1)
                pe.matmul(pQ[:, 0:S], w("wq"), xT[u][:], start=True, stop=True).then_inc(s["qp"], 1)

            def scores(b, u):
                need(pe, s["q"], b + 1)
                need(pe, s["sc"], b - 1)
                for j in range(TB):
                    ins = pe.matmul(pS[u][:, SK * j:SK * j + SK], qT[u][:, P * j:P * j + P],
                                    core.KT[1][:, bass.ds(SK * b, SK)], start=True, stop=True)
                ins.then_inc(s["S"], 1)

            def slot(b, u):
                if live(b - 1):
                    need(pe, s["pk"], b)
                    need(pe, s["PT"], b - 1)
                    for j in range(TB):
                        ins = pe.transpose(pT[:, P * j:P * j + P], pk[1 - u][:, j, :], ident)
                    ins.then_inc(s["PTp"], 1)
                if live(b - 1):
                    need(pe, s["PT"], b)
                    need(pe, s["X"], b - 1)
                    for j in range(TB):
                        ins = pe.matmul(pY[:, P * j:P * j + P], PT[1 - u][:, P * j:P * j + P], core.VWo[:, b - 1, :], start=True, stop=True)
                    ins.then_inc(s["Y"], 1)
                if live(b + 2):
                    x_transposes(b + 2, u)
                    queries(b + 2, u)
                    scores(b + 2, u)

            for b in range(2):
                x_transposes(b, b)
                queries(b, b)
                scores(b, b)
            batch_slots(pe, slot, 2)

        @blk.scalar
        def _(act):
            def x_evac(b, u):
                need(act, s["xTp"], b + 1)
                need(act, s["qp"], b - 1)
                act.activation(xT[u][:], pQ[:, 0:S], ACT.Copy).then_inc(s["xT"], 1)

            def q_evac(b, u):
                need(act, s["qp"], b + 1)
                need(act, s["S"], b - 1)
                act.activation(qT[u][:], pQ[:, 0:S], ACT.Identity, bias=w("bq")).then_inc(s["q"], 1)

            def slot(b, u):
                if live(b - 1):
                    need(act, s["PTp"], b)
                    need(act, s["Y"], b - 2)
                    act.activation(PT[1 - u][:], pT[:, 0:S], ACT.Copy).then_inc(s["PT"], 1)
                if live(b):
                    need(act, s["nm"], b + 1)
                    need(act, s["pk"], b - 1)
                    for j in range(TB):
                        ins = act.activation(pr[u][:, j, :], sc[u][:, j, :], ACT.Exp, bias=nm[u][:, j:j + 1])
                    ins.then_inc(s["P"], 1)
                if live(b + 2):
                    x_evac(b + 2, u)
                    q_evac(b + 2, u)

            rs_act(act)
            for b in range(2):
                x_evac(b, b)
                q_evac(b, b)
            batch_slots(act, slot, 2)

        @blk.gpsimd
        def _(pool):
            def slot(b):
                need(pool, s["xh"], b + 1)
                xs = X[:, bass.ds(TB * b, TB), :]
                pool.tensor_tensor(xs, xs, w("bo").rearrange("p (t d) -> p t d", t=TB), ALU.add).then_inc(s["bo"], 1)

            with pool.Fori(0, B) as b:
                slot(b)

        @blk.vector
        def _(dve):
            OWN = TB * 2 * (TOP // R8)

            def normalise(b, u, tiles=range(TB)):
                if 0 in tiles:
                    need(dve, s["xTp"], b - 1)
                for j in tiles:
                    t = TB * b + j
                    ins = dve.tensor_scalar(xh[u][:, j, :], X[:, t, :], MV[:, t, 0:1], RS[:, bass.ds(t, 1)], ALU.subtract, ALU.mult)
                if TB - 1 in tiles:
                    ins.then_inc(s["xh"], 1)

            def scaled(b, u):
                need(dve, s["S"], b + 1)
                need(dve, s["P"], b - 1)
                dve.tensor_scalar(sc[u][:], pS[u][:, 0:TB * SK].rearrange("p (t k) -> p t k", t=TB), float(P) ** -0.5, None,
                                  ALU.mult).then_inc(s["sc"], 1)

            def best8(b, u, r):
                if r == 0:
                    need_apart(dve, s["sc"], b + 1, s["tick"])
                else:
                    need_apart(dve, s["own"], OWN * b + 2 * TB * r, s["tick"])
                for j in range(TB):
                    dve.max(m8[u][:, j, r, :], (sc if r == 0 else wk)[u][:, j, :]).then_inc(s["own"], 1)

            def mark8(b, u, r):
                need_apart(dve, s["own"], OWN * b + 2 * TB * r + TB, s["tick"])
                if r == 0:
                    dve.tensor_scalar(nm[u][:], m8[u][:, :, 0, 0], -1.0, None, ALU.mult).then_inc(s["nm"], 1)
                for j in range(TB):
                    dve.match_replace(wk[u][:, j, :], m8[u][:, j, r, :], (sc if r == 0 else wk)[u][:, j, :], MARK).then_inc(s["own"], 1)

            def keep(b, u):
                need_apart(dve, s["own"], OWN * b + OWN, s["tick"])
                need(dve, s["P"], b + 1)
                need(dve, s["PTp"], b - 1)
                for j in range(TB):
                    ins = dve.scalar_tensor_tensor(pk[u][:, j, 0:SK], wk[u][:, j, :], MARK, pr[u][:, j, :], ALU.is_equal, ALU.mult,
                                                   accum_out=sm[u][:, j:j + 1])
                ins.then_inc(s["pk"], 1)
                need(dve, s["pk"], b + 1)
                dve.reciprocal(rc[u][:], sm[u][:]).then_inc(s["top"], 1)

            def final(b, u, step):
                if step == 0:
                    need(dve, s["Y"], b + 1)
                    need(dve, s["bo"], b + 1)
                    need(dve, s["top"], b + 1)
                    for j in range(TB):
                        t = TB * b + j
                        ins = dve.scalar_tensor_tensor(X[:, t, :], pY[:, P * j:P * j + P], rc[u][:, j:j + 1], X[:, t, :], ALU.mult, ALU.add)
                    ins.then_inc(s["X"], 1)
                if step == 1:
                    need_apart(dve, s["X"], b + 1, s["tick"])
                    for j in range(TB):
                        ins = dve.bn_stats(bn[:, j, :], X[:, TB * b + j, :])
                    ins.then_inc(s["bn"], 1)
                if step == 2:
                    need_apart(dve, s["bn"], 2 * b + 1, s["tick"])
                    for j in range(TB):
                        ins = dve.bn_aggr(mv[:, j, :], bn[:, j, :])
                    ins.then_inc(s["bn"], 1)
                if step == 3:
                    need(dve, s["bn"], 2 * b + 2)
                    dve.tensor_scalar(MV[:, bass.ds(TB * b, TB), :], mv[:], 1.0, None, ALU.mult)

            def slot(b, u):
                if live(b):
                    scaled(b, u)
                for r in range(TOP // R8):
                    if live(b - 2) and r < 2:
                        final(b - 2, u, 2 * r)
                    if live(b):
                        best8(b, u, r)
                    if live(b - 2) and r < 2:
                        final(b - 2, u, 2 * r + 1)
                    if live(b + 2) and r >= 2:
                        normalise(b + 2, u, [r - 2])
                    if live(b):
                        mark8(b, u, r)
                if live(b):
                    keep(b, u)

            for u in range(2):
                dve.memset(pk[u][:, :, SK:P], 0.0).then_inc(s["zero"], 1)
            rs_dve(dve)
            normalise(0, 0)
            normalise(1, 1)
            batch_slots(dve, slot, 2)


NROT, NE, EH = 4, 6, 256
TAYLOR = 8
SQUARINGS = 6


def fold_rotations(core):
    w = lambda n: core.w("rot", n)
    ident = core.w("ctx", "ident")
    N4 = NROT * P
    with Stage(core, "rot") as st:
        A1, A1T = st.sb("A1", [P, N4]), st.sb("A1T", [P, N4])
        E = [st.sb(f"E{u}", [P, N4]) for u in range(2)]
        ET = [st.sb(f"ET{u}", [P, N4]) for u in range(2)]
        tmp, R = st.sb("tmp", [P, N4]), st.sb("R", [P, P])
        MT, M34 = st.sb("MT", [P, P]), st.sb("M34", [P, P])
        pE, pF = ([st.ps(f"p{n}{h}", [P, 512]) for h in range(2)] for n in "EF")
        pW = st.ps("pW", [P, 3, 512])
        pB = st.ps("pB", [P, 512])
        s_pe, s_dve, s_own = ([st.sem(f"{n}{h}") for h in range(2)] for n in ("pe", "dve", "own"))
        s_r, s_rp, s_high = st.sem("r"), st.sem("rp"), st.sem("high")
        blk = st.block()
        g = lambda t, n: t[:, P * n:P * n + P]

        @blk.scalar
        def _(act):
            act.activation(core.up_h[:], w("up"), ACT.Copy).then_inc(s_high, 1)

        @blk.gpsimd
        def _(pool):
            pool.wait_ge(s_high, 1)
            pool.tensor_tensor(core.up_l[:], w("up"), core.up_h[:], ALU.subtract)

        W = 2 * P
        half = lambda t, h: t[:, W * h:W * h + W]
        U = (TAYLOR - 1) % 2
        V, VT = (U + SQUARINGS) % 2, SQUARINGS % 2

        @blk.tensor
        def _(pe):
            for step in range(TAYLOR - 1):
                for h in range(2):
                    pe.wait_ge(s_dve[h], step + 1)
                    for n in range(2):
                        ins = pe.matmul(g(pE[h], n), g(A1T, 2 * h + n), g(E[step % 2], 2 * h + n), start=True, stop=True)
                    ins.then_inc(s_pe[h], 1)
            for h in range(2):
                pe.wait_ge(s_dve[h], TAYLOR)
                for n in range(2):
                    ins = pe.transpose(g(pF[h], n), g(E[U], 2 * h + n), ident)
                ins.then_inc(s_pe[h], 1)
            for k in range(SQUARINGS):
                for h in range(2):
                    pe.wait_ge(s_dve[h], TAYLOR + 1 + k)
                    for n in range(2):
                        e, t = g(E[(U + k) % 2], 2 * h + n), g(ET[k % 2], 2 * h + n)
                        pe.matmul(g(pE[h], n), t, e, start=True, stop=True)
                        ins = pe.matmul(g(pF[h], n), e, t, start=True, stop=True)
                    ins.then_inc(s_pe[h], 1)
            for h in range(2):
                pe.wait_ge(s_dve[h], TAYLOR + 1 + SQUARINGS)
                if h == 0:
                    ins = pe.matmul(g(pE[0], 0), g(E[V], 1), g(ET[VT], 0), start=True, stop=True)
                else:
                    ins = pe.matmul(g(pE[1], 0), g(ET[VT], 2), g(E[V], 3), start=True, stop=True)
                ins.then_inc(s_pe[h], 1)
            pe.wait_ge(s_r, 1)
            pe.matmul(g(pF[0], 0), MT[:], M34[:], start=True, stop=True).then_inc(s_rp, 1)
            pe.wait_ge(s_r, 2)
            for c in range(2 * NE):
                pe.matmul(pW[:, c // 4, P * (c % 4):P * (c % 4) + P], w("ew2T")[:, P * c:P * c + P], R[:], start=True, stop=True)
            pe.matmul(pB[0:NE, 0:P], w("eb2T"), R[:], start=True, stop=True).then_inc(s_rp, 1)

        @blk.vector
        def _(dve):
            link = [Chain(dve, s_own[h]) for h in range(2)]
            for h in range(2):
                dve.tensor_scalar(half(A1T, h), half(w("gensT"), h), 2.0 ** -SQUARINGS, None, ALU.mult)
                link[h](dve.tensor_scalar(half(A1, h), half(w("gens"), h), 2.0 ** -SQUARINGS, None, ALU.mult))
                dve.tensor_scalar(half(E[0], h), half(A1, h), 1.0 / TAYLOR, None, ALU.mult).then_inc(s_dve[h], 1)
            for step in range(1, TAYLOR):
                for h in range(2):
                    dve.wait_ge(s_pe[h], step)
                    link[h](dve.tensor_tensor(half(tmp, h), pE[h][:, 0:W], half(A1, h), ALU.add))
                    dve.tensor_scalar(half(E[step % 2], h), half(tmp, h), 1.0 / (TAYLOR - step), None, ALU.mult).then_inc(s_dve[h], 1)
            for h in range(2):
                dve.wait_ge(s_pe[h], TAYLOR)
                dve.tensor_copy(half(ET[0], h), pF[h][:, 0:W]).then_inc(s_dve[h], 1)
            i2 = ident.unsqueeze(1).to_broadcast([P, 2, P])
            m2 = lambda t, h: half(t, h).rearrange("p (n d) -> p n d", n=2)
            for k in range(SQUARINGS):
                for h in range(2):
                    last = k == SQUARINGS - 1
                    dve.wait_ge(s_pe[h], TAYLOR + 1 + k)
                    dve.wait_ge(s_dve[h], TAYLOR + 1 + k)
                    link[h](dve.scalar_tensor_tensor(half(E[(U + k + 1) % 2], h), half(E[(U + k) % 2], h), 2.0, pE[h][:, 0:W], ALU.mult, ALU.add))
                    ins = dve.scalar_tensor_tensor(half(ET[(k + 1) % 2], h), half(ET[k % 2], h), 2.0, pF[h][:, 0:W], ALU.mult, ALU.add)
                    if last:
                        link[h](ins)
                        link[h](dve.tensor_tensor(m2(E[V], h), m2(E[V], h), i2, ALU.add))
                        ins = dve.tensor_tensor(m2(ET[VT], h), m2(ET[VT], h), i2, ALU.add)
                    ins.then_inc(s_dve[h], 1)
            dve.wait_ge(s_pe[0], TAYLOR + SQUARINGS + 1)
            link[0](dve.tensor_copy(MT[:], g(pE[0], 0)))
            dve.wait_ge(s_pe[1], TAYLOR + SQUARINGS + 1)
            dve.tensor_copy(M34[:], g(pE[1], 0)).then_inc(s_r, 1)
            dve.wait_ge(s_rp, 1)
            dve.tensor_copy(R[:], g(pF[0], 0)).then_inc(s_r, 1)
            dve.wait_ge(s_rp, 2)
            for n in range(3):
                dve.tensor_copy(core.W2R[:, 512 * n:512 * n + 512], pW[:, n, :])
            dve.tensor_copy(core.b2R[:], pB[0:NE, 0:P])


GT = 4
NG = T // GT


def group_slots(eng, fn):
    fn(0, 0)
    fn(1, 1)
    with eng.Fori(1, NG // 2 - 1) as i:
        fn(2 * i, 0)
        fn(2 * i + 1, 1)
    fn(NG - 2, 0)
    fn(NG - 1, 1)


def more(g, n=1):
    return not isinstance(g, int) or g + n < NG


def ffn_moe_rotated(core):
    X, MV, RS = core.X, core.MV, core.RS
    ident = core.w("ctx", "ident")
    w = lambda n: core.w("ffn0", n)
    NP = NE + 2
    with Stage(core, "ffn0") as st:
        RR = st.sb("RR", [P, T])
        v2 = st.sb("v2", [P, T])
        xn = [st.sb(f"xn{u}", [P, GT, P]) for u in range(2)]
        xh = [st.sb(f"xh{u}", [P, GT, P]) for u in range(2)]
        xT = [st.sb(f"xT{u}", [P, GT * P]) for u in range(2)]
        xTh = [st.sb(f"xTh{u}", [P, GT * P], F32R) for u in range(2)]
        xTl = [st.sb(f"xTl{u}", [P, GT * P], F32R) for u in range(2)]
        hid = [st.sb(f"hid{u}", [P, 2, GT * P]) for u in range(2)]
        acc = [st.sb(f"acc{u}", [P, GT, P]) for u in range(2)]
        ab = [st.sb(f"ab{u}", [P, GT, P]) for u in range(2)]
        wt = [st.sb(f"wt{u}", [P, GT, NE]) for u in range(2)]
        wT = [st.sb(f"wT{u}", [NE, GT * P]) for u in range(2)]
        lg, oa, ob, pr = (st.sb(n, [P, GT, NE]) for n in ("lg", "oa", "ob", "pr"))
        sm = st.sb("sm", [P, 8, GT])
        junk = st.sb("junk", [P, 2 * GT, P])
        zz = st.sb("zz", [P, 2, GT])
        gz = st.sb("gz", [P, 2, GT])
        bn = st.sb("bn", [P, GT, 6])
        mv = st.sb("mv", [P, GT, 2])
        pX, pG, pI, pA = (st.ps(n, [P, 512]) for n in ("pX", "pG", "pI", "pA"))
        pH = [st.ps(f"pH{u}", [P, 512]) for u in range(2)]
        pE = [st.ps(f"pE{u}", [P, GT, P]) for u in range(2)]
        names = ("xn xhp xr xTp xT hi xs lg wt wTp wT in0 acc H h O cmb ab D pab z gt xf own df th z2 own2 own3 vv tick").split()
        s = {n: st.sem(n) for n in names}
        rs_act, rs_dve = token_scales(core, st, MV[:, :, 1], RS[:], "a")
        rr_act, rr_dve = token_scales(core, st, v2[:], RR[:], "b")
        blk = st.block()

        @blk.tensor
        def _(pe):
            def x_transposes(g, u):
                need(pe, s["xn"], g + 1)
                need(pe, s["xT"], g)
                for j in range(GT):
                    ins = pe.transpose(pX[:, P * j:P * j + P], xn[u][:, j, :], ident)
                ins.then_inc(s["xTp"], 1)

            def logits(g, u):
                need(pe, s["xT"], g + 1)
                need(pe, s["wT"], g)
                for j in range(GT):
                    ins = pe.matmul(pG[:, NE * j:NE * j + NE], xT[u][:, P * j:P * j + P], w("gate_w"), start=True, stop=True)
                ins.then_inc(s["lg"], 1)

            def weights_T(g, u):
                need(pe, s["wt"], g + 1)
                for j in range(GT):
                    ins = pe.transpose(pG[0:NE, P * j:P * j + P], wt[u][:, j, :], ident)
                ins.then_inc(s["wTp"], 1)

            def bias_rows(g, u):
                need(pe, s["wT"], g + 1)
                need(pe, s["acc"], g)
                for j in range(GT):
                    ins = pe.matmul(pI[:, P * j:P * j + P], wT[u][:, P * j:P * j + P], core.b2R[:], start=True, stop=True)
                ins.then_inc(s["in0"], 1)

            def up(g, u, p):
                if p == 0:
                    need(pe, s["xs"], g + 1)
                for c in range(2):
                    k0 = slice(EH * p + P * c, EH * p + P * c + P)
                    need(pe, s["h"], 2 * NP * g + 2 * p + c - 1)
                    pe.matmul(pH[c][:], core.up_h[:, k0], xTh[u][:], start=True, stop=False)
                    pe.matmul(pH[c][:], core.up_h[:, k0], xTl[u][:], start=False, stop=False)
                    pe.matmul(pH[c][:], core.up_l[:, k0], xTh[u][:], start=False, stop=True).then_inc(s["H"], 1)

            def down(g, p):
                need(pe, s["h"], 2 * NP * g + 2 * p + 2)
                if p < NE:
                    need(pe, s["cmb"], NE * g + p - 1)
                elif p == NE:
                    need(pe, s["ab"], g)
                for j in range(GT):
                    for c in range(2):
                        hc = hid[p % 2][:, c, P * j:P * j + P]
                        if p < NE:
                            r = 2 * p + c
                            ins = pe.matmul(pE[p % 2][:, j, :], hc, core.W2R[:, P * r:P * r + P], start=(c == 0), stop=(c == 1))
                        else:
                            r = 2 * (p - NE) + c
                            ins = pe.matmul(pA[:, P * j:P * j + P], hc, w("aw2")[:, P * r:P * r + P],
                                            start=(r == 0 and j == 0), stop=(r == 3), skip_group_check=True)
                ins.then_inc(s["O"], 1)

            def group(g, u):
                for p in range(NP):
                    up(g, u, p)
                    if p > 0:
                        down(g, p - 1)
                    elif not isinstance(g, int) or g > 0:
                        down(g - 1, NP - 1)
                    if p == 0:
                        bias_rows(g, u)
                    if more(g):
                        if p == 3:
                            x_transposes(g + 1, 1 - u)
                        if p == 4:
                            logits(g + 1, 1 - u)
                        if p == 7:
                            weights_T(g + 1, 1 - u)

            x_transposes(0, 0)
            logits(0, 0)
            weights_T(0, 0)
            group_slots(pe, group)
            down(NG - 1, NP - 1)

        @blk.scalar
        def _(act):
            def x_evac(g, u):
                need(act, s["xTp"], g + 1)
                need(act, s["H"], 2 * NP * (g - 1))
                act.activation(xT[u][:], pX[:], ACT.Identity, bias=w("ln_b"), scale=w("ln_g")).then_inc(s["xT"], 1)

            def tanh_half(g):
                need(act, s["df"], g + 1)
                act.activation(sm[:, 5, :], sm[:, 4, :], ACT.Tanh, scale=0.5).then_inc(s["th"], 1)

            def w_evac(g, u):
                need(act, s["wTp"], g + 1)
                act.activation(wT[u][:], pG[0:NE, :], ACT.Copy).then_inc(s["wT"], 1)

            def acc_evac(g, u):
                need(act, s["in0"], g + 1)
                need(act, s["xf"], g - 1)
                act.activation(acc[u][:].rearrange("p t d -> p (t d)"), pI[:], ACT.Copy).then_inc(s["acc"], 1)

            def gate(g):
                need(act, s["z"], g + 1)
                act.activation(gz[:, 0, :], zz[:, 0, :], ACT.Tanh, scale=0.5).then_inc(s["gt"], 1)

            def group(g, u):
                for p in range(NP):
                    for c in range(2):
                        r = 2 * p + c
                        need(act, s["H"], 2 * NP * g + r + 1)
                        need(act, s["O"], NP * g + p - 1)
                        b = w("eb1")[:, r:r + 1] if p < NE else w("ab1")[:, r - 2 * NE:r - 2 * NE + 1]
                        act.activation(hid[p % 2][:, c, :], pH[c][:], ACT.Gelu, bias=b).then_inc(s["h"], 1)
                    if p == 0:
                        acc_evac(g, u)
                    if more(g):
                        if p == 3:
                            x_evac(g + 1, 1 - u)
                        if p == 5:
                            tanh_half(g + 1)
                        if p == 7:
                            w_evac(g + 1, 1 - u)
                    if p == 2 and (not isinstance(g, int) or g > 0):
                        gate(g - 1)

            rs_act(act)
            rr_act(act)
            x_evac(0, 0)
            tanh_half(0)
            w_evac(0, 0)
            group_slots(act, group)
            gate(NG - 1)

        @blk.gpsimd
        def _(pool):
            def residual(g, u):
                need(pool, s["xhp"], g + 1)
                pool.tensor_tensor(X[:, bass.ds(GT * g, GT), :], X[:, bass.ds(GT * g, GT), :], xh[u][:], ALU.add).then_inc(s["xr"], 1)

            def add_abel(g, u):
                need(pool, s["ab"], g + 1)
                need(pool, s["xr"], g + 1)
                pool.tensor_tensor(X[:, bass.ds(GT * g, GT), :], X[:, bass.ds(GT * g, GT), :], ab[u][:], ALU.add).then_inc(s["pab"], 1)

            def group(g, u):
                if more(g):
                    residual(g + 1, 1 - u)
                if not isinstance(g, int) or g > 0:
                    add_abel(g - 1, 1 - u)

            residual(0, 0)
            group_slots(pool, group)
            add_abel(NG - 1, 1)

        @blk.vector
        def _(dve):
            GATE = 16

            def normalise(g, u):
                need(dve, s["xTp"], g - 1)
                need(dve, s["xr"], g - 1)
                for j in range(GT):
                    t = GT * g + j
                    ins = dve.tensor_scalar(xn[u][:, j, :], X[:, t, :], MV[:, t, 0:1], RR[:, bass.ds(t, 1)], ALU.subtract, ALU.mult)
                ins.then_inc(s["xn"], 1)
                for j in range(GT):
                    t = GT * g + j
                    ins = dve.tensor_scalar(xh[u][:, j, :], X[:, t, :], MV[:, t, 0:1], RS[:, bass.ds(t, 1)], ALU.subtract, ALU.mult)
                ins.then_inc(s["xhp"], 1)

            def split(g, u):
                need(dve, s["xT"], g + 1)
                need(dve, s["H"], 2 * NP * (g - 1))
                dve.tensor_copy(xTh[u][:], xT[u][:]).then_inc(s["hi"], 1)
                need(dve, s["hi"], g + 1)
                dve.tensor_tensor(xTl[u][:], xT[u][:], xTh[u][:], ALU.subtract).then_inc(s["xs"], 1)

            def gating(g, u, part):
                n = [(0, 7, 12)[part]]

                def link(ins):
                    n[0] += 1
                    ins.then_inc(s["own"], 1)
                    dve.wait_ge(s["own"], GATE * g + n[0])

                bc = lambda a: a.unsqueeze(2).to_broadcast([P, GT, NE])
                row = lambda a: a.unsqueeze(1).to_broadcast([P, GT, NE])
                if part == 0:
                    need(dve, s["lg"], g + 1)
                    need(dve, s["th"], g)
                    link(dve.tensor_tensor(lg[:], pG[:, 0:GT * NE].rearrange("p (t e) -> p t e", e=NE), row(w("gate_b")), ALU.add))
                if part < 2:
                    o, m = ((oa, 0), (ob, 2))[part]
                    link(dve.tensor_reduce(sm[:, m, :], lg[:], AX.X, ALU.max))
                    link(dve.tensor_tensor(pr[:], lg[:], bc(sm[:, m, :]), ALU.is_equal))
                    link(dve.tensor_tensor(pr[:], pr[:], row(w("prio")), ALU.mult))
                    link(dve.tensor_reduce(sm[:, m + 1, :], pr[:], AX.X, ALU.max))
                    link(dve.tensor_tensor(o[:], pr[:], bc(sm[:, m + 1, :]), ALU.is_equal))
                    if part == 0:
                        link(dve.scalar_tensor_tensor(lg[:], o[:], -3e38, lg[:], ALU.mult, ALU.add))
                    else:
                        dve.tensor_tensor(sm[:, 4, :], sm[:, 0, :], sm[:, 2, :], ALU.subtract).then_inc(s["df"], 1)
                else:
                    need(dve, s["th"], g + 1)
                    link(dve.tensor_scalar(sm[:, 6, :], sm[:, 5, :], 0.5, 0.5, ALU.mult, ALU.add))
                    link(dve.tensor_scalar(sm[:, 7, :], sm[:, 5, :], -0.5, 0.5, ALU.mult, ALU.add))
                    link(dve.tensor_tensor(oa[:], oa[:], bc(sm[:, 6, :]), ALU.mult))
                    link(dve.tensor_tensor(ob[:], ob[:], bc(sm[:, 7, :]), ALU.mult))
                    dve.tensor_tensor(wt[u][:], oa[:], ob[:], ALU.add).then_inc(s["wt"], 1)
                    need(dve, s["wt"], g + 1)
                assert n[0] == (7, 12, GATE)[part]

            def combine(g, u, p):
                need(dve, s["O"], NP * g + p + 1)
                if p == 0:
                    need(dve, s["acc"], g + 1)
                else:
                    need(dve, s["cmb"], NE * g + p)
                for j in range(GT):
                    ins = dve.scalar_tensor_tensor(acc[u][:, j, :], pE[p % 2][:, j, :], wt[u][:, j, p:p + 1], acc[u][:, j, :], ALU.mult, ALU.add)
                ins.then_inc(s["cmb"], 1)

            def tail(g, u):
                need(dve, s["O"], NP * g + NP)
                need(dve, s["pab"], g)
                dve.tensor_tensor(ab[u][:], pA[:].rearrange("p (t d) -> p t d", t=GT), w("ab2").unsqueeze(1).to_broadcast([P, GT, P]),
                                  ALU.add).then_inc(s["ab"], 1)

            def tail_gate(g, u):
                need(dve, s["ab"], g + 1)
                need(dve, s["gt"], g)
                for j in range(GT):
                    dve.tensor_tensor_reduce(junk[:, j, :], ab[u][:, j, :], w("g1"), 1.0, 0.0, ALU.mult, ALU.add, zz[:, 0, j:j + 1])
                    ins = dve.tensor_tensor_reduce(junk[:, GT + j, :], acc[u][:, j, :], w("g2"), 1.0, 0.0, ALU.mult, ALU.add, zz[:, 1, j:j + 1])
                ins.then_inc(s["own2"], 1)
                need(dve, s["own2"], g + 1)
                dve.tensor_tensor(zz[:, 0, :], zz[:, 0, :], zz[:, 1, :], ALU.add).then_inc(s["z2"], 1)
                need(dve, s["z2"], g + 1)
                dve.tensor_scalar(zz[:, 0, :], zz[:, 0, :], w("gc_b"), None, ALU.add).then_inc(s["z"], 1)
                dve.tensor_tensor(acc[u][:], acc[u][:], ab[u][:], ALU.subtract).then_inc(s["D"], 1)

            def final(g, u):
                need(dve, s["gt"], g + 1)
                dve.tensor_scalar(gz[:, 1, :], gz[:, 0, :], 0.5, 0.5, ALU.mult, ALU.add).then_inc(s["own3"], 1)
                need(dve, s["own3"], g * 3 + 1)
                need(dve, s["D"], g + 1)
                need(dve, s["pab"], g + 1)
                for j in range(GT):
                    t = GT * g + j
                    ins = dve.scalar_tensor_tensor(X[:, t, :], acc[u][:, j, :], gz[:, 1, j:j + 1], X[:, t, :], ALU.mult, ALU.add)
                ins.then_inc(s["xf"], 1)
                need_apart(dve, s["xf"], g + 1, s["tick"])
                for j in range(GT):
                    ins = dve.bn_stats(bn[:, j, :], X[:, GT * g + j, :])
                ins.then_inc(s["own3"], 1)
                need_apart(dve, s["own3"], g * 3 + 2, s["tick"])
                for j in range(GT):
                    ins = dve.bn_aggr(mv[:, j, :], bn[:, j, :])
                ins.then_inc(s["own3"], 1)
                need(dve, s["own3"], g * 3 + 3)
                dve.tensor_scalar(MV[:, bass.ds(GT * g, GT), :], mv[:], 1.0, None, ALU.mult)

            def group(g, u):
                past = not isinstance(g, int) or g > 0
                if past:
                    tail(g - 1, 1 - u)
                for p in range(NE):
                    combine(g, u, p)
                    if p == 0 and past:
                        tail_gate(g - 1, 1 - u)
                    if more(g):
                        if p == 1:
                            normalise(g + 1, 1 - u)
                        if p == 3:
                            split(g + 1, 1 - u)
                        if p >= 3:
                            gating(g + 1, 1 - u, p - 3)
                if past:
                    final(g - 1, 1 - u)

            rs_dve(dve)
            dve.tensor_tensor(v2[:], MV[:, :, 1], RS[:], ALU.mult).then_inc(s["vv"], 1)
            dve.wait_ge(s["vv"], 1)
            dve.tensor_tensor(v2[:], v2[:], RS[:], ALU.mult).then_inc(s["vv"], 1)
            dve.wait_ge(s["vv"], 2)
            rr_dve(dve)
            dve.tensor_tensor(RR[:], RR[:], RS[:], ALU.mult).then_inc(s["vv"], 1)
            dve.wait_ge(s["vv"], 3)
            normalise(0, 0)
            split(0, 0)
            for part in range(3):
                gating(0, 0, part)
            group_slots(dve, group)
            tail(NG - 1, 1)
            tail_gate(NG - 1, 1)
            final(NG - 1, 1)


N1, H1 = 16, 256
CAP = -(-5 * T * P // (4 * N1))
BITS = 28
SUB = [(0, P), (P, P), (2 * P, CAP - 2 * P)]


def route_top1(core):
    X, MV, RS = core.X, core.MV, core.RS
    nc = core.nc
    ident = core.w("ctx", "ident")
    w = lambda n: core.w("route", n)
    slots = core.slots
    with Stage(core, "route") as st:
        XH = core.XH
        xT = [st.sb(f"xT{u}", [P, GT * P]) for u in range(2)]
        ex, oh, mv, ca, cb, kp = (st.sb(n, [P, T, N1]) for n in ("ex", "oh", "mv", "ca", "cb", "kp"))
        mx, sm, vv = (st.sb(n, [P, T]) for n in ("mx", "sm", "vv"))
        MT = st.sb("MT", [P, 4 * P])
        ones = st.sb("ones", [P, 4 * P])
        hit = st.sb("hit", [P, 4 * P])
        cand, thr, cnt, ge = (st.sb(n, [P, 2]) for n in ("cand", "thr", "cnt", "ge"))
        dg, rows = st.sb("dg", [N1, 2 * N1]), st.sb("rows", [P, 2 * N1])
        zero = st.sb("zero", [P, P])
        pX = [st.ps(f"pX{u}", [P, 512]) for u in range(2)]
        pL, pM, pC, pP, pR = (st.ps(n, [P, 512]) for n in ("pL", "pM", "pC", "pP", "pR"))
        names = "xh xTp xT L own cnt tot thr dx ex mvp MTp rowsp dgr eqr ca prf zst sl zfill".split()
        s = {n: st.sem(n) for n in names}
        s["scat"] = core.gpsimd_dma_sem("scattered")
        rs_act, rs_dve = token_scales(core, st, MV[:, :, 1], RS[:], "a")
        blk = st.block()
        SH = [P, T, N1]
        te = lambda t: t[:].rearrange("p (t e) -> p t e", e=N1)
        bt = lambda a: a.unsqueeze(2).to_broadcast(SH)
        be = lambda a: a.unsqueeze(1).to_broadcast(SH)

        @blk.tensor
        def _(pe):
            def turn(g):
                pe.wait_ge(s["xh"], g + 1)
                if g >= 2:
                    pe.wait_ge(s["xT"], g - 1)
                for j in range(GT):
                    ins = pe.transpose(pX[g % 2][:, P * j:P * j + P], XH[:, GT * g + j, :], ident)
                ins.then_inc(s["xTp"], 1)

            turn(0)
            for g in range(NG):
                if g + 1 < NG:
                    turn(g + 1)
                pe.wait_ge(s["xT"], g + 1)
                for j in range(GT):
                    at = (GT * g + j) * N1
                    ins = pe.matmul(pL[:, at:at + N1], xT[g % 2][:, P * j:P * j + P], w("Wg"), start=True, stop=True)
                ins.then_inc(s["L"], 1)
            pe.wait_ge(s["mvp"], 1)
            for j in range(4):
                ins = pe.transpose(pM[:, P * j:P * j + P], mv[:].rearrange("p t e -> p (t e)")[:, P * j:P * j + P], ident)
            ins.then_inc(s["MTp"], 1)
            def totals(k):
                pe.wait_ge(s["cnt"], k + 1)
                pe.matmul(pC[:, 0:1], w("same"), cnt[:, 0:1], start=True, stop=True).then_inc(s["tot"], 1)

            with pe.Fori(0, BITS // 4) as i:
                for q in range(4):
                    totals(4 * i + q)
            totals(BITS)
            pe.wait_ge(s["dgr"], 1)
            pe.matmul(pR[:, 0:2 * N1], ones[0:N1, 0:P], dg[:], start=True, stop=True).then_inc(s["rowsp"], 1)
            for n in range(2):
                src = (ca, kp)[n]
                pe.wait_ge(s["eqr"], n + 1)
                pe.matmul(pP[:], w("below"), src[:].rearrange("p t e -> p (t e)"), start=True, stop=False)
                pe.wait_ge(s["ca"], n + 1)
                pe.matmul(pP[:], ones[:, 0:P], cb[:].rearrange("p t e -> p (t e)"), start=False, stop=True).then_inc(s["prf"], 1)

        @blk.scalar
        def _(act):
            rs_act(act)
            for g in range(NG):
                act.wait_ge(s["xTp"], g + 1)
                if g >= 2:
                    act.wait_ge(s["L"], g - 1)
                act.activation(xT[g % 2][:], pX[g % 2][:], ACT.Copy).then_inc(s["xT"], 1)
            act.wait_ge(s["dx"], 1)
            act.activation(ex[:], ex[:], ACT.Exp).then_inc(s["ex"], 1)

        @blk.vector
        def _(dve):
            link = Chain(dve, s["own"])
            dve.memset(ones[:], 1.0)
            dve.memset(zero[:], 0.0).then_inc(s["zst"], 1)
            rs_dve(dve)
            for g in range(NG):
                for t in range(GT * g, GT * g + GT):
                    ins = dve.tensor_scalar(XH[:, t, :], X[:, t, :], MV[:, t, 0:1], RS[:, t:t + 1], ALU.subtract, ALU.mult)
                ins.then_inc(s["xh"], 1)
            dve.wait_ge(s["L"], NG)
            L3 = pL[:].rearrange("p (t e) -> p t e", e=N1)
            link(dve.tensor_reduce(mx[:], L3, AX.X, ALU.max))
            dve.tensor_tensor(ex[:], L3, bt(mx[:]), ALU.subtract).then_inc(s["dx"], 1)
            dve.wait_ge(s["ex"], 1)
            link(dve.tensor_reduce(mx[:], ex[:], AX.X, ALU.max))
            link(dve.tensor_reduce(sm[:], ex[:], AX.X, ALU.add))
            link(dve.reciprocal(vv[:], sm[:]))
            link(dve.tensor_tensor(vv[:], vv[:], mx[:], ALU.mult))
            link(dve.tensor_tensor(oh[:], ex[:], bt(mx[:]), ALU.is_equal))
            link(dve.tensor_tensor(oh[:], oh[:], be(w("prio")), ALU.mult))
            link(dve.tensor_reduce(mx[:], oh[:], AX.X, ALU.max))
            link(dve.tensor_tensor(oh[:], oh[:], bt(mx[:]), ALU.is_equal))
            dve.tensor_tensor(mv[:], oh[:], bt(vv[:]), ALU.mult).then_inc(s["mvp"], 1)
            dve.memset(thr[:], 0.0)
            link(dve.memset(cand[:], 1.0))
            dve.wait_ge(s["MTp"], 1)
            link(dve.tensor_copy(MT[:], pM[:]))
            own0 = link.n
            def search(k):
                dve.scalar_tensor_tensor(hit[:], MT[:], cand[:, 0:1], ones[:], ALU.is_ge, ALU.mult, accum_out=cnt[:, 0:1]).then_inc(s["cnt"], 1)
                dve.wait_ge(s["tot"], k + 1)
                dve.tensor_scalar(ge[:, 0:1], pC[:, 0:1], float(CAP), w("pow2")[:, bass.ds(k, 1)], ALU.is_ge, ALU.mult).then_inc(s["thr"], 1)
                dve.wait_ge(s["thr"], 2 * k + 1)
                dve.tensor_scalar(cand[:, 0:1], thr[:, 0:1], ge[:, 0:1], w("pow2")[:, bass.ds(k + 1, 1)], ALU.add, ALU.add).then_inc(s["own"], 1)
                dve.tensor_scalar(thr[:, 0:1], thr[:, 0:1], ge[:, 0:1], None, ALU.add).then_inc(s["thr"], 1)
                dve.wait_ge(s["own"], own0 + k + 1)

            with dve.Fori(0, BITS // 4) as i:
                for q in range(4):
                    search(4 * i + q)
            dve.wait_ge(s["thr"], 2 * BITS)
            link.n = own0 + BITS
            dve.scalar_tensor_tensor(hit[:], MT[:], thr[:, 0:1], ones[:], ALU.is_gt, ALU.mult, accum_out=cnt[:, 0:1]).then_inc(s["cnt"], 1)
            dve.wait_ge(s["tot"], BITS + 1)
            link(dve.tensor_scalar(ge[:, 0:1], pC[:, 0:1], -1.0, float(CAP), ALU.mult, ALU.add))
            dve.tensor_scalar(dg[:, 0:N1], ident[0:N1, 0:N1], thr[0:N1, 0:1], None, ALU.mult).then_inc(s["own"], 1)
            link.n += 1
            dve.wait_ge(s["own"], link.n)
            dve.tensor_scalar(dg[:, N1:2 * N1], ident[0:N1, 0:N1], ge[0:N1, 0:1], None, ALU.mult).then_inc(s["dgr"], 1)
            dve.wait_ge(s["rowsp"], 1)
            link(dve.tensor_copy(rows[:], pR[:, 0:2 * N1]))
            link(dve.tensor_tensor(ca[:], mv[:], be(rows[:, 0:N1]), ALU.is_equal))
            dve.tensor_tensor(ca[:], ca[:], oh[:], ALU.mult).then_inc(s["eqr"], 1)
            dve.wait_ge(s["eqr"], 1)

            def tiles_before(src):
                link(dve.memset(cb[:, 0:1, :], 0.0))
                link(dve.tensor_copy(cb[:, 1:T, :], src[:, 0:T - 1, :]))
                a, b = cb, ex
                for d in (1, 2, 4, 8, 16):
                    dve.tensor_copy(b[:, 0:d, :], a[:, 0:d, :])
                    last = dve.tensor_tensor(b[:, d:T, :], a[:, d:T, :], a[:, 0:T - d, :], ALU.add)
                    link(last)
                    a, b = b, a
                dve.tensor_copy(cb[:], a[:]).then_inc(s["ca"], 1)

            tiles_before(ca)
            link(dve.tensor_tensor(kp[:], mv[:], be(rows[:, 0:N1]), ALU.is_gt))
            dve.wait_ge(s["prf"], 1)
            P3 = pP[:].rearrange("p (t e) -> p t e", e=N1)
            link(dve.tensor_tensor(ex[:], P3, be(rows[:, N1:2 * N1]), ALU.is_lt))
            link(dve.tensor_tensor(ex[:], ex[:], ca[:], ALU.mult))
            dve.tensor_tensor(kp[:], kp[:], ex[:], ALU.add).then_inc(s["eqr"], 1)
            dve.wait_ge(s["eqr"], 2)
            tiles_before(kp)
            link(dve.tensor_reduce(sm[:], kp[:], AX.X, ALU.add))
            dve.wait_ge(s["prf"], 2)
            link(dve.tensor_tensor(ex[:], P3, be(w("base")), ALU.add))
            link(dve.tensor_tensor(ex[:], ex[:], kp[:], ALU.mult))
            link(dve.tensor_reduce(mx[:], ex[:], AX.X, ALU.add))
            link(dve.tensor_scalar(sm[:], sm[:], -float(2 * N1 * CAP), float(2 * N1 * CAP), ALU.mult, ALU.add))
            dve.tensor_tensor(slots[:], sm[:], mx[:], ALU.add).then_inc(s["sl"], 1)
            split_trees(core, st, dve)

        @blk.sync
        def _(sp):
            sp.dma_start(core.pack["tree_full"][:], core.A["tree_full"]).then_inc(core.trees_loaded, 16)
            sp.wait_ge(s["zst"], 1)
            for q in range(N1 * CAP // P):
                sp.dma_start(core.xs[P * q:P * q + P, :], zero[:]).then_inc(s["zfill"], 16)

        @blk.gpsimd
        def _(pool):
            pool.wait_ge(s["sl"], 1)
            pool.wait_ge(s["zfill"], 16 * (N1 * CAP // P))
            for t in range(T):
                pool.indirect_dma_start(core.xs[:, :], bass.IndirectOffsetOnAxis(ap=slots[:, t:t + 1], axis=0), XH[:, t, :], None,
                                        bounds_check=N1 * CAP - 1, oob_is_err=False).then_inc(s["scat"], 16)
            pool.wait_ge(s["scat"], 16 * T)


def expert_slots(eng, slot):
    for q in range(4):
        slot(q, q)
    with eng.Fori(1, N1 // 4 - 1) as i:
        for q in range(4):
            slot(4 * i + q, q)
    for q in range(4):
        slot(N1 - 4 + q, q)


def run_experts(core, masks):
    X, MV = core.X, core.MV
    ident = core.w("ctx", "ident")
    w = lambda n: core.w("route", n)
    A = core.A
    with Stage(core, "exp") as st:
        two = lambda name, shape: [st.sb(f"{name}{u}", shape) for u in range(2)]
        four = lambda name, shape: [st.sb(f"{name}{v}", shape) for v in range(4)]
        W1, W2, b2, xe = four("W1", [P, H1]), four("W2", [P, 2, P]), four("b2", [P, P]), four("xe", [P, 3, P])
        xT, hid, ye = two("xT", [P, CAP]), two("hid", [P, 2, CAP]), two("ye", [P, 3, P])
        YG = core.XH
        bn, mv = st.sb("bn", [P, GT, 6]), st.sb("mv", [P, GT, 2])
        pX = [st.ps(f"pX{u}", [P, 512]) for u in range(2)]
        pH = [st.ps(f"pH{u}", [P, 512]) for u in range(2)]
        pY = [st.ps(f"pY{u}", [P, 512]) for u in range(2)]
        pM = [st.ps(f"pM{u}", [P, P]) for u in range(2)]
        prep = prep_parts(core, 2, False, st, [pH[0][:], pH[1][:]], [pX[0][:], pX[1][:], pY[0][:], pY[1][:]])
        mask_prep = [mask_parts(core, L, masks[L], st, pM[L - 2][:]) for L in (2, 3)]
        names = "xTp xT H h Yp Y own bn".split()
        s = {n: st.sem(n) for n in names}
        s_ld, s_st = [st.sem(f"ld{v}") for v in range(4)], [core.gpsimd_dma_sem(f"rows_stored{u}") for u in range(2)]
        s_g = [core.gpsimd_dma_sem(f"gathered{u}") for u in range(4)]
        blk = st.block()
        LD = 5 * 16 // 4

        @blk.sync
        def _(sp):
            def load(e, q):
                need(sp, s["Yp"], e - 3)
                need(sp, s["Y"], e - 3)
                sp.dma_start(W1[q][:], A["L1_W1"][bass.ds(e, 1), :, :].rearrange("e d h -> (e d) h")).then_inc(s_ld[q], 16)
                sp.dma_start(W2[q][:], A["L1_W2"][bass.ds(e, 1), :, :].rearrange("e (c h) d -> (e h) c d", c=2)).then_inc(s_ld[q], 16)
                sp.dma_start(b2[q][:], A["L1_b2"][bass.ds(e, 1), :].to_broadcast([P, P])).then_inc(s_ld[q], 16)
                sp.dma_start(xe[q][:, 0:2, :], core.xs[bass.ds(CAP * e, 2 * P), :].rearrange("(t p) d -> p t d", t=2)).then_inc(s_ld[q], 16)
                sp.dma_start(xe[q][0:CAP - 2 * P, 2, :], core.xs[bass.ds(CAP * e + 2 * P, CAP - 2 * P), :]).then_inc(s_ld[q], 16)

            expert_slots(sp, load)

        @blk.tensor
        def _(pe):
            def turn(e, q):
                u = q % 2
                pe.wait_ge(s_ld[q], LD * (e - q + 4))
                need(pe, s["xT"], e - 1)
                for j, (o, n) in enumerate(SUB):
                    ins = pe.transpose(pX[u][:, o:o + n], xe[q][0:n, j, :], ident[0:n, 0:n])
                ins.then_inc(s["xTp"], 1)

            def up(e, q):
                need(pe, s["xT"], e + 1)
                for c in range(2):
                    need(pe, s["h"], 2 * e + c - 1)
                    pe.matmul(pH[c][:, 0:CAP], W1[q][:, P * c:P * c + P], xT[q % 2][:], start=True, stop=True).then_inc(s["H"], 1)

            def down(e, q):
                u = q % 2
                need(pe, s["h"], 2 * e + 2)
                need(pe, s["Y"], e - 1)
                for j, (o, n) in enumerate(SUB):
                    for c in range(2):
                        ins = pe.matmul(pY[u][0:n, P * j:P * j + P], hid[u][:, c, o:o + n], W2[q][:, c, :], start=(c == 0), stop=(c == 1))
                ins.then_inc(s["Yp"], 1)

            def slot(e, q):
                if not isinstance(e, int) or e + 1 < N1:
                    turn(e + 1, (q + 1) % 4)
                up(e, q)
                if not isinstance(e, int) or e > 0:
                    down(e - 1, (q - 1) % 4)

            turn(0, 0)
            expert_slots(pe, slot)
            down(N1 - 1, 3)
            pe.wait_ge(s["Y"], N1)
            prep[0](pe)
            for on_tensor, _ in mask_prep:
                on_tensor(pe)

        @blk.scalar
        def _(act):
            def slot(e, q):
                for c in range(2):
                    need(act, s["H"], 2 * e + c + 1)
                    need(act, s["Yp"], e - 1)
                    act.activation(hid[q % 2][:, c, :], pH[c][:, 0:CAP], ACT.Gelu_apprx_tanh,
                                   bias=w("b1")[:, bass.ds(2 * e + c, 1)]).then_inc(s["h"], 1)

            expert_slots(act, slot)
            prep[1](act)

        @blk.vector
        def _(dve):
            def x_evac(e, q):
                need(dve, s["xTp"], e + 1)
                need(dve, s["H"], 2 * (e - 1))
                dve.tensor_copy(xT[q % 2][:], pX[q % 2][:, 0:CAP]).then_inc(s["xT"], 1)

            def rows_out(e, q):
                u = q % 2
                need(dve, s["Yp"], e + 1)
                need(dve, s_st[u], 16 * (e - u))
                for j, (o, n) in enumerate(SUB):
                    ins = dve.tensor_tensor(ye[u][0:n, j, :], pY[u][0:n, P * j:P * j + P], b2[q][0:n, :], ALU.add)
                ins.then_inc(s["Y"], 1)

            def slot(e, q):
                if not isinstance(e, int) or e + 1 < N1:
                    x_evac(e + 1, (q + 1) % 4)
                if not isinstance(e, int) or e > 0:
                    rows_out(e - 1, (q - 1) % 4)

            x_evac(0, 0)
            expert_slots(dve, slot)
            rows_out(N1 - 1, 3)
            prep[2](dve)
            for _, on_vector in mask_prep:
                on_vector(dve)
            for g in range(NG):
                dve.wait_ge(s_g[g % 4], 16 * GT * (g // 4 + 1))
                x4 = X[:, GT * g:GT * g + GT, :]
                dve.tensor_tensor(x4, x4, YG[:, GT * g:GT * g + GT, :], ALU.add).then_inc(s["own"], 1)
                dve.wait_ge(s["own"], g + 1)
                for j in range(GT):
                    ins = dve.bn_stats(bn[:, j, :], X[:, GT * g + j, :])
                ins.then_inc(s["bn"], 1)
                dve.wait_ge(s["bn"], g + 1)
                for j in range(GT):
                    dve.bn_aggr(MV[:, GT * g + j, :], bn[:, j, :])

        @blk.gpsimd
        def _(pool):
            def store(e, q):
                u = q % 2
                need(pool, s["Y"], e + 1)
                pool.dma_start(core.ys[bass.ds(CAP * e, 2 * P), :].rearrange("(t p) d -> p t d", t=2), ye[u][:, 0:2, :]).then_inc(s_st[u], 16)
                pool.dma_start(core.ys[bass.ds(CAP * e + 2 * P, CAP - 2 * P), :], ye[u][0:CAP - 2 * P, 2, :]).then_inc(s_st[u], 16)

            expert_slots(pool, store)
            for u in range(2):
                pool.wait_ge(s_st[u], 16 * N1)
            for t in range(T):
                g = t // GT
                if g >= 4 and t % GT == 0:
                    pool.wait_ge(s_g[g % 4], 16 * GT * (g // 4))
                pool.indirect_dma_start(YG[:, t, :], None, core.ys[:, :], bass.IndirectOffsetOnAxis(ap=core.slots[:, t:t + 1], axis=0),
                                        bounds_check=N1 * CAP - 1, oob_is_err=False).then_inc(s_g[g % 4], 16)


NT, LW, NLEAF = 3, 64, 16
NCH = NLEAF * LW // P
STEPS = NT * NCH
SELP = 64
MIXC = NCH * P + P
BIG = 2.0 ** 100
GT_P = GT * P


def tree_buffers(core, stack):
    sb = lambda name, shape, dt: stack.enter_context(core.nc.sbuf_tensor(name, shape, dt))
    core.w1h, core.w2h = sb("w1h", [P, STEPS * P], F32R), sb("w2h", [P, STEPS * P], F32R)
    core.w1l, core.w2l = sb("w1l", [P, STEPS * P], F32R), sb("w2l", [P, STEPS * P], F32R)
    core.mix = sb("mix", [P, 2, MIXC], BF16)


def split_trees(core, st, dve):
    w = lambda n: core.w("tree_full", n)
    dve.wait_ge(core.trees_loaded, 16)
    link = Chain(dve, st.sem("split"))
    t1, t2 = st.sb("t1", [P, MIXC], BF16), st.sb("t2", [P, MIXC], BF16)
    r = st.sb("r", [P, MIXC])
    for full, hi, lo in ((w("w1"), core.w1h, core.w1l), (w("w2"), core.w2h, core.w2l)):
        link(dve.tensor_copy(hi[:], full))
        dve.tensor_tensor(lo[:], full, hi[:], ALU.subtract)
    part = lambda rows, i: core.w("tree", "part")[0:rows, i:i + 1]
    for n, (name, rows) in enumerate((("mixqk", P), ("mixv", SELP))):
        q = slice(0, rows)
        out = core.mix[q, n, :]
        link(dve.tensor_copy(t1[q, :], w(name)))
        link(dve.tensor_tensor(r[q, :], w(name), t1[q, :], ALU.subtract))
        link(dve.tensor_copy(t2[q, :], r[q, :]))
        link(dve.tensor_tensor(r[q, :], r[q, :], t2[q, :], ALU.subtract))
        link(dve.tensor_scalar(t1[q, :], t1[q, :], part(rows, 0), None, ALU.mult))
        link(dve.scalar_tensor_tensor(t1[q, :], t2[q, :], part(rows, 1), t1[q, :], ALU.mult, ALU.add))
        link(dve.scalar_tensor_tensor(out, r[q, :], part(rows, 2), t1[q, :], ALU.mult, ALU.add))


def attention_trees(core):
    X, MV, RS = core.X, core.MV, core.RS
    ident = core.w("ctx", "ident")
    w = lambda n: core.w("tree", n)
    SC = float(P) ** -0.5
    with Stage(core, "tree") as st:
        two = lambda name, shape, dt=F32: [st.sb(f"{name}{u}", shape, dt) for u in range(2)]
        xh, xT = st.sb("xh", [P, GT, P]), st.sb("xT", [P, GT_P])
        xTh, xTl = two("xTh", [P, GT_P], F32R), two("xTl", [P, GT_P], F32R)
        zs, go = st.sb("zs", [P, GT * NT, NLEAF]), st.sb("go", [P, GT * NT, NLEAF, 2])
        r2, r3 = st.sb("r2", [P, GT * NT, 2, 2]), st.sb("r3", [P, GT * NT, 4, 2])
        r4 = st.sb("r4", [P, GT * NT, 8, 2])
        oh = st.sb("oh", [P, GT, NT + 1, 4, NLEAF])
        sel = two("sel", [P, 2, GT_P], BF16)
        hh, hl = two("hh", [P, GT_P], F32R), two("hl", [P, GT_P], F32R)
        qT, kT, vv = two("qT", [P, GT_P]), two("kT", [P, GT_P]), two("vv", [P, GT_P])
        vT = st.sb("vT", [P, GT_P])
        pr, PT = two("pr", [P, S]), two("PT", [P, S])
        nm, sm, rc = two("nm", [P, 1]), two("sm", [P, 1]), two("rc", [P, 1])
        bn, mv = two("bn", [P, 6]), two("mv", [P, 2])
        pX, pS, pT, pO = (st.ps(n, [P, 512]) for n in ("pX", "pS", "pT", "pO"))
        pH = [st.ps(f"pH{u}", [P, 512]) for u in range(2)]
        pY = [st.ps(f"pY{u}", [P, 512]) for u in range(2)]
        names = "xh xTp xT xs np own oh ohp sel zero H h lo c Y y vTp v S nm mx P PTp PT O rc X bn mv tick".split()
        s = {n: st.sem(n) for n in names}
        rs_act, rs_dve = token_scales(core, st, MV[:, :, 1], RS[:], "a")
        blk = st.block()
        past = lambda g: not isinstance(g, int) or g > 0
        rows = lambda p: (slice(SELP * (p % 2), SELP * (p % 2) + SELP), p // 2)

        @blk.tensor
        def _(pe):
            def x_transposes(g, u):
                need(pe, s["xh"], g + 1)
                need(pe, s["sel"], 2 * g)
                for j in range(GT):
                    ins = pe.transpose(pX[:, P * j:P * j + P], xh[:, j, :], ident)
                ins.then_inc(s["xTp"], 1)

            def nodes(g, u):
                need(pe, s["xT"], g + 1)
                for j in range(GT):
                    ins = pe.matmul(pX[:, NT * NLEAF * j:NT * NLEAF * (j + 1)], xT[:, P * j:P * j + P], w("nodes"), start=True, stop=True)
                ins.then_inc(s["np"], 1)

            def select(g, u, n):
                if n == 0:
                    need(pe, s["oh"], g + 1)
                else:
                    need(pe, s["sel"], 2 * g + 1)
                for j in range(GT):
                    src = oh[:, j, 2 * n:2 * n + 2, :, :].rearrange("p n r l -> p (n r l)")
                    ins = pe.transpose(pX[:, P * j:P * j + P], src, ident)
                ins.then_inc(s["ohp"], 1)

            def hidden(g, u, k):
                m = STEPS * g + k
                p, c = divmod(k, NCH)
                if k == 0:
                    need(pe, s["xs"], g + 1)
                    need(pe, s["sel"], 2 * g + 2)
                need(pe, s["lo"], m - 1)
                q, n = rows(p)
                k0 = slice(P * k, P * k + P)
                pe.matmul(pH[k % 2][:], core.w1h[:, k0], xTh[u][:], start=True, stop=False)
                pe.matmul(pH[k % 2][:], core.w1h[:, k0], xTl[u][:], start=False, stop=False)
                pe.matmul(pH[k % 2][:], core.w1l[:, k0], xTh[u][:], start=False, stop=False)
                pe.matmul(pH[k % 2][:], core.mix[q, n, P * c:P * c + P], sel[u][q, n, :], start=False, stop=True).then_inc(s["H"], 1)

            def out(g, u, k):
                m = STEPS * g + k
                p, c = divmod(k, NCH)
                q, n = rows(p)
                bank = pY[(u + p) % 2]
                if c == 0:
                    need(pe, s["y"], NT * g + p - 1)
                need(pe, s["lo"], m + 1)
                k0 = slice(P * k, P * k + P)
                b2 = core.mix[q, n, NCH * P:MIXC]
                parts = ((hh, core.w2h), (hh, core.w2l), (hl, core.w2h))
                for i, (h, w2) in enumerate(parts):
                    ins = pe.matmul(bank[:], w2[:, k0], h[k % 2][:], start=(c == 0 and i == 0), stop=False)
                ins.then_inc(s["c"], 1)
                if c == NCH - 1:
                    pe.matmul(bank[:], b2, sel[u][q, n, :], start=False, stop=True).then_inc(s["Y"], 1)

            def v_transposes(g, u):
                need(pe, s["y"], NT * (g + 1))
                need(pe, s["PT"], GT * g)
                for j in range(GT):
                    ins = pe.transpose(pT[:, P * j:P * j + P], vT[:, P * j:P * j + P], ident)
                ins.then_inc(s["vTp"], 1)

            def scores(g, u, j):
                t = GT * g + j
                need(pe, s["y"], NT * (g + 1))
                need(pe, s["P"], t)
                b0 = S * (j // TB)
                pe.matmul(pS[:, 0:S], qT[u][:, P * j:P * j + P], kT[u][:, b0:b0 + S], start=True, stop=True).then_inc(s["S"], 1)

            def turn(g, u, j):
                t = GT * g + j
                need(pe, s["P"], t + 1)
                need(pe, s["PT"], t)
                if j == 0:
                    need(pe, s["v"], g + 1)
                for n in range(TB):
                    ins = pe.transpose(pT[:, P * n:P * n + P], pr[j % 2][:, P * n:P * n + P], ident)
                ins.then_inc(s["PTp"], 1)

            def attend(g, u, j):
                t = GT * g + j
                need(pe, s["PT"], t + 1)
                need(pe, s["X"], t)
                for n in range(TB):
                    k0 = P * (TB * (j // TB) + n)
                    ins = pe.matmul(pO[:, 0:P], PT[j % 2][:, P * n:P * n + P], vv[u][:, k0:k0 + P], start=(n == 0), stop=(n == TB - 1))
                ins.then_inc(s["O"], 1)

            def attention(g, u, k):
                if k == 1:
                    v_transposes(g, u)
                for j in range(GT):
                    if k == 3 * j + 1:
                        scores(g, u, j)
                    if k == 3 * j + 4:
                        turn(g, u, j)
                    if k == 3 * j + 6:
                        attend(g, u, j)

            def group(g, u):
                for k in range(STEPS):
                    if k < STEPS - 1:
                        hidden(g, u, k + 1)
                    elif more(g):
                        hidden(g + 1, 1 - u, 0)
                    if past(g):
                        attention(g - 1, 1 - u, k)
                    if more(g):
                        if k == 14:
                            x_transposes(g + 1, 1 - u)
                        if k == 16:
                            nodes(g + 1, 1 - u)
                        if k == 20:
                            select(g + 1, 1 - u, 0)
                        if k == 21:
                            select(g + 1, 1 - u, 1)
                    out(g, u, k)

            x_transposes(0, 0)
            nodes(0, 0)
            select(0, 0, 0)
            select(0, 0, 1)
            hidden(0, 0, 0)
            group_slots(pe, group)
            for k in range(STEPS):
                attention(NG - 1, 1, k)

        @blk.scalar
        def _(act):
            def hidden(g, u, k):
                m = STEPS * g + k
                need(act, s["H"], m + 1)
                need(act, s["c"], m - 1)
                act.activation(hh[k % 2][:], pH[k % 2][:], ACT.Relu).then_inc(s["h"], 1)

            def x_evac(g, u):
                need(act, s["xTp"], g + 1)
                need(act, s["xs"], g)
                act.activation(xT[:], pX[:], ACT.Copy).then_inc(s["xT"], 1)

            def out(g, u, p):
                need(act, s["Y"], NT * g + p + 1)
                if p == 0:
                    need(act, s["O"], GT * (g - 1))
                if p == 2:
                    need(act, s["vTp"], g)
                act.activation((qT[u], kT[u], vT)[p][:], pY[(u + p) % 2][:], ACT.Copy).then_inc(s["y"], 1)

            def attention(g, u, k):
                if k == 1:
                    need(act, s["vTp"], g + 1)
                    act.activation(vv[u][:], pT[:], ACT.Copy).then_inc(s["v"], 1)
                for j in range(GT):
                    t = GT * g + j
                    if k == 3 * j + 2:
                        need(act, s["nm"], t + 1)
                        need(act, s["PTp"], t - 1)
                        need(act, s["rc"], t - 1)
                        act.activation(pr[j % 2][:], pS[:, 0:S], ACT.Exp, bias=nm[j % 2][:, 0:1], scale=SC,
                                       accum_out=sm[j % 2][:, 0:1]).then_inc(s["P"], 1)
                    if k == 3 * j + 4:
                        need(act, s["PTp"], t + 1)
                        need(act, s["O"], t - 1)
                        act.activation(PT[j % 2][:], pT[:, 0:S], ACT.Copy).then_inc(s["PT"], 1)

            def group(g, u):
                for k in range(STEPS):
                    hidden(g, u, k)
                    if k == 0 and past(g):
                        out(g - 1, 1 - u, 2)
                    if k in (NCH, 2 * NCH):
                        out(g, u, k // NCH - 1)
                    if past(g):
                        attention(g - 1, 1 - u, k)
                    if k == 14 and more(g):
                        x_evac(g + 1, 1 - u)

            rs_act(act)
            x_evac(0, 0)
            group_slots(act, group)
            out(NG - 1, 1, 2)
            for k in range(STEPS):
                attention(NG - 1, 1, k)

        @blk.vector
        def _(dve):
            def normalise(g, u):
                need(dve, s["xTp"], g)
                for j in range(GT):
                    t = GT * g + j
                    ins = dve.tensor_scalar(xh[:, j, :], X[:, t, :], MV[:, t, 0:1], RS[:, bass.ds(t, 1)], ALU.subtract, ALU.mult)
                ins.then_inc(s["xh"], 1)

            LINKS = 5

            def route(g, u, step):
                def link(n, ins):
                    ins.then_inc(s["own"], 1)
                    need(dve, s["own"], LINKS * g + n)
                if step == 0:
                    need(dve, s["xT"], g + 1)
                    link(1, dve.tensor_copy(xTh[u][:], xT[:]))
                if step == 1:
                    dve.tensor_tensor(xTl[u][:], xT[:], xTh[u][:], ALU.subtract).then_inc(s["xs"], 1)
                if step == 2:
                    need(dve, s["np"], g + 1)
                    nb = w("node_b").rearrange("p (n l) -> p n l", l=NLEAF).unsqueeze(1).to_broadcast([P, GT, NT, NLEAF])
                    link(2, dve.tensor_tensor(zs[:].rearrange("p (t n) l -> p t n l", n=NT),
                                              pX[:, 0:GT * NT * NLEAF].rearrange("p (t n l) -> p t n l", n=NT, l=NLEAF), nb, ALU.add))
                    dve.tensor_scalar(go[:, :, :, 1], zs[:], 0.0, None, ALU.is_ge)
                    link(3, dve.tensor_scalar(go[:, :, :, 0], zs[:], 0.0, None, ALU.is_lt))
                if step == 3:
                    link(4, dve.tensor_tensor(r2[:], go[:, :, 1:3, :], go[:, :, 0, :].unsqueeze(3).to_broadcast([P, GT * NT, 2, 2]), ALU.mult))
                    r2f = r2[:].rearrange("p t a b -> p t (a b)")
                    link(5, dve.tensor_tensor(r3[:], go[:, :, 3:7, :], r2f.unsqueeze(3).to_broadcast([P, GT * NT, 4, 2]), ALU.mult))
                    r3f = r3[:].rearrange("p t a b -> p t (a b)")
                    dve.tensor_tensor(r4[:], go[:, :, 7:15, :], r3f.unsqueeze(3).to_broadcast([P, GT * NT, 8, 2]), ALU.mult).then_inc(s["zero"], 1)
                if step == 4:
                    need(dve, s["zero"], g + 2)
                    need(dve, s["ohp"], 2 * g)
                    r4f = r4[:].rearrange("p t a b -> p t (a b)")
                    for j in range(GT):
                        leaves = r4f[:, NT * j:NT * j + NT, :].unsqueeze(2).to_broadcast([P, NT, 4, NLEAF])
                        ins = dve.tensor_copy(oh[:, j, 0:NT, :, :], leaves)
                    ins.then_inc(s["oh"], 1)
                if step in (5, 6):
                    n = step - 5
                    need(dve, s["ohp"], 2 * g + n + 1)
                    r = P if n == 0 else SELP
                    dve.tensor_scalar(sel[u][0:r, n, :], pX[0:r, :], w("part")[0:r, 3:4], None, ALU.subtract).then_inc(s["sel"], 1)

            def low(g, u, k):
                m = STEPS * g + k
                need(dve, s["h"], m + 1)
                dve.scalar_tensor_tensor(hl[k % 2][:], pH[k % 2][:], 0.0, hh[k % 2][:], ALU.max, ALU.subtract).then_inc(s["lo"], 1)

            def shift(g, u, j):
                t = GT * g + j
                need(dve, s["S"], t + 1)
                need(dve, s["P"], t - 1)
                dve.tensor_reduce(nm[j % 2][:], pS[:, 0:S], AX.X, ALU.max, negate=True).then_inc(s["mx"], 1)
                need(dve, s["mx"], t + 1)
                dve.tensor_scalar(nm[j % 2][:], nm[j % 2][:], SC, None, ALU.mult).then_inc(s["nm"], 1)

            def final(g, u, j):
                t = GT * g + j
                need(dve, s["P"], t + 1)
                dve.reciprocal(rc[j % 2][:], sm[j % 2][:]).then_inc(s["rc"], 1)
                need(dve, s["rc"], t + 1)
                need(dve, s["O"], t + 1)
                dve.scalar_tensor_tensor(X[:, t, :], pO[:, 0:P], rc[j % 2][:, 0:1], X[:, t, :], ALU.mult, ALU.add).then_inc(s["X"], 1)

            def statistics(g, u, j):
                t = GT * g + j
                need_apart(dve, s["X"], t + 1, s["tick"])
                dve.bn_stats(bn[j % 2][:], X[:, t, :]).then_inc(s["bn"], 1)
                need_apart(dve, s["bn"], t + 1, s["tick"])
                dve.bn_aggr(mv[j % 2][:], bn[j % 2][:]).then_inc(s["mv"], 1)
                need(dve, s["mv"], t + 1)
                dve.tensor_scalar(MV[:, t, :], mv[j % 2][:], 1.0, None, ALU.mult)

            def attention(g, u, k):
                for j in range(GT):
                    if k == 3 * j + 1:
                        shift(g, u, j)
                    if k == 3 * j + 6:
                        final(g, u, j)
                    if k == 3 * j + 8:
                        statistics(g, u, j)

            def group(g, u):
                for k in range(STEPS):
                    low(g, u, k)
                    if past(g):
                        attention(g - 1, 1 - u, k)
                    if more(g):
                        if k == 12:
                            normalise(g + 1, 1 - u)
                        if 15 <= k < 22:
                            route(g + 1, 1 - u, k - 15)

            rs_dve(dve)
            dve.memset(oh[:], 0.0).then_inc(s["zero"], 1)
            normalise(0, 0)
            for step in range(7):
                route(0, 0, step)
            group_slots(dve, group)
            for k in range(STEPS):
                attention(NG - 1, 1, k)


MAGIC = 1.5 * 2.0 ** 23


def quantised_linear(core):
    X, MV, RS, XH = core.X, core.MV, core.RS, core.XH
    ident = core.w("ctx", "ident")
    w = lambda n: core.w("q8", n)
    with Stage(core, "q8") as st:
        two = lambda name, shape, dt=F32: [st.sb(f"{name}{u}", shape, dt) for u in range(2)]
        W8, idb = st.sb("W8", [P, P], BF16), st.sb("idb", [P, P], BF16)
        XQ = st.sb("XQ", [P, T, P], BF16)
        qT, yo = two("qT", [P, GT_P], BF16), two("yo", [P, GT, P])
        am, amr, one, xs = st.sb("am", [P, NG]), st.sb("amr", [P, P]), st.sb("one", [1, P]), st.sb("xs", [P, 2])
        pA, pB = st.ps("pA", [P, 512]), st.ps("pB", [P, 512])
        pT = [st.ps(f"pT{u}", [P, 1024], BF16) for u in range(2)]
        pY = [st.ps(f"pY{u}", [P, 512]) for u in range(2)]
        names = "w8 own amx amt am1 xsp xq qTp qT Y o b out".split()
        s = {n: st.sem(n) for n in names}
        rs_act, rs_dve = token_scales(core, st, MV[:, :, 1], RS[:], "a")
        blk = st.block()

        @blk.tensor
        def _(pe):
            pe.wait_ge(s["amx"], 1)
            pe.transpose(pA[:, 0:P], amr[:], ident).then_inc(s["amt"], 1)
            pe.wait_ge(s["am1"], 1)
            pe.matmul(pB[:, 0:1], one[:], xs[0:1, 0:1], start=True, stop=True).then_inc(s["xsp"], 1)
            pe.wait_ge(s["w8"], 2)

            def turn(g):
                pe.wait_ge(s["xq"], g + 1)
                if g >= 2:
                    pe.wait_ge(s["qT"], g - 1)
                for j in range(GT):
                    ins = pe.transpose(pT[g % 2][:, P * j:P * j + P], XQ[:, GT * g + j, :], idb[:])
                ins.then_inc(s["qTp"], 1)

            turn(0)
            for g in range(NG):
                if g + 1 < NG:
                    turn(g + 1)
                pe.wait_ge(s["qT"], g + 1)
                if g >= 2:
                    pe.wait_ge(s["o"], g - 1)
                for j in range(GT):
                    ins = pe.matmul(pY[g % 2][:, P * j:P * j + P], qT[g % 2][:, P * j:P * j + P], W8[:], start=True, stop=True)
                ins.then_inc(s["Y"], 1)

        @blk.scalar
        def _(act):
            rs_act(act)
            act.activation(W8[:], core.W8i[:].bitcast(I8), ACT.Copy).then_inc(s["w8"], 1)
            act.activation(idb[:], ident, ACT.Copy).then_inc(s["w8"], 1)
            for g in range(NG):
                act.wait_ge(s["qTp"], g + 1)
                if g >= 2:
                    act.wait_ge(s["Y"], g - 1)
                act.activation(qT[g % 2][:], pT[g % 2][:, 0:GT_P], ACT.Copy).then_inc(s["qT"], 1)

        @blk.gpsimd
        def _(pool):
            for g in range(NG):
                pool.wait_ge(s["b"], g + 1)
                x4 = X[:, GT * g:GT * g + GT, :]
                pool.tensor_tensor(x4, x4, w("bias").unsqueeze(1).to_broadcast([P, GT, P]), ALU.add).then_inc(s["out"], 1)

        @blk.vector
        def _(dve):
            link = Chain(dve, s["own"])
            dve.memset(one[:], 1.0)
            dve.memset(amr[:], 0.0)
            rs_dve(dve)
            for g in range(NG):
                for j in range(GT):
                    t = GT * g + j
                    ins = dve.tensor_scalar(XH[:, t, :], X[:, t, :], MV[:, t, 0:1], RS[:, t:t + 1], ALU.subtract, ALU.mult)
                ins.then_inc(s["b"], 1)
                dve.wait_ge(s["b"], g + 1)
                ins = dve.tensor_reduce(am[:, g:g + 1], XH[:, GT * g:GT * g + GT, :], AX.XY, ALU.max, apply_absolute_value=True)
            link(ins)
            dve.tensor_reduce(amr[:, 0:1], am[:], AX.X, ALU.max).then_inc(s["amx"], 1)
            dve.wait_ge(s["amt"], 1)
            dve.tensor_reduce(xs[0:1, 0:1], pA[0:1, 0:P], AX.X, ALU.max).then_inc(s["am1"], 1)
            dve.wait_ge(s["xsp"], 1)
            link(dve.tensor_scalar(xs[:, 1:2], pB[:, 0:1], 1.0 / 127.0, EPS, ALU.mult, ALU.max))
            link(dve.reciprocal(xs[:, 0:1], xs[:, 1:2]))
            for g in range(NG):
                x4 = XH[:, GT * g:GT * g + GT, :]
                link(dve.tensor_scalar(x4, x4, xs[:, 0:1], MAGIC, ALU.mult, ALU.add))
                link(dve.tensor_scalar(x4, x4, MAGIC, 127.0, ALU.subtract, ALU.min))
                dve.tensor_scalar(XQ[:, GT * g:GT * g + GT, :], x4, -128.0, None, ALU.max).then_inc(s["xq"], 1)
            for g in range(NG):
                dve.wait_ge(s["Y"], g + 1)
                yv = pY[g % 2][:].rearrange("p (t d) -> p t d", t=GT)
                dve.scalar_tensor_tensor(yo[g % 2][:], yv, xs[:, 1:2], w("wscale").unsqueeze(1).to_broadcast([P, GT, P]),
                                         ALU.mult, ALU.mult).then_inc(s["o"], 1)
                dve.wait_ge(s["o"], g + 1)
                dve.wait_ge(s["out"], g + 1)
                x4 = X[:, GT * g:GT * g + GT, :]
                dve.tensor_tensor(x4, x4, yo[g % 2][:], ALU.add).then_inc(s["b"], 1)

        @blk.sync
        def _(sp):
            for g in range(NG):
                sp.wait_ge(s["b"], NG + g + 1)
                sp.dma_start(core.A["out"].rearrange("(t p) d -> p t d", p=P)[:, GT * g:GT * g + GT, :],
                             X[:, GT * g:GT * g + GT, :]).then_inc(core.stored, 16)
            sp.wait_ge(core.stored, 16 * NG)


PACKS = ("ctx", "mha0", "top", "route", "mha2", "tree", "mha3", "q8")


def tiles(a, n=T):
    return a.rearrange("(t p) d -> p t d", t=n)


def place(core, stack, names):
    for name in names:
        width = max(hi for _, hi, _ in core.lay[name].values())
        core.pack[name] = stack.enter_context(core.nc.sbuf_tensor("w_" + name, [P, width], F32))


def load_later(core, sp):
    A = core.A
    core.loads = 0

    def later(to, src):
        sp.dma_start(to, src).then_inc(core.loaded, 16)
        core.loads += 1

    for name in ("rot", "ffn0") + PACKS[2:]:
        later(core.pack[name][:], A[name])
    later(core.W8i[:], A["W8"])
    later(core.raw2[:], tiles(A["mask2"], TB))
    for q in range(NG):
        later(core.raw3[:, GT * q:GT * q + GT, :], tiles(A["mask3"])[:, GT * q:GT * q + GT, :])


def load(core):
    A = core.A
    with Stage(core, "load") as st:
        s_first, s_bn = st.sem("first"), st.sem("bn")
        bn = st.sb("bn", [P, T, 6])
        blk = st.block()

        @blk.sync
        def _(sp):
            def x_load(q):
                sp.dma_start(core.X[:, GT * q:GT * q + GT, :], tiles(A["x"])[:, GT * q:GT * q + GT, :]).then_inc(core.x_loaded[q], 16)

            for q in range(NG // 2):
                x_load(q)
            for name in ("ctx", "mha0"):
                sp.dma_start(core.pack[name][:], A[name]).then_inc(s_first, 16)
            sp.dma_start(core.itok[:], A["itok"].to_broadcast([P, B * SK])).then_inc(s_first, 16)
            for q in range(NG // 2, NG):
                x_load(q)
            sp.wait_ge(s_first, 48)

        @blk.vector
        def _(dve):
            first_statistics(core, dve, bn, s_bn, range(NG // 2))


def four_layers(nc, A, layouts):
    with ExitStack() as ctx:
        core = Core(nc, ctx, A, layouts)
        core.loaded = ctx.enter_context(nc.semaphore("loaded"))
        core.stored = ctx.enter_context(nc.semaphore("stored"))
        core.x_loaded = [ctx.enter_context(nc.semaphore(f"x_loaded{q}")) for q in range(NG)]
        core.KT, core.VB = {}, {}
        core.XH = core.sb("XH", [P, T, P])
        place(core, ctx, PACKS)
        core.W8i = core.sb("W8i", [P, P // 4], I32)
        core.raw2, core.raw3 = core.sb("raw2", [P, TB, SK], I32), core.sb("raw3", [P, T, SK])
        core.slots = core.sb("slots", [P, T], I32)
        core.xs = nc.dram_tensor("slots_in", [N1 * CAP, P], F32, kind="Internal").ap()
        core.ys = nc.dram_tensor("slots_out", [N1 * CAP, P], F32, kind="Internal").ap()
        sb = lambda stack, name, shape, dt=F32: stack.enter_context(nc.sbuf_tensor(name, shape, dt))

        def attention_buffers(L, stack):
            core.KT[L], core.VB[L] = sb(stack, f"KT{L}", [P, B * SK]), sb(stack, f"VB{L}", [P, B, CH, VW])

        with ExitStack() as layer0:
            core.W2R, core.b2R = sb(layer0, "W2R", [P, 2 * NE * P]), sb(layer0, "b2R", [NE, P])
            core.up_h, core.up_l = (sb(layer0, n, [P, (NE + 2) * EH], F32R) for n in ("up_h", "up_l"))
            place(core, layer0, ["ffn0"])
            with ExitStack() as early:
                place(core, early, ["rot"])
                core.itok = sb(early, "itok", [P, B * SK], I32)
                load(core)
                attention_buffers(0, early)
                prep_key_mask(core, early)
                prep_mha(core, 0, True, statistics=True)
                mha(core, 0, key_mask=True)
                fold_rotations(core)
            ffn_moe_rotated(core)
        with ExitStack() as layer:
            core.KT[1], core.VWo = sb(layer, "KT1", [P, B * SK]), sb(layer, "VWo", [P, B, P])
            prep_top(core)
            attention_top(core)
        masks = {2: Mask(core.raw2, -1e-9, True), 3: Mask(core.raw3, NEG, False)}
        with ExitStack() as stack:
            core.trees_loaded = ctx.enter_context(nc.semaphore("trees_loaded"))
            for L in (2, 3):
                mask_buffers(core, L, masks[L], stack)
            with ExitStack() as trees:
                tree_buffers(core, trees)
                with ExitStack() as layer2:
                    attention_buffers(2, layer2)
                    with ExitStack() as layer:
                        place(core, layer, ["tree_full"])
                        route_top1(core)
                    run_experts(core, masks)
                    mha(core, 2, masks[2])
                attention_trees(core)
            attention_buffers(3, stack)
            prep_mha(core, 3, False)
            mha(core, 3, masks[3])
        quantised_linear(core)


def packs(I):
    import numpy as np
    f = lambda a: np.asarray(a, np.float32)
    row = lambda v, n=1: np.tile(np.asarray(v).reshape(1, -1), (P, n))
    col = lambda v: np.asarray(v).reshape(-1, P).T
    z = np.zeros(P, np.float32)
    ctxT = np.asarray(I["ctx_1024"]).transpose(2, 0, 1)
    pidx = np.arange(P)
    neg3, rest = np.zeros(3, np.float32), np.float32(NEG)
    for i in range(3):
        neg3[i] = (np.array([rest]).view(np.uint32) & np.uint32(0xFFFF0000)).view(np.float32)[0]
        rest = np.float32(rest - neg3[i])
    out = {}
    out["ctx"] = [("ident", np.eye(P, dtype=np.float32)),
                  ("ctxT2", np.repeat(ctxT[:, :, None, :], 2, 2).reshape(P, -1)),
                  ("bmask", (pidx[:, None] // HD == np.arange(H)[None]).astype(np.float32))]
    n = "L0_xattn_"
    out["mha0"] = [("wq", I[n + "Wq"]), ("wk", I[n + "Wk"]), ("wv", I[n + "Wv"]), ("wo", I[n + "Wo"]),
                   ("bq", col(z)), ("bk", col(z)), ("bv", row(z)), ("bo", row(I[n + "bo"], 2)), ("neg3", neg3[:, None])]
    n = "L0_ffn_"
    A = lambda k: np.asarray(I[n + k])
    out["rot"] = [("gens", A("gens").transpose(1, 0, 2).reshape(P, -1)), ("gensT", A("gens").transpose(2, 0, 1).reshape(P, -1)),
                  ("ew2T", A("ew2").reshape(-1, P).T), ("eb2T", A("eb2").T),
                  ("up", np.concatenate([A("ew1").transpose(1, 0, 2).reshape(P, -1), A("aw1")], 1))]
    out["ffn0"] = [("aw2", A("aw2").reshape(4, P, P).transpose(1, 0, 2).reshape(P, -1)),
                   ("eb1", col(A("eb1"))), ("ab1", col(A("ab1"))), ("gate_w", A("gate_w")), ("gate_b", row(A("gate_b"))),
                   ("prio", row(NE - np.arange(NE, dtype=np.float32))), ("ln_g", col(A("ln_g"))), ("ln_b", col(A("ln_b"))),
                   ("ab2", row(A("ab2"))), ("g1", row(A("gc_w")[:P])), ("g2", row(A("gc_w")[P:])), ("gc_b", row(A("gc_b")))]
    n = "L1_xattn_"
    out["top"] = [(k, np.asarray(I[n + "W" + k[1]]).T) for k in ("wq", "wk", "wv", "wo")] + [
        (k, col(I[n + k])) for k in ("bq", "bk", "bv")] + [("bo", row(I[n + "bo"], 2))]
    n = "L1_ffn_"
    A = lambda k: np.asarray(I[n + k])
    out["route"] = [("Wg", A("Wg")), ("b1", col(A("b1"))), ("prio", row(N1 - np.arange(N1, dtype=np.float32))),
                    ("same", (pidx[:, None] % N1 == pidx[None] % N1).astype(np.float32)),
                    ("below", (pidx[:, None] < pidx[None]).astype(np.float32)),
                    ("base", row(CAP * np.arange(N1, dtype=np.float32))),
                    ("pow2", row(2.0 ** -np.arange(BITS + 1, dtype=np.float32)))]
    n = "L2_xattn_"
    out["mha2"] = [(k, np.asarray(I[n + k]).T) for k in ("wq", "wk", "wv", "wo")] + [
        ("bq", col(I[n + "bq"])), ("bk", col(I[n + "bk"])), ("bv", row(I[n + "bv"])), ("bo", row(I[n + "bo"], 2))]
    n = "L3_xattn_"
    out["mha3"] = [(k.lower(), np.asarray(I[n + k]).transpose(1, 0, 2).reshape(P, P)) for k in ("Wq", "Wk", "Wv")] + [
        ("wo", I[n + "Wo"]), ("bq", col(I[n + "bq"])), ("bk", col(I[n + "bk"])), ("bv", row(I[n + "bv"])), ("bo", row(I[n + "bo"], 2))]
    trees = lambda key: [np.asarray(I[f"L2_ffn_{p}_{key}"]) for p in "qkv"]
    pad = lambda a, rows: np.concatenate([a, np.zeros((rows - len(a),) + a.shape[1:], a.dtype)])
    chosen = np.arange(NCH * P)[None] // LW == np.arange(NLEAF)[:, None]
    mixes = []
    for b1, b2 in zip(trees("b1"), trees("b2")):
        own = np.where(chosen, b1.reshape(1, -1), np.float32(0))
        first = np.concatenate([np.where(chosen, np.float32(BIG), np.float32(0)), np.zeros((NLEAF, P), np.float32)], 1)
        mixes.append(np.concatenate([first] + 3 * [np.concatenate([own, b2], 1)]))
    copy = pidx % SELP // NLEAF
    part = np.stack([copy <= 1, copy == 2, copy == 3, copy == 0], 1).astype(np.float32)
    out["tree_full"] = [
                   ("w1", np.concatenate([a.transpose(1, 0, 2).reshape(P, -1) for a in trees("w1")], 1)),
                   ("w2", np.concatenate([a.reshape(NCH, P, P).transpose(1, 0, 2).reshape(P, -1) for a in trees("w2")], 1)),
                   ("mixqk", np.concatenate(mixes[0:2])), ("mixv", mixes[2])]
    out["tree"] = [("part", part),
                   ("nodes", np.concatenate([pad(a, NLEAF).T for a in trees("node_w")], 1)),
                   ("node_b", row(np.concatenate([pad(a, NLEAF) for a in trees("node_b")])))]
    out["q8"] = [("wscale", row(I["L3_ffn_weight_scale"])), ("bias", row(I["L3_ffn_bias"]))]
    return out


def pack_layout(pack):
    lay, at = {}, 0
    for name, a in pack:
        lay[name] = (at, at + a.shape[1], a.shape[0])
        at += a.shape[1]
    return lay


def kernel(**inputs):
    import numpy as np
    import concourse.bacc as bacc
    from concourse.bass_utils import run_bass_kernel_spmd

    I = {name: np.asarray(a) for name, a in inputs.items()}
    parts = packs(I)
    layouts = {name: pack_layout(pack) for name, pack in parts.items()}
    arrays = {name: np.concatenate([np.concatenate([a, np.zeros((P - a.shape[0], a.shape[1]), a.dtype)]) for _, a in pack], 1)
              for name, pack in parts.items()}
    arrays["x"] = I["x"].reshape(B * S, P)
    arrays["itok"] = I["itok_BxS2_0_99"].reshape(1, B * SK)
    arrays["mask2"] = I["mask_1x1xSxS2_if1"].reshape(S, SK)
    arrays["mask3"] = I["mask_Bx1xSxS2_ff1"].reshape(B * S, SK)
    arrays["W8"] = np.ascontiguousarray(I["L3_ffn_weight_int8"].T).view(np.int32)
    for key in ("W1", "W2", "b2"):
        arrays["L1_" + key] = I["L1_ffn_" + key]
    arrays = {name: np.ascontiguousarray(a) for name, a in arrays.items()}

    nc = bacc.Bacc("TRN2", target_bir_lowering=False, num_devices=1)
    A = {name: nc.dram_tensor(f"in_{name}_dram", a.shape, mybir.dt.from_np(a.dtype), kind="ExternalInput").ap()
         for name, a in arrays.items()}
    A["out"] = nc.dram_tensor("out_0_dram", [B * S, P], F32, kind="ExternalOutput").ap()
    four_layers(nc, A, layouts)
    r = run_bass_kernel_spmd(nc, [{f"in_{name}_dram": a for name, a in arrays.items()}], core_ids=[0])
    return r.results[0]["out_0_dram"].reshape(B, S, P)
```
